# Optimizing a Trainium2 kernel written in Bass

```python
import numpy as np
import jax
import jax.numpy as jnp

def _softmax(x, axis=-1):
    return jax.nn.softmax(x, axis=axis)

def _gelu(x):
    return jax.nn.gelu(x, approximate=True)

def _silu(x):
    return jax.nn.silu(x)

def _sigmoid(x):
    return jax.nn.sigmoid(x)

def _layernorm(x, axis=-1, eps=1e-05):
    m = jnp.mean(x, axis=axis, keepdims=True)
    v = jnp.var(x, axis=axis, keepdims=True)
    return (x - m) / jnp.sqrt(v + eps)

def _scatter_add(tgt, idx, src, axis=0):
    return tgt.at[idx].add(src)

def _segment_sum(src, seg, n):
    return jax.ops.segment_sum(src, seg, n)
kernel_name = 'mk_gps_d1_gnn_r8_b0dcb8'

def setup_inputs(seed: int=0):
    np.random.seed(seed)
    _w = jnp.asarray

    def _rec_inputs():
        import jax
        import jax.numpy as jnp
        _gk = jax.random.key(seed)
        x = -8.776e-05 + 1 * jax.random.normal(jax.random.fold_in(_gk, 1), (6250, 256), jnp.float32)
        _s = jax.random.randint(jax.random.fold_in(_gk, 2), (50000,), 0, 6250, jnp.int32)
        _d = jax.random.randint(jax.random.fold_in(_gk, 3), (50000,), 0, 6250, jnp.int32)
        _loop = jnp.arange(6250, dtype=jnp.int32)
        src = jnp.concatenate([_s, _d, _loop])
        dst = jnp.concatenate([_d, _s, _loop])
        _o = jnp.argsort(dst, stable=True)
        src = src[_o]
        dst = dst[_o]
        edge_attr_256 = 2.93046e-05 + 1.00006 * jax.random.normal(jax.random.fold_in(_gk, 11), (106250, 256), jnp.float32)
        return (x, src, dst, edge_attr_256)
    x, src, dst, edge_attr_256 = _rec_inputs()

    def _L0_gnn_setup():
        import jax, jax.numpy as jnp
        import numpy as np
        N, E, D = (2500, 40000, 256)
        H, C = (8, 32)
        key = jax.random.key(seed)
        ks = jax.random.split(key, 12)
        s = 1.0 / np.sqrt(D)
        return {'x': jax.random.normal(ks[0], (N, D), jnp.float32), 'edge_index': jax.random.randint(ks[1], (2, E), 0, N, jnp.int64), 'edge_attr': jax.random.normal(ks[2], (E, D), jnp.float32), 'Wq': jax.random.normal(ks[3], (D, H * C), jnp.float32) * s, 'bq': jnp.zeros((H * C,), jnp.float32), 'Wk': jax.random.normal(ks[4], (D, H * C), jnp.float32) * s, 'bk': jnp.zeros((H * C,), jnp.float32), 'Wv': jax.random.normal(ks[5], (D, H * C), jnp.float32) * s, 'bv': jnp.zeros((H * C,), jnp.float32), 'We': jax.random.normal(ks[6], (D, H * C), jnp.float32) * s, 'Ws': jax.random.normal(ks[7], (D, H * C), jnp.float32) * s, 'bs': jnp.zeros((H * C,), jnp.float32)}
    _L0_gnn_all = _L0_gnn_setup()
    _L0_gnn_in = {k: v for k, v in _L0_gnn_all.items() if k in ('Wq', 'bq', 'Wk', 'bk', 'Wv', 'bv', 'We', 'Ws', 'bs')}
    del _L0_gnn_all

    def _L0_mix_setup():
        import jax, jax.numpy as jnp
        import numpy as np
        D_MODEL = 256
        NHEAD = 8
        D_HEAD = D_MODEL // NHEAD
        DIM_FF = 1024
        B, L = (4, 2048)
        LN_EPS = 1e-05

        def _layernorm(x, g, b):
            mu = jnp.mean(x, axis=-1, keepdims=True)
            var = jnp.mean((x - mu) ** 2, axis=-1, keepdims=True)
            return (x - mu) * jax.lax.rsqrt(var + LN_EPS) * g + b

        def _phi(x):
            return jnp.where(x > 0, x + 1.0, jnp.exp(x))
        key = jax.random.key(seed)
        ks = jax.random.split(key, 16)
        s_in = 1.0 / np.sqrt(D_MODEL)
        s_ff = 1.0 / np.sqrt(DIM_FF)
        inp = {'x': jax.random.normal(ks[0], (B, L, D_MODEL), dtype=jnp.float32), 'Wq': jax.random.normal(ks[1], (D_MODEL, D_MODEL), dtype=jnp.float32) * s_in, 'bq': jnp.zeros((D_MODEL,), jnp.float32), 'Wk': jax.random.normal(ks[2], (D_MODEL, D_MODEL), dtype=jnp.float32) * s_in, 'bk': jnp.zeros((D_MODEL,), jnp.float32), 'Wv': jax.random.normal(ks[3], (D_MODEL, D_MODEL), dtype=jnp.float32) * s_in, 'bv': jnp.zeros((D_MODEL,), jnp.float32), 'Wo': jax.random.normal(ks[4], (D_MODEL, D_MODEL), dtype=jnp.float32) * s_in, 'bo': jnp.zeros((D_MODEL,), jnp.float32), 'W1': jax.random.normal(ks[5], (D_MODEL, DIM_FF), dtype=jnp.float32) * s_in, 'b1': jnp.zeros((DIM_FF,), jnp.float32), 'W2': jax.random.normal(ks[6], (DIM_FF, D_MODEL), dtype=jnp.float32) * s_ff, 'b2': jnp.zeros((D_MODEL,), jnp.float32), 'ln1_g': jnp.ones((D_MODEL,), jnp.float32), 'ln1_b': jnp.zeros((D_MODEL,), jnp.float32), 'ln2_g': jnp.ones((D_MODEL,), jnp.float32), 'ln2_b': jnp.zeros((D_MODEL,), jnp.float32)}
        return inp
    _L0_mix_all = _L0_mix_setup()
    _L0_mix_in = {k: v for k, v in _L0_mix_all.items() if k in ('Wq', 'bq', 'Wk', 'bk', 'Wv', 'bv', 'Wo', 'bo', 'W1', 'b1', 'W2', 'b2', 'ln1_g', 'ln1_b', 'ln2_g', 'ln2_b')}
    del _L0_mix_all

    def _L0_ffn_setup():
        import jax, jax.numpy as jnp
        import numpy as np
        B, T, D, H, E = (16, 512, 256, 512, 8)
        key = jax.random.key(seed)
        ks = jax.random.split(key, 5)
        x = jax.random.normal(ks[0], (B, T, D), dtype=jnp.float32)
        gate_w = jax.random.normal(ks[1], (D, E), dtype=jnp.float32) * 0.02
        gate_b = jnp.zeros((E,), dtype=jnp.float32)
        W1 = jax.random.normal(ks[2], (E, D, H), dtype=jnp.float32) * 0.02
        b1 = jnp.zeros((E, H), dtype=jnp.float32)
        W2 = jax.random.normal(ks[3], (E, H, D), dtype=jnp.float32) * 0.02
        b2 = jnp.zeros((E, D), dtype=jnp.float32)
        return {'x': x, 'gate_w': gate_w, 'gate_b': gate_b, 'W1': W1, 'b1': b1, 'W2': W2, 'b2': b2}
    _L0_ffn_all = _L0_ffn_setup()
    _L0_ffn_in = {k: v for k, v in _L0_ffn_all.items() if k in ('gate_w', 'gate_b', 'W1', 'b1', 'W2', 'b2')}
    del _L0_ffn_all
    return {'x': x, 'src': src, 'dst': dst, 'edge_attr_256': edge_attr_256, 'L0_gnn_Wq': _L0_gnn_in['Wq'], 'L0_gnn_bq': _L0_gnn_in['bq'], 'L0_gnn_Wk': _L0_gnn_in['Wk'], 'L0_gnn_bk': _L0_gnn_in['bk'], 'L0_gnn_Wv': _L0_gnn_in['Wv'], 'L0_gnn_bv': _L0_gnn_in['bv'], 'L0_gnn_We': _L0_gnn_in['We'], 'L0_gnn_Ws': _L0_gnn_in['Ws'], 'L0_gnn_bs': _L0_gnn_in['bs'], 'L0_mix_Wq': _L0_mix_in['Wq'], 'L0_mix_bq': _L0_mix_in['bq'], 'L0_mix_Wk': _L0_mix_in['Wk'], 'L0_mix_bk': _L0_mix_in['bk'], 'L0_mix_Wv': _L0_mix_in['Wv'], 'L0_mix_bv': _L0_mix_in['bv'], 'L0_mix_Wo': _L0_mix_in['Wo'], 'L0_mix_bo': _L0_mix_in['bo'], 'L0_mix_W1': _L0_mix_in['W1'], 'L0_mix_b1': _L0_mix_in['b1'], 'L0_mix_W2': _L0_mix_in['W2'], 'L0_mix_b2': _L0_mix_in['b2'], 'L0_mix_ln1_g': _L0_mix_in['ln1_g'], 'L0_mix_ln1_b': _L0_mix_in['ln1_b'], 'L0_mix_ln2_g': _L0_mix_in['ln2_g'], 'L0_mix_ln2_b': _L0_mix_in['ln2_b'], 'L0_ffn_gate_w': _L0_ffn_in['gate_w'], 'L0_ffn_gate_b': _L0_ffn_in['gate_b'], 'L0_ffn_W1': _L0_ffn_in['W1'], 'L0_ffn_b1': _L0_ffn_in['b1'], 'L0_ffn_W2': _L0_ffn_in['W2'], 'L0_ffn_b2': _L0_ffn_in['b2']}

def reference(x, src, dst, edge_attr_256, L0_gnn_Wq, L0_gnn_bq, L0_gnn_Wk, L0_gnn_bk, L0_gnn_Wv, L0_gnn_bv, L0_gnn_We, L0_gnn_Ws, L0_gnn_bs, L0_mix_Wq, L0_mix_bq, L0_mix_Wk, L0_mix_bk, L0_mix_Wv, L0_mix_bv, L0_mix_Wo, L0_mix_bo, L0_mix_W1, L0_mix_b1, L0_mix_W2, L0_mix_b2, L0_mix_ln1_g, L0_mix_ln1_b, L0_mix_ln2_g, L0_mix_ln2_b, L0_ffn_gate_w, L0_ffn_gate_b, L0_ffn_W1, L0_ffn_b1, L0_ffn_W2, L0_ffn_b2):
    import jax
    import jax.numpy as jnp

    def _L0_gnn_ref(x, edge_index, edge_attr, Wq, bq, Wk, bk, Wv, bv, We, Ws, bs):
        import jax, jax.numpy as jnp
        import numpy as np
        N, E, D = (2500, 40000, 256)
        H, C = (8, 32)
        n = x.shape[0]
        src, dst = (edge_index[0], edge_index[1])
        q = (x @ Wq + bq).reshape(n, H, C)
        k = (x @ Wk + bk).reshape(n, H, C)
        v = (x @ Wv + bv).reshape(n, H, C)
        e = (edge_attr @ We).reshape(-1, H, C)
        kj = k[src] + e
        alpha = jnp.einsum('ehc,ehc->eh', q[dst], kj) / jnp.sqrt(jnp.float32(C))
        amax = jax.ops.segment_max(alpha, dst, num_segments=n)
        ea = jnp.exp(alpha - amax[dst])
        denom = jax.ops.segment_sum(ea, dst, num_segments=n)
        alpha = ea / (denom[dst] + 1e-16)
        msg = (v[src] + e) * alpha[:, :, None]
        out = jax.ops.segment_sum(msg, dst, num_segments=n)
        out = out.reshape(n, H * C) + (x @ Ws + bs)
        return out

    def _L0_mix_ref(x, Wq, bq, Wk, bk, Wv, bv, Wo, bo, W1, b1, W2, b2, ln1_g, ln1_b, ln2_g, ln2_b):
        import jax, jax.numpy as jnp
        import numpy as np
        D_MODEL = 256
        NHEAD = 8
        D_HEAD = D_MODEL // NHEAD
        DIM_FF = 1024
        B, L = (4, 2048)
        LN_EPS = 1e-05

        def _layernorm(x, g, b):
            mu = jnp.mean(x, axis=-1, keepdims=True)
            var = jnp.mean((x - mu) ** 2, axis=-1, keepdims=True)
            return (x - mu) * jax.lax.rsqrt(var + LN_EPS) * g + b

        def _phi(x):
            return jnp.where(x > 0, x + 1.0, jnp.exp(x))
        Bq, Lq, _ = x.shape
        q = (x @ Wq + bq).reshape(Bq, Lq, NHEAD, D_HEAD)
        k = (x @ Wk + bk).reshape(Bq, Lq, NHEAD, D_HEAD)
        v = (x @ Wv + bv).reshape(Bq, Lq, NHEAD, D_HEAD)
        q_phi = _phi(q)
        k_phi = _phi(k)
        kv = jnp.einsum('blhd,blhe->bhde', k_phi, v)
        k_sum = k_phi.sum(axis=1)
        z = 1.0 / (jnp.einsum('blhd,bhd->blh', q_phi, k_sum) + 1e-06)
        out = jnp.einsum('blhd,bhde,blh->blhe', q_phi, kv, z)
        out = out.reshape(Bq, Lq, D_MODEL) @ Wo + bo
        x = _layernorm(x + out, ln1_g, ln1_b)
        ff = jax.nn.relu(x @ W1 + b1) @ W2 + b2
        x = _layernorm(x + ff, ln2_g, ln2_b)
        return x

    def _L0_ffn_ref(x, gate_w, gate_b, W1, b1, W2, b2):
        import jax, jax.numpy as jnp
        import numpy as np
        B, T, D, H, E = (16, 512, 256, 512, 8)
        Bb, Tt, Dd = x.shape
        Ee = gate_w.shape[1]
        xf = x.reshape(-1, Dd)
        N = xf.shape[0]
        logits = xf @ gate_w + gate_b
        probs = jax.nn.softmax(logits, axis=-1)
        top2_vals, top2_idx = jax.lax.top_k(probs, 2)
        cw = jnp.zeros((N, Ee), dtype=xf.dtype).at[jnp.arange(N)[:, None], top2_idx].add(top2_vals)

        def step(acc, params):
            w1, bb1, w2, bb2, we = params
            h = jax.nn.gelu(xf @ w1 + bb1, approximate=False)
            y = h @ w2 + bb2
            return (acc + we[:, None] * y, None)
        out, _ = jax.lax.scan(step, jnp.zeros_like(xf), (W1, b1, W2, b2, cw.T))
        return out.reshape(Bb, Tt, Dd)
    edge_index = jnp.stack([src, dst])
    xn = _layernorm(x, axis=-1)
    x = x + _L0_gnn_ref(xn, edge_index, edge_attr_256, L0_gnn_Wq, L0_gnn_bq, L0_gnn_Wk, L0_gnn_bk, L0_gnn_Wv, L0_gnn_bv, L0_gnn_We, L0_gnn_Ws, L0_gnn_bs) + _L0_mix_ref(xn[None], L0_mix_Wq, L0_mix_bq, L0_mix_Wk, L0_mix_bk, L0_mix_Wv, L0_mix_bv, L0_mix_Wo, L0_mix_bo, L0_mix_W1, L0_mix_b1, L0_mix_W2, L0_mix_b2, L0_mix_ln1_g, L0_mix_ln1_b, L0_mix_ln2_g, L0_mix_ln2_b)[0]
    x = x + _L0_ffn_ref(_layernorm(x, axis=-1)[None], L0_ffn_gate_w, L0_ffn_gate_b, L0_ffn_W1, L0_ffn_b1, L0_ffn_W2, L0_ffn_b2)[0]
    return x

_drawn_inputs = setup_inputs


def setup_inputs(seed=0):
    import zlib

    import numpy as np

    out = dict(_drawn_inputs(seed))
    spreads = {'L0_gnn_bq': (0.0, 0.27),
     'L0_gnn_bk': (0.0, 2.0),
     'L0_gnn_bv': (0.0, 0.1),
     'L0_gnn_bs': (0.0, 0.1),
     'L0_mix_bq': (0.0, 2.0),
     'L0_mix_bk': (0.0, 2.0),
     'L0_mix_bv': (0.0, 0.1),
     'L0_mix_bo': (0.0, 0.1),
     'L0_mix_b1': (0.0, 0.306),
     'L0_mix_b2': (0.0, 0.1),
     'L0_mix_ln1_g': (1.0, 0.2),
     'L0_mix_ln1_b': (0.0, 0.1),
     'L0_mix_ln2_g': (1.0, 0.2),
     'L0_mix_ln2_b': (0.0, 0.1),
     'L0_ffn_gate_b': (0.0, 0.8),
     'L0_ffn_b1': (0.0, 0.8),
     'L0_ffn_b2': (0.0, 0.707)}
    factors = {'L0_mix_Wq': 8.0,
     'L0_mix_Wk': 8.0,
     'L0_mix_Wv': 8.0,
     'L0_ffn_gate_w': 4.435,
     'L0_ffn_W1': 6.507,
     'L0_ffn_W2': 6.108}
    for name, (base, spread) in spreads.items():
        noise = np.random.default_rng([zlib.crc32(name.encode()), seed]).standard_normal(out[name].shape)
        drawn = base * np.exp(spread * noise) if base else spread * noise
        out[name] = jnp.asarray(drawn.astype(out[name].dtype))
    for name, factor in factors.items():
        out[name] = (out[name] * factor).astype(out[name].dtype)
    return out
```

```python
from contextlib import ExitStack

import concourse.bass as bass
from concourse import mybir

F32 = mybir.dt.float32
I32 = mybir.dt.int32
ALU = mybir.AluOpType
ACT = mybir.ActivationFunctionType
AX = mybir.AxisListType.X

P = 128
N, E, D, H = 6250, 106250, 256, 8
C = D // H
KD = D // P
NT = -(-N // P)
NP = NT * P
LAST = N - (NT - 1) * P
G = 8
PAIRS = G // 2
NG = -(-E // (P * G))
TILES = NG * G
EP = TILES * P
SCALE = float(C) ** -0.5
BIG = 1e30
MSG = D + H
ROW = MSG + H + 1
CHUNKS = -(-TILES // P)
FF = 1024
FC = FF // P
HD = 512
HC = HD // P
NE = 8
MACRO = 7
MACROS = NT // MACRO
HALF = MACRO * P // 2
KVW = P + H // KD
LN_EPS = 1e-5


class Carve:

    def __init__(self, arena, size):
        self.arena, self.size, self.at = arena, size, 0

    def __call__(self, *shape):
        n = 1
        for s in shape:
            n *= s
        piece = self.arena[:, self.at:self.at + n]
        self.at += n
        assert self.at <= self.size, (self.at, self.size)
        if len(shape) == 2:
            return piece.rearrange("p (a b) -> p a b", a=shape[0])
        if len(shape) == 3:
            return piece.rearrange("p (a b c) -> p a b c", a=shape[0], b=shape[1])
        return piece


def rows_as_tiles(ap):
    return ap.rearrange("(t p) c -> p t c", p=P)


def over_partitions(ap):
    return ap.rearrange("(o n) -> o n", o=1).to_broadcast([P, ap.shape[0]])


def per_channel(ap):
    return ap.rearrange("(k p) -> p k", p=P)


def per_head(ap, tiles=None):
    if tiles is None:
        return ap.rearrange("p (h o) -> p h o", o=1).to_broadcast([P, H, C])
    return ap.rearrange("p t (h o) -> p t h o", o=1).to_broadcast([P, tiles, H, C])


def hold(eng, sem, value, passed):
    eng.wait_ge(sem, value)
    eng.sem_inc(passed, 1)


def heads(ap):
    return ap.rearrange("p (h c) -> p h c", h=H)


def build(nc, x, src, dst, edge_attr_256, L0_gnn_Wq, L0_gnn_bq, L0_gnn_Wk, L0_gnn_bk, L0_gnn_Wv, L0_gnn_bv,
          L0_gnn_We, L0_gnn_Ws, L0_gnn_bs, L0_mix_Wq, L0_mix_bq, L0_mix_Wk, L0_mix_bk, L0_mix_Wv, L0_mix_bv,
          L0_mix_Wo, L0_mix_bo, L0_mix_W1, L0_mix_b1, L0_mix_W2, L0_mix_b2, L0_mix_ln1_g, L0_mix_ln1_b,
          L0_mix_ln2_g, L0_mix_ln2_b, L0_ffn_gate_w, L0_ffn_gate_b, L0_ffn_W1, L0_ffn_b1, L0_ffn_W2, L0_ffn_b2,
          out):
    ctx = ExitStack()
    with ctx:
        def sb(name, shape, dt=F32):
            return ctx.enter_context(nc.sbuf_tensor(name, shape, dt))

        def stage(program, *operands):
            own = []

            def sem(name):
                own.append(nc.alloc_semaphore(name))
                return own[-1]

            program(nc, sem, psum, *operands)
            nc.clear_and_free_semaphores(own)
            nc.all_engine_barrier()

        def dram(name, shape, dt=F32):
            return nc.dram_tensor(name, shape, dt, kind="Internal").ap()

        kv_d = dram("kv_d", [NP, 2 * D])
        q_d = dram("q_d", [NP, D])
        xn_d = dram("xn_d", [NP, D])
        xs_d = dram("xs_d", [NP, D])
        x1_d = dram("x1_d", [NP, D])
        part_d = dram("part_d", [EP, ROW])
        extra_d = dram("extra_d", [NP, ROW])

        psum = [ctx.enter_context(nc.psum_tensor(f"bank{i}", [P, 512], F32)) for i in range(8)]
        ident = sb("ident", [P, P])
        eps = sb("eps", [P, 1])
        src_t = sb("src_t", [P, TILES], I32)
        dst_t = sb("dst_t", [P, TILES], I32)
        dst_f = sb("dst_f", [P, TILES])
        state = sb("state", [P, KD, KVW])
        last_i = sb("last_i", [P, NT], I32)
        node_f = sb("node_f", [P, NT])
        ARENA = 49500
        arena = sb("arena", [P, ARENA])

        stage(prepare, ident, eps, src_t, dst_t, dst_f, state, node_f, Carve(arena, ARENA), x, src, dst,
                (L0_gnn_Wk, L0_gnn_Wv, L0_gnn_Wq, L0_gnn_Ws, L0_mix_Wk, L0_mix_Wv),
                (L0_gnn_bk, L0_gnn_bv, L0_gnn_bq, L0_gnn_bs, L0_mix_bk, L0_mix_bv),
                kv_d, q_d, xn_d, xs_d, extra_d)
        stage(edges_and_mix, ident, eps, src_t, dst_t, dst_f, state, Carve(arena, ARENA), dst,
                      edge_attr_256, L0_gnn_We,
                      (L0_mix_Wq, L0_mix_Wo, L0_mix_W1, L0_mix_W2), (L0_mix_bq, L0_mix_b1),
                      (L0_mix_bo, L0_mix_ln1_g, L0_mix_ln1_b, L0_mix_b2, L0_mix_ln2_g, L0_mix_ln2_b),
                      kv_d, q_d, xn_d, xs_d, x1_d, part_d)
        stage(merge, ident, dst_f, node_f, last_i, Carve(arena, ARENA), dst, part_d, extra_d)
        stage(experts, ident, eps, node_f, last_i, Carve(arena, ARENA), part_d, extra_d, x1_d,
                L0_ffn_gate_w, L0_ffn_gate_b, L0_ffn_W1, L0_ffn_b1, L0_ffn_W2, L0_ffn_b2, out)


def prepare(nc, sem, psum, ident, eps, src_t, dst_t, dst_f, state, node_f, carve, x, src, dst, weights, biases,
            kv_d, q_d, xn_d, xs_d, extra_d):
    w6 = carve(6, KD, D)
    b6 = carve(6, D)
    xt = [carve(D) for _ in range(2)]
    xn = [carve(D) for _ in range(2)]
    xnT = [carve(KD, P) for _ in range(2)]
    kv = [carve(2 * D) for _ in range(2)]
    qs = [carve(2 * D) for _ in range(2)]
    mk = [carve(D) for _ in range(2)]
    mv = [carve(KD, P + 1) for _ in range(2)]
    neg = [carve(D) for _ in range(2)]
    phi = [carve(D) for _ in range(2)]
    st6 = carve(6)
    mom = [carve(2) for _ in range(2)]
    std = [carve(1) for _ in range(2)]
    rstd = carve(1)
    empty = carve(ROW)
    rows_i = carve(2, CHUNKS, P)
    rows_f = carve(2, CHUNKS, P)
    node_i = carve(NT)

    passed = sem("pa_passed")
    loaded, ident0, made = sem("prep_loaded"), sem("ident_zeroed"), sem("consts_made")
    rows_in, rows_cast, rowT_ps, rowT_sb = sem("rows_in"), sem("rows_cast"), sem("rowT_ps"), sem("rowT_sb")
    x_in = [sem(f"x_in{b}") for b in range(2)]
    stats, mom_ready, std_ready, rstd_ready, xn_ready = (sem(n) for n in (
        "pa_stats", "pa_mom", "pa_std", "pa_rstd", "xn_ready"))
    xnT_ps, xnT_sb, kv_ps, qs_ps, mix_ps, acc_done = (sem(n) for n in (
        "xnT_ps", "xnT_sb", "kv_ps", "qs_ps", "mixkv_ps", "state_added"))
    kv_sb, sum_sb, xs_sb, mk_sb, neg_sb, exp_sb, phi_sb = (sem(n) for n in (
        "kv_sb", "xs_part", "xs_sb", "mixk_sb", "neg_sb", "exp_sb", "phi_sb"))
    stored = [sem(f"pa_stored{b}") for b in range(2)]
    extra_out, state_zero, state_done = sem("extra_out"), sem("state_zeroed"), sem("state_copied")
    T, KV, QS, MX, A0, A1 = psum[0], psum[1], psum[2], psum[3], psum[4], psum[5]
    src_v, dst_v = src.rearrange("(t e) -> t e", e=P), dst.rearrange("(t e) -> t e", e=P)
    full = TILES // P
    rest = TILES - full * P
    NROWS = 4 if rest else 2

    def drive(eng, step):
        for i in range(2):
            step(i, i % 2, i // 2)
        with eng.Fori(0, (NT - 3) // 2) as k:
            step(2 * k + 2, 0, k + 1)
            step(2 * k + 3, 1, k + 1)
        step(NT - 1, (NT - 1) % 2, (NT - 1) // 2)

    assert NT % 2 == 1

    with nc.Block() as block:
        @block.sync
        def _(eng):
            eng.dma_start(xt[0], x[0:P, :]).then_inc(x_in[0], 16)
            eng.dma_start(xt[1], x[P:2 * P, :]).then_inc(x_in[1], 16)
            for w in range(6):
                eng.dma_start(w6[:, w], weights[w].rearrange("(k p) n -> p k n", p=P)).then_inc(loaded, 16)
            for w in range(6):
                eng.dma_start(b6[:, w], over_partitions(biases[w])).then_inc(loaded, 16)
            for a, view in enumerate((src_v, dst_v)):
                eng.dma_start(rows_i[:, a, 0:full].bitcast(I32),
                              view[0:full * P].rearrange("(k p) e -> p k e", p=P)).then_inc(rows_in, 16)
                if rest:
                    eng.dma_start(rows_i[0:rest, a, full].bitcast(I32),
                                  view[full * P:TILES]).then_inc(rows_in, 16)
            eng.wait_ge(made, 6)
            eng.dma_start(rows_as_tiles(extra_d),
                          empty.rearrange("p (o c) -> p o c", o=1).to_broadcast([P, NT, ROW])).then_inc(extra_out, 16)

            def store(i, b, u):
                eng.wait_ge(xn_ready, i + 1)
                eng.dma_start(xn_d[bass.ds(i * P, P), :], xn[b]).then_inc(stored[b], 16)
                eng.wait_ge(kv_sb, i + 1)
                eng.dma_start(kv_d[bass.ds(i * P, P), :], kv[b]).then_inc(stored[b], 16)
                eng.wait_ge(xs_sb, i + 1)
                eng.dma_start(q_d[bass.ds(i * P, P), :], qs[b][:, 0:D]).then_inc(stored[b], 16)
                eng.dma_start(xs_d[bass.ds(i * P, P), :], qs[b][:, D:]).then_inc(stored[b], 16)

            def step(i, b, u):
                store(i, b, u)
                eng.dma_start(xt[b], x[bass.ds((i + 2) * P, P), :]).then_inc(x_in[b], 16)

            step(0, 0, 0)
            with eng.Fori(0, (NT - 3) // 2) as k:
                step(2 * k + 1, 1, k)
                step(2 * k + 2, 0, k + 1)
            for i in (NT - 2, NT - 1):
                store(i, i % 2, i // 2)
            for b in range(2):
                eng.wait_ge(stored[b], 64 * ((NT + 1 - b) // 2))
            eng.wait_ge(extra_out, 16)

        @block.gpsimd
        def _(eng):
            eng.memset(ident[:], 0.0).then_inc(ident0, 1)
            eng.memset(eps[:], LN_EPS).then_inc(made, 1)
            eng.memset(empty[:, 0:MSG], 0.0).then_inc(made, 1)
            eng.memset(empty[:, MSG:ROW], -BIG).then_inc(made, 1)
            for b in range(2):
                eng.memset(mv[b][:, :, P:P + 1], 1.0).then_inc(made, 1)
            eng.wait_ge(ident0, 1)
            eng.affine_select(out=ident[:], in_=ident[:], compare_op=ALU.not_equal, fill=1.0, base=0,
                              pattern=[[-1, P]], channel_multiplier=1).then_inc(made, 1)
            eng.iota(node_i.bitcast(I32), pattern=[[P, NT]], base=0, channel_multiplier=1).then_inc(ident0, 1)
            eng.wait_ge(ident0, 2)
            eng.tensor_copy(node_f[:], node_i.bitcast(I32)).then_inc(made, 1)

        @block.tensor
        def _(eng):
            eng.wait_ge(made, 6)
            for n in range(2 * CHUNKS):
                a, k = divmod(n, CHUNKS)
                rows = P if k < full else rest
                eng.wait_ge(rows_cast, a + 1)
                if n >= 2:
                    eng.wait_ge(rowT_sb, n - 1)
                eng.transpose(psum[6 + n % 2][:, 0:rows], rows_f[0:rows, a, k], ident[0:rows, 0:rows])\
                   .then_inc(rowT_ps, 1)
            eng.wait_ge(loaded, 12 * 16)

            def add_state(i, b, u, first, last):
                rows = LAST if last else P
                eng.wait_ge(phi_sb, i + 1)
                for c, bank in enumerate((A0, A1)):
                    mm = eng.matmul(bank[:, 0:P + 1], phi[b][0:rows, c * P:(c + 1) * P], mv[b][0:rows, c, :],
                                    start=first, stop=last, skip_group_check=True)
                mm.then_inc(acc_done, 1)

            def step(i, b, u):
                eng.wait_ge(xn_ready, i + 1)
                if not isinstance(i, int) or i >= 1:
                    eng.wait_ge(xnT_sb, i)
                for c in range(KD):
                    mm = eng.transpose(T[:, c * P:(c + 1) * P], xn[b][:, c * P:(c + 1) * P], ident[:])
                mm.then_inc(xnT_ps, 1)
                if not isinstance(i, int) or i >= 1:
                    eng.wait_ge(mk_sb, 2 * i)
                eng.wait_ge(xnT_sb, i + 1)
                for n, (bank, done) in enumerate(((KV, kv_ps), (QS, qs_ps), (MX, mix_ps))):
                    for c in range(KD):
                        mm = eng.matmul(bank[:].rearrange("p (w n) -> p w n", w=2), xnT[b][:, c],
                                        w6[:, 2 * n:2 * n + 2, c], start=c == 0, stop=c == KD - 1)
                    mm.then_inc(done, 1)

            step(0, 0, 0)
            step(1, 1, 0)
            add_state(0, 0, 0, True, False)
            with eng.Fori(0, (NT - 3) // 2) as k:
                step(2 * k + 2, 0, k + 1)
                add_state(2 * k + 1, 1, k, False, False)
                step(2 * k + 3, 1, k + 1)
                add_state(2 * k + 2, 0, k + 1, False, False)
            i = NT - 1
            step(i, i % 2, i // 2)
            add_state(i - 1, (i - 1) % 2, (i - 1) // 2, False, False)
            add_state(i, i % 2, i // 2, False, True)

        @block.scalar
        def _(eng):
            eng.wait_ge(made, 6)

            def deviation(i, b):
                eng.wait_ge(mom_ready, i + 1)
                eng.activation(std[b], mom[b][:, 1:2], ACT.Sqrt, bias=eps[:]).then_inc(std_ready, 1)

            def step(i, b, u):
                eng.wait_ge(xnT_ps, i + 1)
                if not isinstance(i, int) or i >= 2:
                    eng.wait_ge(mix_ps, i - 1)
                eng.activation(xnT[b].rearrange("p k n -> p (k n)"), T[:, 0:D], ACT.Copy).then_inc(xnT_sb, 1)
                if not isinstance(i, int) or i < NT - 1:
                    deviation(i + 1, 1 - b)
                eng.wait_ge(neg_sb, i + 1)
                eng.activation(neg[b], neg[b], ACT.Exp).then_inc(exp_sb, 1)

            deviation(0, 0)
            drive(eng, step)

        @block.vector
        def _(eng):
            eng.wait_ge(rows_in, 16 * NROWS)
            for a in range(2):
                eng.tensor_copy(rows_f[:, a, 0:full], rows_i[:, a, 0:full].bitcast(I32))
                last = eng.tensor_copy(rows_f[0:rest, a, full], rows_i[0:rest, a, full].bitcast(I32))
                last.then_inc(rows_cast, 1)
            for n in range(2 * CHUNKS):
                a, k = divmod(n, CHUNKS)
                rows = P if k < full else rest
                eng.wait_ge(rowT_ps, n + 1)
                if a:
                    eng.tensor_copy(dst_f[:, k * P:k * P + rows], psum[6 + n % 2][:, 0:rows])
                eng.tensor_copy((src_t, dst_t)[a][:, k * P:k * P + rows], psum[6 + n % 2][:, 0:rows])\
                   .then_inc(rowT_sb, 1)
            eng.wait_ge(loaded, 12 * 16)
            eng.wait_ge(made, 6)

            def normalise(i, b, u):
                eng.wait_ge(x_in[b], 16 * (u + 1))
                eng.bn_stats(st6, xt[b]).then_inc(stats, 1)
                hold(eng, stats, i + 1, passed)
                eng.bn_aggr(mom[b], st6).then_inc(mom_ready, 1)
                eng.wait_ge(std_ready, i + 1)
                eng.reciprocal(rstd, std[b]).then_inc(rstd_ready, 1)
                eng.wait_ge(rstd_ready, i + 1)
                if not isinstance(i, int) or i >= 2:
                    eng.wait_ge(stored[b], 64 * u)
                eng.tensor_scalar(xn[b], xt[b], mom[b][:, 0:1], rstd, ALU.subtract, ALU.mult).then_inc(xn_ready, 1)

            def add_bias(i, b, u):
                eng.wait_ge(kv_ps, i + 1)
                eng.tensor_tensor(kv[b], KV[:], b6[:, 0:2].rearrange("p w n -> p (w n)"), ALU.add).then_inc(kv_sb, 1)
                eng.wait_ge(qs_ps, i + 1)
                eng.tensor_tensor(qs[b], QS[:], b6[:, 2:4].rearrange("p w n -> p (w n)"), ALU.add).then_inc(sum_sb, 1)
                eng.wait_ge(mix_ps, i + 1)
                if not isinstance(i, int) or i >= 2:
                    eng.wait_ge(acc_done, i - 1)
                eng.tensor_tensor(mk[b], MX[:, 0:D], b6[:, 4], ALU.add).then_inc(mk_sb, 1)
                eng.tensor_tensor(mv[b][:, :, 0:P], MX[:, D:].rearrange("p (k n) -> p k n", k=KD),
                                  b6[:, 5].rearrange("p (k n) -> p k n", k=KD), ALU.add).then_inc(mk_sb, 1)
                eng.wait_ge(sum_sb, i + 1)
                eng.tensor_tensor(qs[b][:, D:], qs[b][:, D:], xt[b], ALU.add).then_inc(xs_sb, 1)
                eng.wait_ge(mk_sb, 2 * i + 1)
                eng.tensor_scalar(neg[b], mk[b], 0.0, None, ALU.min).then_inc(neg_sb, 1)

            def feature(i, b, u):
                eng.wait_ge(exp_sb, i + 1)
                eng.scalar_tensor_tensor(phi[b], mk[b], 0.0, neg[b], ALU.max, ALU.add).then_inc(phi_sb, 1)

            normalise(0, 0, 0)
            pass_two(0, normalise, add_bias, feature)
            with eng.Fori(1, (NT - 1) // 2) as k:
                pass_two(k, normalise, add_bias, feature)
            i = NT - 1
            add_bias(i, i % 2, i // 2)
            feature(i, i % 2, i // 2)
            eng.memset(state[:], 0.0).then_inc(state_zero, 1)
            eng.wait_ge(state_zero, 1)
            eng.wait_ge(acc_done, NT)
            for c, bank in enumerate((A0, A1)):
                for h in range(H // KD):
                    rows = slice(h * C, (h + 1) * C)
                    eng.tensor_copy(state[rows, c, h * C:(h + 1) * C], bank[rows, h * C:(h + 1) * C])
                    last = eng.tensor_copy(state[rows, c, P + h:P + h + 1], bank[rows, P:P + 1])
            last.then_inc(state_done, 1)
            eng.wait_ge(state_done, 1)


def pass_two(k, normalise, add_bias, feature):
    normalise(2 * k + 1, 1, k)
    add_bias(2 * k, 0, k)
    feature(2 * k, 0, k)
    normalise(2 * k + 2, 0, k + 1)
    add_bias(2 * k + 1, 1, k)
    feature(2 * k + 1, 1, k)



def edges_and_mix(nc, sem, psum, ident, eps, src_t, dst_t, dst_f, state, carve, dst, edge_attr, We, mats, columns,
                  rows, kv_d, q_d, xn_d, xs_d, x1_d, part_d):
    we = carve(KD, D)
    ea = [carve(G, D) for _ in range(2)]
    kv = [carve(G, 2 * D) for _ in range(2)]
    q = [carve(G, D) for _ in range(2)]
    dst_all = [carve(G, P) for _ in range(2)]
    dst_row = [carve(P) for _ in range(2)]
    eaT = [carve(2 * KD, P) for _ in range(2)]
    kj = [carve(2, D) for _ in range(2)]
    ve = [carve(G, D) for _ in range(2)]
    alpha = [carve(G * H) for _ in range(2)]
    src_c = [carve(G) for _ in range(2)]
    dst_c = [carve(G) for _ in range(2)]
    dst_cf = [carve(G) for _ in range(2)]
    same = [carve(G, P) for _ in range(2)]
    msg = [carve(G, MSG) for _ in range(2)]
    part = [carve(G, ROW) for _ in range(2)]
    keep = carve(P + 1)
    left, peak, diff, prob = carve(P), carve(P), carve(P), carve(P)
    wq, wo, w1, w2 = carve(KD, D), carve(KD, D), carve(KD, FF), carve(FC, D)
    bq, b1 = carve(KD), carve(FC)
    bo, g1, h1, b2, g2, h2 = (carve(D) for _ in range(6))
    mx_xn, mx_xs, mx_out = carve(D), carve(D), carve(D)
    xnT, qneg, qpos, attn, attnT = carve(KD, P), carve(KD, P), carve(KD, P), carve(D), carve(KD, P)
    den, y, xm, x1, x1T, hid = carve(H), carve(D), carve(D), carve(D), carve(KD, P), carve(FC, P)
    m_st6, m_mom, m_std, m_rstd = carve(6), carve(2), carve(1), carve(1)
    SG = G * H
    T, E_ps, U, S, M = psum[0:2], psum[2:4], psum[4:6], psum[6], psum[7]

    passed = sem("b_passed")
    loaded, edge_made = sem("b_loaded"), sem("b_made")
    ea_in = [sem(f"ea_in{b}") for b in range(2)]
    all_in = [sem(f"dst_all_in{b}") for b in range(2)]
    row_in = [sem(f"dst_row_in{b}") for b in range(2)]
    gathered = [[sem(f"gathered{b}_{j}") for j in range(PAIRS)] for b in range(2)]
    index_ready, eaT_ps, eaT_sb, e_ps = sem("index_ready"), sem("eaT_ps"), sem("eaT_sb"), sem("e_ps")
    kj_ready, ve_ready, prod_ready, alpha_ready = sem("kj_ready"), sem("ve_ready"), sem("prod_ready"), sem("alpha_ready")
    same_row, keep_ready, alphaT_ps, left_ready = sem("same_row"), sem("keep_ready"), sem("alphaT_ps"), sem("left_ready")
    peak_ready, diff_ready, prob_ready, back_ps = sem("peak_ready"), sem("diff_ready"), sem("prob_ready"), sem("back_ps")
    dstc_ready, weights_sb, peaks_sb, same_ready = sem("dstc_ready"), sem("weights_sb"), sem("peaks_sb"), sem("same_ready")
    msg_ready, u_ps, u_sb = sem("msg_ready"), sem("u_ps"), sem("u_sb")
    part_out = [sem(f"part_out{b}") for b in range(2)]
    mx_in = sem("mx_in")
    mx_ps = [sem(f"mx_ps{n}") for n in range(9)]
    mx_act = [sem(f"mx_act{n}") for n in range(8)]
    mx_dve = [sem(f"mx_dve{n}") for n in range(18)]
    mx_stored = sem("mx_stored")

    def seen(v, n=1):
        return not isinstance(v, int) or v >= n

    FIRST = 3
    def drive(eng, step, before=None, mix=None, after=None):
        for g in range(FIRST):
            step(g, g % 2, g // 2, None)
        with eng.Fori(0, NT) as k:
            if before:
                before(k)
            step(2 * k + 3, 1, k + 1, (k, 0))
            step(2 * k + 4, 0, k + 2, (k, 8))
            if after:
                after(k)
        for g in range(FIRST + 2 * NT, NG + 1):
            step(g, g % 2, g // 2, None)

    with nc.Block() as block:
        @block.sync
        def _(eng):
            eng.dma_start(we, We.rearrange("(k p) n -> p k n", p=P)).then_inc(loaded, 16)
            edge_rows = rows_as_tiles(edge_attr)
            dst_rows = dst.rearrange("(t e) -> t e", e=P)
            part_rows = rows_as_tiles(part_d)

            def load(g, b):
                if seen(g, 2):
                    eng.wait_ge(eaT_ps, PAIRS * (g - 1))
                eng.dma_start(ea[b], edge_rows[:, bass.ds(g * G, G), :]).then_inc(ea_in[b], 16)
                if seen(g, 2):
                    hold(eng, keep_ready, g - 1, passed)
                    hold(eng, same_ready, G * (g - 1), passed)
                eng.dma_start(dst_row[b][0:SG].bitcast(I32),
                              dst_rows[bass.ds(g * G, G), :].rearrange("t (o e) -> t o e", o=1)
                              .to_broadcast([G, H, P])).then_inc(row_in[b], 16)
                eng.dma_start(dst_all[b].rearrange("p t e -> p (t e)").bitcast(I32),
                              dst[bass.ds(g * G * P, G * P)].rearrange("(o e) -> o e", o=1)
                              .to_broadcast([P, G * P])).then_inc(all_in[b], 16)

            def store(g, b):
                eng.wait_ge(u_sb, G * (g + 1))
                eng.wait_ge(peaks_sb, g + 1)
                eng.dma_start(part_rows[:, bass.ds(g * G, G), :], part[b]).then_inc(part_out[b], 16)

            def step(g, b, u, mix):
                if isinstance(g, int) and g == NG:
                    store(g - 2, b)
                    return
                load(g, b)
                if seen(g, 2):
                    store(g - 2, b)

            def step0(g, b, u, mix):
                step(g, b, u, mix)
                if isinstance(g, int) and g == 0:
                    w = 0
                    for to, of in ((wq, mats[0]), (wo, mats[1]), (w1, mats[2]), (w2, mats[3])):
                        eng.dma_start(to, of.rearrange("(k p) n -> p k n", p=P)).then_inc(loaded, 16)
                    for to, of in ((bq, columns[0]), (b1, columns[1])):
                        with nc.allow_non_contiguous_dma("biases, once"):
                            eng.dma_start(to, per_channel(of)).then_inc(loaded, 16)
                    for to, of in zip((bo, g1, h1, b2, g2, h2), rows):
                        eng.dma_start(to, over_partitions(of)).then_inc(loaded, 16)

            def before(k):
                eng.wait_ge(mx_dve[17], k)
                eng.dma_start(mx_xn, xn_d[bass.ds(k * P, P), :]).then_inc(mx_in, 16)
                eng.dma_start(mx_xs, xs_d[bass.ds(k * P, P), :]).then_inc(mx_in, 16)

            def after(k):
                eng.wait_ge(mx_dve[17], k + 1)
                eng.dma_start(x1_d[bass.ds(k * P, P), :], mx_out).then_inc(mx_stored, 16)

            drive(eng, step0, before=before, after=after)
            store(NG - 1, (NG - 1) % 2)
            for b in range(2):
                eng.wait_ge(part_out[b], 16 * (NG // 2))
            eng.wait_ge(mx_stored, 16 * NT)

        @block.gpsimd
        def _(eng):
            def step(g, b, u, mix):
                if isinstance(g, int) and g == NG:
                    return
                if seen(g, 2):
                    eng.wait_ge(alpha_ready, PAIRS * (g - 1))
                eng.tensor_copy(src_c[b].bitcast(I32), src_t[:, bass.ds(g * G, G)]).then_inc(index_ready, 1)
                eng.tensor_copy(dst_c[b].bitcast(I32), dst_t[:, bass.ds(g * G, G)]).then_inc(index_ready, 1)
                hold(eng, index_ready, 2 * g + 2, passed)
                for t in range(G):
                    done = gathered[b][t // 2]
                    eng.indirect_dma_start(kv[b][:, t], None, kv_d, bass.IndirectOffsetOnAxis(
                        src_c[b][:, t:t + 1].bitcast(I32), 0), bounds_check=NP - 1, oob_is_err=False).then_inc(done, 16)
                    eng.indirect_dma_start(q[b][:, t], None, q_d, bass.IndirectOffsetOnAxis(
                        dst_c[b][:, t:t + 1].bitcast(I32), 0), bounds_check=NP - 1, oob_is_err=False).then_inc(done, 16)

            drive(eng, step)

        @block.tensor
        def _(eng):
            eng.wait_ge(loaded, 16)

            def mix_slot(mix, s):
                if mix is None:
                    return
                k, s = mix[0], mix[1] + s
                if s == 0:
                    eng.wait_ge(mx_in, 32 * (k + 1))
                    for c in range(KD):
                        mm = eng.transpose(M[:, c * P:(c + 1) * P], mx_xn[:, c * P:(c + 1) * P], ident[:])
                    mm.then_inc(mx_ps[0], 1)
                elif s == 1:
                    eng.wait_ge(mx_act[0], k + 1)
                    for o in range(KD):
                        for c in range(KD):
                            mm = eng.matmul(M[:, o * P:(o + 1) * P], wq[:, c, o * P:(o + 1) * P], xnT[:, c],
                                            start=c == 0, stop=c == KD - 1)
                    mm.then_inc(mx_ps[1], 1)
                elif s == 3:
                    eng.wait_ge(mx_dve[1], k + 1)
                    for c in range(KD):
                        mm = eng.matmul(M[:, c * KVW:(c + 1) * KVW], qneg[:, c], state[:, c], start=True, stop=True)
                    mm.then_inc(mx_ps[2], 1)
                elif s == 4:
                    eng.wait_ge(mx_dve[4], k + 1)
                    for c in range(KD):
                        mm = eng.transpose(M[:, c * P:(c + 1) * P], attn[:, c * P:(c + 1) * P], ident[:])
                    mm.then_inc(mx_ps[3], 1)
                elif s == 5:
                    eng.wait_ge(mx_act[3], k + 1)
                    for c in range(KD):
                        mm = eng.matmul(M[:, 0:D], attnT[:, c], wo[:, c], start=c == 0, stop=c == KD - 1)
                    mm.then_inc(mx_ps[4], 1)
                elif s == 7:
                    eng.wait_ge(mx_dve[10], k + 1)
                    for c in range(KD):
                        mm = eng.transpose(M[:, c * P:(c + 1) * P], x1[:, c * P:(c + 1) * P], ident[:])
                    mm.then_inc(mx_ps[5], 1)
                elif s in (8, 9):
                    part_ = s - 8
                    eng.wait_ge(mx_act[5 + part_], k + 1)
                    for f in range(FC // 2):
                        ff = part_ * (FC // 2) + f
                        for c in range(KD):
                            mm = eng.matmul(M[:, f * P:(f + 1) * P], w1[:, c, ff * P:(ff + 1) * P], x1T[:, c],
                                            start=c == 0, stop=c == KD - 1)
                    mm.then_inc(mx_ps[6 + part_], 1)
                elif s == 10:
                    eng.wait_ge(mx_act[7], k + 1)
                    for f in range(FC):
                        mm = eng.matmul(M[:, 0:D], hid[:, f], w2[:, f], start=f == 0, stop=f == FC - 1)
                    mm.then_inc(mx_ps[8], 1)

            def transposes(g, b, u, j):
                if j == 0:
                    eng.wait_ge(ea_in[b], 16 * (u + 1))
                if seen(g, 1) or j >= 2:
                    eng.wait_ge(eaT_sb, PAIRS * g + j - 1)
                for t in range(2):
                    for c in range(KD):
                        mm = eng.transpose(T[j % 2][:, (t * KD + c) * P:(t * KD + c + 1) * P],
                                           ea[b][:, 2 * j + t, c * P:(c + 1) * P], ident[:])
                mm.then_inc(eaT_ps, 1)

            def project(g, j):
                eng.wait_ge(eaT_sb, PAIRS * g + j + 1)
                if seen(g, 1) or j >= 2:
                    eng.wait_ge(ve_ready, PAIRS * g + j - 1)
                for t in range(2):
                    for c in range(KD):
                        mm = eng.matmul(E_ps[j % 2][:, t * D:(t + 1) * D], eaT[j % 2][:, t * KD + c], we[:, c],
                                        start=c == 0, stop=c == KD - 1)
                mm.then_inc(e_ps, 1)

            def scores_to_rows(g, b):
                hold(eng, alpha_ready, PAIRS * (g + 1), passed)
                if seen(g):
                    hold(eng, peaks_sb, g, passed)
                eng.transpose(S[0:SG, 0:P], alpha[b], ident[:]).then_inc(alphaT_ps, 1)

            def rows_back(g):
                hold(eng, prob_ready, g + 1, passed)
                eng.transpose(S[:, P:P + SG], prob[0:SG], ident[0:SG, 0:SG])
                eng.transpose(S[:, P + SG:P + 2 * SG], peak[0:SG], ident[0:SG, 0:SG]).then_inc(back_ps, 1)

            def sum_nodes(g, b, tiles):
                for t in tiles:
                    if t % 2 == 0:
                        eng.wait_ge(msg_ready, PAIRS * g + t // 2 + 1)
                    if seen(g) or t >= 2:
                        eng.wait_ge(u_sb, G * g + t - 1)
                    eng.matmul(U[t % 2][:, 0:MSG], same[b][:, t], msg[b][:, t], start=True, stop=True)\
                       .then_inc(u_ps, 1)

            def step(g, b, u, mix):
                one = not (isinstance(g, int) and g == NG)
                two = seen(g)
                if one:
                    transposes(g, b, u, 0)
                    transposes(g, b, u, 1)
                mix_slot(mix, 0)
                if one:
                    project(g, 0)
                mix_slot(mix, 1)
                if two:
                    scores_to_rows(g - 1, 1 - b)
                if one:
                    transposes(g, b, u, 2)
                mix_slot(mix, 2)
                if one:
                    project(g, 1)
                mix_slot(mix, 3)
                if two:
                    rows_back(g - 1)
                if one:
                    transposes(g, b, u, 3)
                mix_slot(mix, 4)
                if one:
                    project(g, 2)
                mix_slot(mix, 5)
                if two:
                    sum_nodes(g - 1, 1 - b, range(0, G // 2))
                mix_slot(mix, 6)
                if one:
                    project(g, 3)
                mix_slot(mix, 7)
                if two:
                    sum_nodes(g - 1, 1 - b, range(G // 2, G))
                if isinstance(g, int) and g == FIRST - 1:
                    eng.wait_ge(loaded, 13 * 16)

            drive(eng, step)

        @block.scalar
        def _(eng):
            def mix_slot(mix, s):
                if mix is None:
                    return
                k, s = mix[0], mix[1] + s
                if s == 0:
                    eng.wait_ge(mx_ps[0], k + 1)
                    eng.activation(xnT.rearrange("p k n -> p (k n)"), M[:, 0:D], ACT.Copy).then_inc(mx_act[0], 1)
                elif s == 1:
                    eng.wait_ge(mx_dve[0], k + 1)
                    for c in range(KD):
                        eng.activation(qpos[:, c], M[:, c * P:(c + 1) * P], ACT.Relu, bias=bq[:, c:c + 1])
                    eng.activation(qneg.rearrange("p k n -> p (k n)"), qneg.rearrange("p k n -> p (k n)"), ACT.Exp)\
                       .then_inc(mx_act[1], 1)
                elif s == 4:
                    eng.wait_ge(mx_ps[3], k + 1)
                    eng.activation(attnT.rearrange("p k n -> p (k n)"), M[:, 0:D], ACT.Copy).then_inc(mx_act[3], 1)
                elif s == 6:
                    eng.wait_ge(mx_dve[6], k + 1)
                    eng.activation(m_std, m_mom[:, 1:2], ACT.Sqrt, bias=eps[:]).then_inc(mx_act[4], 1)
                elif s == 7:
                    eng.wait_ge(mx_ps[5], k + 1)
                    eng.activation(x1T.rearrange("p k n -> p (k n)"), M[:, 0:D], ACT.Copy).then_inc(mx_act[5], 1)
                elif s in (8, 9):
                    part_ = s - 8
                    eng.wait_ge(mx_ps[6 + part_], k + 1)
                    for f in range(FC // 2):
                        ff = part_ * (FC // 2) + f
                        last = eng.activation(hid[:, ff], M[:, f * P:(f + 1) * P], ACT.Relu, bias=b1[:, ff:ff + 1])
                    last.then_inc(mx_act[6 + part_], 1)
                elif s == 11:
                    eng.wait_ge(mx_dve[13], k + 1)
                    eng.activation(m_std, m_mom[:, 1:2], ACT.Sqrt, bias=eps[:]).then_inc(mx_act[2], 1)

            def move(g, j):
                eng.wait_ge(eaT_ps, PAIRS * g + j + 1)
                if seen(g, 1) or j >= 2:
                    eng.wait_ge(e_ps, PAIRS * g + j - 1)
                eng.activation(eaT[j % 2].rearrange("p k n -> p (k n)"), T[j % 2][:], ACT.Copy).then_inc(eaT_sb, 1)

            def exponentials(g):
                eng.wait_ge(diff_ready, g + 1)
                if seen(g):
                    eng.wait_ge(back_ps, g)
                eng.activation(prob[0:SG], diff[0:SG], ACT.Exp, scale=SCALE).then_inc(prob_ready, 1)

            def sums_out(g, b, u, tiles):
                for t in tiles:
                    eng.wait_ge(u_ps, G * g + t + 1)
                    if t == 0 and seen(g, 2):
                        eng.wait_ge(part_out[b], 16 * u)
                    eng.activation(part[b][:, t, 0:MSG], U[t % 2][:, 0:MSG], ACT.Copy).then_inc(u_sb, 1)

            def step(g, b, u, mix):
                one = not (isinstance(g, int) and g == NG)
                two = seen(g)
                if one:
                    move(g, 0)
                    move(g, 1)
                mix_slot(mix, 0)
                mix_slot(mix, 1)
                if one:
                    move(g, 2)
                mix_slot(mix, 2)
                if two:
                    exponentials(g - 1)
                mix_slot(mix, 3)
                if one:
                    move(g, 3)
                mix_slot(mix, 4)
                mix_slot(mix, 5)
                if two:
                    sums_out(g - 1, 1 - b, u - 1 + b, range(0, G // 2))
                mix_slot(mix, 6)
                mix_slot(mix, 7)
                if two:
                    sums_out(g - 1, 1 - b, u - 1 + b, range(G // 2, G))

            drive(eng, step)

        @block.vector
        def _(eng):
            eng.memset(keep[:], -BIG).then_inc(edge_made, 1)
            eng.wait_ge(edge_made, 1)

            def mix_slot(mix, s):
                if mix is None:
                    return
                k, s = mix[0], mix[1] + s

                def moments(first, done):
                    eng.bn_stats(m_st6, y).then_inc(mx_dve[first], 1)
                    hold(eng, mx_dve[first], k + 1, passed)
                    eng.bn_aggr(m_mom, m_st6).then_inc(mx_dve[done], 1)

                if s == 1:
                    eng.wait_ge(mx_ps[1], k + 1)
                    for c in range(KD):
                        last = eng.tensor_scalar(qneg[:, c], M[:, c * P:(c + 1) * P], bq[:, c:c + 1], 0.0,
                                                 ALU.add, ALU.min)
                    last.then_inc(mx_dve[0], 1)
                elif s == 2:
                    eng.wait_ge(mx_act[1], k + 1)
                    eng.tensor_tensor(qneg, qneg, qpos, ALU.add).then_inc(mx_dve[1], 1)
                elif s == 3:
                    eng.wait_ge(mx_ps[2], k + 1)
                    sums = M[:, 0:KD * KVW].rearrange("p (c w) -> p c w", c=KD)
                    eng.tensor_scalar(den.rearrange("p (c h) -> p c h", c=KD), sums[:, :, P:KVW], 1e-6, None,
                                      ALU.add).then_inc(mx_dve[2], 1)
                    eng.wait_ge(mx_dve[2], k + 1)
                    eng.reciprocal(den, den).then_inc(mx_dve[3], 1)
                    eng.wait_ge(mx_dve[3], k + 1)
                    hk = H // KD
                    for c in range(KD):
                        last = eng.tensor_tensor(
                            attn[:, c * P:(c + 1) * P].rearrange("p (h c) -> p h c", h=hk),
                            M[:, c * KVW:c * KVW + P].rearrange("p (h c) -> p h c", h=hk),
                            den[:, c * hk:(c + 1) * hk].rearrange("p (h o) -> p h o", o=1).to_broadcast([P, hk, C]),
                            ALU.mult)
                    last.then_inc(mx_dve[4], 1)
                elif s == 5:
                    eng.tensor_tensor(xm, mx_xn, bo, ALU.add).then_inc(mx_dve[5], 1)
                    eng.wait_ge(mx_ps[4], k + 1)
                    eng.wait_ge(mx_dve[5], k + 1)
                    eng.tensor_tensor(y, M[:, 0:D], xm, ALU.add).then_inc(mx_dve[7], 1)
                    eng.wait_ge(mx_dve[7], k + 1)
                    moments(16, 6)
                elif s == 10:
                    eng.tensor_tensor(xm, x1, b2, ALU.add).then_inc(mx_dve[11], 1)
                    eng.wait_ge(mx_ps[8], k + 1)
                    eng.wait_ge(mx_dve[11], k + 1)
                    eng.tensor_tensor(y, M[:, 0:D], xm, ALU.add).then_inc(mx_dve[12], 1)
                    eng.wait_ge(mx_dve[12], k + 1)
                    moments(15, 13)

            def pair(g, b, u, j):
                n = PAIRS * g + j
                e2 = E_ps[j % 2][:].rearrange("p (t c) -> p t c", t=2)
                eng.wait_ge(gathered[b][j], 64 * (u + 1))
                eng.wait_ge(e_ps, n + 1)
                if seen(g, 1) or j >= 2:
                    eng.wait_ge(alpha_ready, n - 1)
                eng.tensor_tensor(kj[j % 2], kv[b][:, 2 * j:2 * j + 2, 0:D], e2, ALU.add).then_inc(kj_ready, 1)
                eng.tensor_tensor(ve[b][:, 2 * j:2 * j + 2], kv[b][:, 2 * j:2 * j + 2, D:], e2, ALU.add)\
                   .then_inc(ve_ready, 1)
                eng.wait_ge(kj_ready, n + 1)
                eng.tensor_tensor(kj[j % 2], kj[j % 2], q[b][:, 2 * j:2 * j + 2], ALU.mult).then_inc(prod_ready, 1)

            def score(g, b, j):
                n = PAIRS * g + j
                eng.wait_ge(prod_ready, n + 1)
                eng.tensor_reduce(alpha[b][:, 2 * j * H:2 * (j + 1) * H],
                                  kj[j % 2].rearrange("p t (h c) -> p (t h) c", h=H), AX, ALU.add)\
                   .then_inc(alpha_ready, 1)

            def same_nodes(g, b, tiles):
                for t in tiles:
                    eng.tensor_scalar(same[b][:, t], dst_all[b][:, t].bitcast(I32), dst_cf[b][:, t:t + 1], None,
                                      ALU.is_equal).then_inc(same_ready, 1)

            def neighbours(g, b, u):
                eng.wait_ge(row_in[b], 16 * (u + 1))
                row = dst_row[b][0:SG].bitcast(I32)
                eng.tensor_tensor(keep[0:SG, 1:P], row[:, 1:P], row[:, 0:P - 1], ALU.is_equal).then_inc(same_row, 1)
                eng.tensor_copy(dst_cf[b], dst_f[:, bass.ds(g * G, G)]).then_inc(dstc_ready, 1)
                eng.wait_ge(same_row, g + 1)
                eng.tensor_scalar(keep[0:SG, 1:P], keep[0:SG, 1:P], 1.0, BIG, ALU.subtract, ALU.mult)\
                   .then_inc(keep_ready, 1)
                eng.wait_ge(dstc_ready, g + 1)
                eng.wait_ge(all_in[b], 16 * (u + 1))
                if seen(g, 2):
                    eng.wait_ge(u_ps, G * (g - 1))
                same_nodes(g, b, range(0, 4))

            def maxima(g):
                eng.wait_ge(keep_ready, g + 1)
                eng.wait_ge(alphaT_ps, g + 1)
                if seen(g):
                    eng.wait_ge(back_ps, g)
                eng.tensor_tensor_scan(left[0:SG], keep[0:SG, 0:P], S[0:SG, 0:P], -BIG, ALU.add, ALU.max)\
                   .then_inc(left_ready, 1)
                eng.wait_ge(left_ready, g + 1)
                eng.tensor_tensor_scan(peak[0:SG, ::-1], keep[0:SG, 1:P + 1][:, ::-1], left[0:SG, ::-1], -BIG,
                                       ALU.add, ALU.max).then_inc(peak_ready, 1)
                eng.wait_ge(peak_ready, g + 1)
                if seen(g):
                    eng.wait_ge(prob_ready, g)
                eng.tensor_tensor(diff[0:SG], S[0:SG, 0:P], peak[0:SG], ALU.subtract).then_inc(diff_ready, 1)

            def weights_in(g, b, u):
                eng.wait_ge(back_ps, g + 1)
                eng.tensor_copy(msg[b][:, :, D:MSG], S[:, P:P + SG].rearrange("p (t h) -> p t h", t=G))\
                   .then_inc(weights_sb, 1)
                if seen(g, 2):
                    eng.wait_ge(part_out[b], 16 * u)
                eng.tensor_copy(part[b][:, :, MSG + H], dst_cf[b])
                eng.tensor_copy(part[b][:, :, MSG:MSG + H], S[:, P + SG:P + 2 * SG].rearrange("p (t h) -> p t h", t=G))\
                   .then_inc(peaks_sb, 1)
                eng.wait_ge(weights_sb, g + 1)

            def messages(g, b, j):
                t = slice(2 * j, 2 * j + 2)
                eng.tensor_tensor(msg[b][:, t, 0:D].rearrange("p t (h c) -> p t h c", h=H),
                                  ve[b][:, t].rearrange("p t (h c) -> p t h c", h=H),
                                  per_head(msg[b][:, t, D:MSG], 2), ALU.mult).then_inc(msg_ready, 1)

            def normalised(mix, s):
                k = mix[0]
                first = mix[1] + s == 6
                n = 8 if first else 14
                z = x1 if first else y
                per = 2 if first else 4
                eng.wait_ge(mx_act[4] if first else mx_act[2], k + 1)
                eng.reciprocal(m_rstd, m_std).then_inc(mx_dve[n], 1)
                eng.wait_ge(mx_dve[n], per * k + 1)
                eng.tensor_scalar(z, y, m_mom[:, 0:1], m_rstd, ALU.subtract, ALU.mult).then_inc(mx_dve[n], 1)
                eng.wait_ge(mx_dve[n], per * k + 2)
                if first:
                    eng.tensor_tensor(z, z, g1, ALU.mult).then_inc(mx_dve[9], 1)
                    eng.wait_ge(mx_dve[9], k + 1)
                    eng.tensor_tensor(z, z, h1, ALU.add).then_inc(mx_dve[10], 1)
                else:
                    eng.tensor_tensor(z, z, g2, ALU.mult).then_inc(mx_dve[n], 1)
                    eng.wait_ge(mx_dve[n], per * k + 3)
                    eng.tensor_tensor(z, z, h2, ALU.add).then_inc(mx_dve[n], 1)
                    eng.wait_ge(mx_dve[n], per * k + 4)
                    if seen(k):
                        eng.wait_ge(mx_stored, 16 * k)
                    eng.tensor_tensor(mx_out, z, mx_xs, ALU.add).then_inc(mx_dve[17], 1)

            def slot(mix, s):
                if mix is None:
                    return
                if mix[1] + s in (6, 11):
                    normalised(mix, s)
                else:
                    mix_slot(mix, s)

            def step(g, b, u, mix):
                one = not (isinstance(g, int) and g == NG)
                two = seen(g)
                h, c, w = g - 1, 1 - b, u - 1 + b
                if two:
                    neighbours(h, c, w)
                slot(mix, 0)
                if one:
                    pair(g, b, u, 0)
                if two:
                    same_nodes(h, c, range(4, G))
                if one:
                    score(g, b, 0)
                slot(mix, 1)
                if two:
                    maxima(h)
                slot(mix, 2)
                if one:
                    pair(g, b, u, 1)
                    score(g, b, 1)
                slot(mix, 3)
                if two:
                    weights_in(h, c, w)
                slot(mix, 4)
                if one:
                    pair(g, b, u, 2)
                if two:
                    messages(h, c, 0)
                if one:
                    score(g, b, 2)
                if two:
                    messages(h, c, 1)
                slot(mix, 5)
                if two:
                    messages(h, c, 2)
                slot(mix, 6)
                if one:
                    pair(g, b, u, 3)
                if two:
                    messages(h, c, 3)
                if one:
                    score(g, b, 3)
                slot(mix, 7)
                if isinstance(g, int) and g == FIRST - 1:
                    eng.wait_ge(loaded, 13 * 16)

            drive(eng, step)


def merge(nc, sem, psum, ident, dst_f, node_f, last_i, carve, dst, part_d, extra_d):
    MR = 104
    MC = TILES // MR
    assert MR * MC == TILES
    FAR = 100000.0
    pick, ends, hits = carve(P), carve(TILES), carve(TILES)
    tile_f, tile_i, cnt = carve(NT), carve(NT), carve(NT)
    lots = [carve(P) for _ in range(2)]
    at = [carve(1) for _ in range(2)]
    row, ext, res = carve(ROW), carve(ROW), carve(ROW)
    nxt, prev, own1 = carve(1), carve(1), carve(1)
    own1_i = carve(1)
    over, first, key, to_f, to_i, from_i = (carve(1) for _ in range(6))
    keys, keysT, same = carve(MR), carve(MR), carve(MR)
    keep, left, peak = carve(MR + 1), carve(MR), carve(MR)
    d, w = carve(2 * H), carve(2 * H)
    ends_ps, K, S, Sum = psum[0:2], psum[2], psum[3], psum[4]

    passed = sem("mg_passed")
    made, pick0 = sem("mg_made"), sem("pick0")
    ends_done, chain = sem("ends_ps"), sem("mg_dve")
    tiles_found, at_ready = sem("tiles_found"), sem("at_ready")
    lots_in = [sem(f"lots_in{b}") for b in range(2)]
    counted, found = sem("counted"), sem("last_found")
    mg_in, index_made, keys_made, ext_in = sem("mg_in"), sem("mg_index"), sem("mg_keys"), sem("ext_in")
    keyT_ps, peakT, weights, scaled, sum_ps, res_ready, res_out = (sem(n) for n in (
        "keyT_ps", "peakT", "mg_weights", "mg_scaled", "mg_sum_ps", "res_ready", "res_out"))
    peaks_made, diffs = sem("mg_peaks"), sem("mg_diffs")
    dst_rows = dst.rearrange("(t e) -> t e", e=P)
    parts = part_d.rearrange("(t e) w -> t e w", e=P)

    def chunk_rows(eng, c):
        STEPS = 12
        n = [0]

        def link(ins):
            n[0] += 1
            ins.then_inc(chain, 1)
            eng.wait_ge(chain, NT + 2 + STEPS * c + n[0])

        r = slice(0, MR)
        node = row[r, MSG + H:ROW]
        eng.wait_ge(mg_in, 48 * (c + 1))
        link(eng.tensor_tensor(over[r], node, nxt[r].bitcast(I32), ALU.is_equal))
        link(eng.tensor_tensor(first[r], node, prev[r].bitcast(I32), ALU.not_equal))
        link(eng.scalar_tensor_tensor(key[r], node, own1[r], over[r], ALU.add, ALU.mult))
        link(eng.tensor_tensor(key[r], key[r], own1[r], ALU.subtract))
        eng.tensor_copy(keys[r], key[r].to_broadcast([MR, MR])).then_inc(keys_made, 1)
        link(eng.tensor_tensor(first[r], first[r], over[r], ALU.mult))
        link(eng.scalar_tensor_tensor(to_f[r], node, FAR, first[r], ALU.subtract, ALU.mult))
        eng.wait_ge(res_out, 16 * c)
        eng.tensor_scalar(to_i[r].bitcast(I32), to_f[r], FAR, None, ALU.add).then_inc(index_made, 1)
        eng.tensor_copy(from_i[r].bitcast(I32), node).then_inc(index_made, 1)
        eng.wait_ge(keyT_ps, c + 1)
        link(eng.tensor_copy(keysT[r], K[r, 0:MR]))
        eng.tensor_scalar(same[r], keysT[r], key[r], None, ALU.is_equal).then_inc(scaled, 1)
        link(eng.tensor_tensor(keep[0:H, 1:MR], keysT[0:H, 1:MR], keysT[0:H, 0:MR - 1], ALU.is_equal))
        link(eng.tensor_scalar(keep[0:H, 1:MR], keep[0:H, 1:MR], 1.0, BIG, ALU.subtract, ALU.mult))
        link(eng.tensor_tensor_scan(left[0:H], keep[0:H, 0:MR], S[0:H, 0:MR], -BIG, ALU.add, ALU.max))
        eng.tensor_tensor_scan(peak[0:H, ::-1], keep[0:H, 1:MR + 1][:, ::-1], left[0:H, ::-1], -BIG,
                               ALU.add, ALU.max).then_inc(peaks_made, 1)
        eng.wait_ge(peakT, c + 1)
        eng.wait_ge(ext_in, 16 * (c + 1))
        link(eng.tensor_tensor(res[r, MSG:MSG + H], S[r, P:P + H], ext[r, MSG:MSG + H], ALU.max))
        eng.tensor_tensor(d[r, 0:H], row[r, MSG:MSG + H], res[r, MSG:MSG + H], ALU.subtract).then_inc(diffs, 1)
        eng.tensor_tensor(d[r, H:], ext[r, MSG:MSG + H], res[r, MSG:MSG + H], ALU.subtract).then_inc(diffs, 1)
        eng.wait_ge(weights, c + 1)

        def weigh(rows, ws):
            eng.tensor_tensor(heads(rows[r, 0:D]), heads(rows[r, 0:D]),
                              ws.rearrange("p (h o) -> p h o", o=1).to_broadcast([MR, H, C]), ALU.mult)
            return eng.tensor_tensor(rows[r, D:MSG], rows[r, D:MSG], ws, ALU.mult)

        weigh(row, w[r, 0:H]).then_inc(scaled, 1)
        link(weigh(ext, w[r, H:]))
        eng.tensor_copy(res[r, MSG + H:ROW], node)
        eng.wait_ge(sum_ps, c + 1)
        eng.tensor_tensor(res[r, 0:MSG], ext[r, 0:MSG], Sum[r, 0:MSG], ALU.add).then_inc(res_ready, 1)
        assert n[0] == STEPS, n

    with nc.Block() as block:
        @block.sync
        def _(eng):
            eng.wait_ge(made, 4)

            with eng.Fori(0, MC) as c:
                eng.wait_ge(res_ready, c)
                with nc.allow_non_contiguous_dma("one number of a tile"):
                    eng.dma_start(row[0:MR], parts[bass.ds(c * MR, MR), P - 1, :]).then_inc(mg_in, 16)
                    eng.dma_start(nxt[0:MR].bitcast(I32), dst_rows[bass.ds(c * MR + 1, MR), 0:1]).then_inc(mg_in, 16)
                    eng.dma_start(prev[1:MR].bitcast(I32), dst_rows[bass.ds(c * MR, MR - 1), P - 1:P])\
                       .then_inc(mg_in, 16)

        @block.gpsimd
        def _(eng):
            eng.memset(pick, 0.0).then_inc(pick0, 1)
            eng.memset(prev.bitcast(I32), -1).then_inc(made, 1)
            eng.memset(keep, -BIG).then_inc(made, 1)
            eng.iota(own1_i.bitcast(I32), pattern=[[0, 1]], base=1, channel_multiplier=1).then_inc(pick0, 1)
            eng.wait_ge(pick0, 2)
            eng.affine_select(out=pick, in_=pick, compare_op=ALU.not_equal, fill=1.0, base=-(P - 1),
                              pattern=[[0, P]], channel_multiplier=1).then_inc(made, 1)
            eng.tensor_copy(own1, own1_i.bitcast(I32)).then_inc(made, 1)

            eng.wait_ge(tiles_found, 1)

            def look_up(i, b, u):
                if not isinstance(i, int) or i >= 2:
                    eng.wait_ge(counted, i - 1)
                eng.tensor_copy(at[b].bitcast(I32), tile_i[:, bass.ds(i, 1)].bitcast(I32)).then_inc(at_ready, 1)
                hold(eng, at_ready, i + 1, passed)
                eng.indirect_dma_start(lots[b].bitcast(I32), None, dst_rows, bass.IndirectOffsetOnAxis(
                    at[b].bitcast(I32), 0), bounds_check=TILES - 1, oob_is_err=False).then_inc(lots_in[b], 16)

            look_up(0, 0, 0)
            with eng.Fori(0, (NT - 1) // 2) as k:
                look_up_pair(k, look_up)

            with eng.Fori(0, MC) as c:
                eng.wait_ge(index_made, 2 * c + 2)
                hold(eng, res_out, 16 * c, passed)
                eng.indirect_dma_start(ext[0:MR], None, extra_d, bass.IndirectOffsetOnAxis(
                    from_i[0:MR].bitcast(I32), 0), bounds_check=NP - 1, oob_is_err=False).then_inc(ext_in, 16)
                hold(eng, res_ready, c + 1, passed)
                eng.indirect_dma_start(extra_d, bass.IndirectOffsetOnAxis(to_i[0:MR].bitcast(I32), 0),
                                       res[0:MR], None, bounds_check=NP - 1, oob_is_err=False).then_inc(res_out, 16)
            eng.wait_ge(res_out, 16 * MC)

        @block.tensor
        def _(eng):
            eng.wait_ge(made, 4)
            half = TILES // 2
            for n in range(2):
                mm = eng.matmul(ends_ps[n][:, 0:half], pick, dst_f[:, n * half:(n + 1) * half], start=True, stop=True)
            mm.then_inc(ends_done, 1)
            with eng.Fori(0, MC) as c:
                hold(eng, keys_made, c + 1, passed)
                eng.transpose(K[0:MR, 0:MR], keys[0:MR], ident[0:MR, 0:MR])
                eng.transpose(S[0:H, 0:MR], row[0:MR, MSG:MSG + H], ident[0:MR, 0:MR]).then_inc(keyT_ps, 1)
                hold(eng, peaks_made, c + 1, passed)
                eng.transpose(S[0:MR, P:P + H], peak[0:H], ident[0:H, 0:H]).then_inc(peakT, 1)
                hold(eng, scaled, 2 * c + 2, passed)
                eng.matmul(Sum[0:MR, 0:MSG], same[0:MR], row[0:MR, 0:MSG], start=True, stop=True).then_inc(sum_ps, 1)

        @block.scalar
        def _(eng):
            with eng.Fori(0, MC) as c:
                eng.wait_ge(diffs, 2 * c + 2)
                eng.activation(w[0:MR], d[0:MR], ACT.Exp, scale=SCALE).then_inc(weights, 1)

        @block.vector
        def _(eng):
            eng.wait_ge(made, 4)
            eng.wait_ge(ends_done, 1)
            half = TILES // 2
            for n in range(2):
                last = eng.tensor_copy(ends[:, n * half:(n + 1) * half], ends_ps[n][:, 0:half])
            last.then_inc(chain, 1)
            eng.wait_ge(chain, 1)
            with eng.Fori(0, NT) as i:
                eng.tensor_scalar(hits, ends, node_f[:, bass.ds(i, 1)], 0.0, ALU.is_le, ALU.add,
                                  accum_out=tile_f[:, bass.ds(i, 1)]).then_inc(chain, 1)
                eng.wait_ge(chain, i + 2)
            eng.tensor_scalar(tile_f, tile_f, float(TILES - 1), None, ALU.min).then_inc(chain, 1)
            eng.wait_ge(chain, NT + 2)
            eng.tensor_copy(tile_i.bitcast(I32), tile_f).then_inc(tiles_found, 1)

            def count(i, b, u):
                eng.wait_ge(lots_in[b], 16 * (u + 1))
                eng.tensor_scalar(hits[:, 0:P], lots[b].bitcast(I32), node_f[:, bass.ds(i, 1)], 0.0, ALU.is_le,
                                  ALU.add, accum_out=cnt[:, bass.ds(i, 1)]).then_inc(counted, 1)
                eng.wait_ge(counted, i + 1)

            count(0, 0, 0)
            with eng.Fori(0, (NT - 1) // 2) as k:
                count(2 * k + 1, 1, k)
                count(2 * k + 2, 0, k + 1)
            eng.scalar_tensor_tensor(tile_f, tile_f, float(P), cnt, ALU.mult, ALU.add).then_inc(found, 1)
            eng.wait_ge(found, 1)
            eng.tensor_scalar(last_i[:], tile_f, -1.0, 0.0, ALU.add, ALU.max).then_inc(found, 1)

            with eng.Fori(0, MC) as c:
                chunk_rows(eng, c)


def look_up_pair(k, look_up):
    look_up(2 * k + 1, 1, k)
    look_up(2 * k + 2, 0, k + 1)


def experts(nc, sem, psum, ident, eps, node_f, last_i, carve, part_d, extra_d, x1_d, gate_w, gate_b, W1, b1, W2,
            b2, out):
    w1 = carve(NE * KD, HD)
    w2 = carve(NE * HC, D)
    xfT = carve(KD, NP)
    acc = carve(NT, D)
    gw, gb = carve(KD, NE), carve(NE)
    b1c = carve(NE * HC)
    b2r = carve(D)
    cw = carve(NT, NE)
    lead = carve(NE)
    lead_i = carve(NE)
    cwT = carve(MACRO * P)
    cwm = carve(MACRO, NE)
    hid_at = carve.at
    hid = carve(HC, MACRO * P)
    early = Carve(carve.arena, hid_at + HC * MACRO * P)
    early.at = hid_at
    row = [early(ROW) for _ in range(2)]
    ext = [early(ROW) for _ in range(2)]
    x1 = [early(D) for _ in range(2)]
    at = [early(1) for _ in range(2)]
    xfTt = [early(KD, P) for _ in range(2)]
    has, off, peak, d, w = early(1), early(1), early(H), early(2 * H), early(2 * H)
    st6, mom, std, rstd, xf = early(6), early(2), early(1), early(1), early(D)
    late = Carve(carve.arena, hid_at + HC * MACRO * P)
    late.at = hid_at
    prob, hit, rank, one, two = (late(NT, NE) for _ in range(5))
    top = late(NT)

    passed = sem("ex_passed")
    made, lead0, loaded, gates_in = sem("ex_made"), sem("lead0"), sem("ex_loaded"), sem("gates_in")
    at_ready = sem("ex_at")
    row_in = [sem(f"main_in{b}") for b in range(2)]
    ext_in = [sem(f"extra_in{b}") for b in range(2)]
    chain, diffs, weights, mom_ready, std_ready = (sem(n) for n in (
        "ex_dve", "ex_diffs", "ex_weights", "ex_mom", "ex_std"))
    xfT_kept, cw_ready = sem("xfT_kept"), sem("cw_block")
    xf_ready, xfT_ps, xfT_sb, gate_ps, logits = (sem(n) for n in ("xf_ready", "xfT_ps", "xfT_sb", "gate_ps", "logits"))
    shifted, exps, routed = sem("gates_shifted"), sem("gates_exp"), sem("routed")
    cwT_ps, cwT_sb, h_ps, hid_ready, y_ps, added = (sem(n) for n in (
        "cwT_ps", "cwT_sb", "h_ps", "hid_ready", "y_ps", "added"))
    out_done = sem("out_done")
    T, L = psum[0:2], psum[2:4]
    Hb, Y = psum[0:4], psum[4:8]
    YS = (NE + 1) * MACRO

    def drive(eng, step):
        for i in range(3):
            step(i, i % 2, i // 2)
        with eng.Fori(1, (NT - 1) // 2) as k:
            step(2 * k + 1, 1, k)
            step(2 * k + 2, 0, k + 1)

    with nc.Block() as block:
        @block.sync
        def _(eng):
            eng.dma_start(gw, gate_w.rearrange("(k p) n -> p k n", p=P)).then_inc(gates_in, 16)
            eng.dma_start(gb, over_partitions(gate_b)).then_inc(gates_in, 16)

            def step(i, b, u):
                if not isinstance(i, int) or i >= 2:
                    eng.wait_ge(xf_ready, i - 1)
                eng.dma_start(ext[b], extra_d[bass.ds(i * P, P), :]).then_inc(ext_in[b], 16)
                eng.dma_start(x1[b], x1_d[bass.ds(i * P, P), :]).then_inc(ext_in[b], 16)
                if isinstance(i, int) and i == 2:
                    eng.dma_start(w1, W1.rearrange("e (k p) n -> p (e k) n", p=P)).then_inc(loaded, 16)
                    eng.dma_start(w2, W2.rearrange("e (k p) n -> p (e k) n", p=P)).then_inc(loaded, 16)
                    with nc.allow_non_contiguous_dma("biases, once"):
                        eng.dma_start(b1c, b1.rearrange("e (k p) -> p (e k)", p=P)).then_inc(loaded, 16)
                    eng.dma_start(b2r[0:NE], b2).then_inc(loaded, 16)

            drive(eng, step)
            rows = out[0:(NT - 1) * P, :].rearrange("(t p) c -> p t c", p=P)
            with eng.Fori(0, MACROS - 1) as m:
                eng.wait_ge(added, YS * m + YS)
                eng.dma_start(rows[:, bass.ds(m * MACRO, MACRO), :], acc[:, bass.ds(m * MACRO, MACRO), :])\
                   .then_inc(out_done, 16)
            eng.wait_ge(added, YS * MACROS)
            first = NT - MACRO
            eng.dma_start(rows[:, first:NT - 1, :], acc[:, first:NT - 1, :]).then_inc(out_done, 16)
            eng.dma_start(out[(NT - 1) * P:N, :], acc[0:LAST, NT - 1, :]).then_inc(out_done, 16)
            eng.wait_ge(out_done, 16 * (MACROS + 1))

        @block.gpsimd
        def _(eng):
            eng.iota(lead_i.bitcast(I32), pattern=[[-1, NE]], base=NE, channel_multiplier=0).then_inc(lead0, 1)
            eng.wait_ge(lead0, 1)
            eng.tensor_copy(lead, lead_i.bitcast(I32)).then_inc(made, 1)

            def step(i, b, u):
                if not isinstance(i, int) or i >= 2:
                    eng.wait_ge(xf_ready, i - 1)
                eng.tensor_copy(at[b].bitcast(I32), last_i[:, bass.ds(i, 1)]).then_inc(at_ready, 1)
                hold(eng, at_ready, i + 1, passed)
                eng.indirect_dma_start(row[b], None, part_d, bass.IndirectOffsetOnAxis(at[b].bitcast(I32), 0),
                                       bounds_check=EP - 1, oob_is_err=False).then_inc(row_in[b], 16)

            def keep_tile(i, b):
                eng.wait_ge(xfT_sb, i + 1)
                eng.tensor_copy(xfT[:, :, bass.ds(i * P, P)], xfTt[b]).then_inc(xfT_kept, 1)

            step(0, 0, 0)
            step(1, 1, 0)
            keep_tile(0, 0)
            step(2, 0, 1)
            with eng.Fori(1, (NT - 1) // 2) as k:
                keep_tile(2 * k - 1, 1)
                step(2 * k + 1, 1, k)
                keep_tile(2 * k, 0)
                step(2 * k + 2, 0, k + 1)
            keep_tile(NT - 2, 1)
            keep_tile(NT - 1, 0)

        @block.tensor
        def _(eng):
            eng.wait_ge(gates_in, 32)

            def step(i, b, u):
                eng.wait_ge(xf_ready, i + 1)
                for c in range(KD):
                    mm = eng.transpose(T[b][:, c * P:(c + 1) * P], xf[:, c * P:(c + 1) * P], ident[:])
                mm.then_inc(xfT_ps, 1)
                eng.wait_ge(xfT_sb, i + 1)
                if not isinstance(i, int) or i >= 2:
                    eng.wait_ge(logits, i - 1)
                for c in range(KD):
                    mm = eng.matmul(L[b][:, 0:NE], xfTt[b][:, c], gw[:, c], start=c == 0,
                                    stop=c == KD - 1)
                mm.then_inc(gate_ps, 1)

            drive(eng, step)
            eng.wait_ge(routed, 1)
            eng.wait_ge(xfT_kept, NT)
            eng.wait_ge(loaded, 64)

            def up(m, e, j):
                n = e * HC + j
                if not isinstance(m, int) or m or n >= 2:
                    eng.wait_ge(hid_ready, NE * HC * m + n - 1)
                for half in range(2):
                    for c in range(KD):
                        mm = eng.matmul(Hb[2 * (n % 2) + half][:, 0:HALF], w1[:, e * KD + c, j * P:(j + 1) * P],
                                        xfT[:, c, bass.ds(m * MACRO * P + half * HALF, HALF)],
                                        start=c == 0, stop=c == KD - 1)
                mm.then_inc(h_ps, 1)

            def free(m, n):
                if n >= 4:
                    eng.wait_ge(added, YS * m + n - 3)

            def macro(m):
                eng.wait_ge(cw_ready, m + 1)
                for t in range(MACRO):
                    mm = eng.transpose(Y[t // 4][0:NE, (t % 4) * P:(t % 4 + 1) * P], cwm[:, t], ident[:])
                mm.then_inc(cwT_ps, 1)
                up(m, 0, 0)
                eng.wait_ge(cwT_sb, m + 1)
                for t in range(MACRO):
                    free(m, t)
                    eng.matmul(Y[t % 4][:, 0:D], cwT[0:NE, t * P:(t + 1) * P], b2r[0:NE], start=True, stop=True)\
                       .then_inc(y_ps, 1)
                for e in range(NE):
                    for j in range(1, HC):
                        up(m, e, j)
                    if e < NE - 1:
                        up(m, e + 1, 0)
                    eng.wait_ge(hid_ready, NE * HC * m + (e + 1) * HC)
                    for t in range(MACRO):
                        n = (e + 1) * MACRO + t
                        free(m, n)
                        for j in range(HC):
                            mm = eng.matmul(Y[n % 4][:, 0:D], hid[:, j, t * P:(t + 1) * P], w2[:, e * HC + j],
                                            start=j == 0, stop=j == HC - 1)
                        mm.then_inc(y_ps, 1)

            macro(0)
            with eng.Fori(1, MACROS) as m:
                macro(m)

        @block.scalar
        def _(eng):
            def step(i, b, u):
                eng.wait_ge(diffs, 2 * i + 2)
                eng.activation(w, d, ACT.Exp, scale=SCALE).then_inc(weights, 1)
                eng.wait_ge(mom_ready, i + 1)
                eng.activation(std, mom[:, 1:2], ACT.Sqrt, bias=eps[:]).then_inc(std_ready, 1)
                eng.wait_ge(xfT_ps, i + 1)
                if not isinstance(i, int) or i >= 2:
                    eng.wait_ge(gate_ps, i - 1)
                    eng.wait_ge(xfT_kept, i - 1)
                eng.activation(xfTt[b].rearrange("p k n -> p (k n)"), T[b][:, 0:D], ACT.Copy).then_inc(xfT_sb, 1)

            drive(eng, step)
            eng.wait_ge(shifted, 1)
            eng.activation(prob.rearrange("p t e -> p (t e)"), prob.rearrange("p t e -> p (t e)"), ACT.Exp)\
               .then_inc(exps, 1)
            eng.wait_ge(loaded, 64)
            eng.wait_ge(routed, 1)

            with eng.Fori(0, MACROS) as m:
                for e in range(NE):
                    for j in range(HC):
                        n = e * HC + j
                        eng.wait_ge(h_ps, NE * HC * m + n + 1)
                        if j == 0:
                            eng.wait_ge(y_ps, YS * m + (e + 1) * MACRO if e else YS * m)
                        for half in range(2):
                            last = eng.activation(hid[:, j, half * HALF:(half + 1) * HALF],
                                                  Hb[2 * (n % 2) + half][:, 0:HALF], ACT.Gelu, bias=b1c[:, n:n + 1])
                        last.then_inc(hid_ready, 1)

        @block.vector
        def _(eng):
            eng.wait_ge(gates_in, 32)
            eng.wait_ge(made, 1)
            STEPS = 13

            def step(i, b, u):
                n = [0]

                def link(ins):
                    n[0] += 1
                    ins.then_inc(chain, 1)
                    eng.wait_ge(chain, STEPS * i + n[0])

                eng.wait_ge(row_in[b], 16 * (u + 1))
                eng.wait_ge(ext_in[b], 32 * (u + 1))
                link(eng.tensor_tensor(has, row[b][:, MSG + H:ROW], node_f[:, bass.ds(i, 1)], ALU.is_equal))
                link(eng.tensor_scalar(off, has, 1.0, BIG, ALU.subtract, ALU.mult))
                link(eng.tensor_scalar(row[b][:, MSG:MSG + H], row[b][:, MSG:MSG + H], has, off, ALU.mult, ALU.add))
                link(eng.tensor_tensor(peak, row[b][:, MSG:MSG + H], ext[b][:, MSG:MSG + H], ALU.max))
                eng.tensor_tensor(d[:, 0:H], row[b][:, MSG:MSG + H], peak, ALU.subtract).then_inc(diffs, 1)
                eng.tensor_tensor(d[:, H:], ext[b][:, MSG:MSG + H], peak, ALU.subtract).then_inc(diffs, 1)
                eng.wait_ge(weights, i + 1)
                link(eng.tensor_scalar(w[:, 0:H], w[:, 0:H], has, None, ALU.mult))
                for rows, ws in ((row[b], w[:, 0:H]), (ext[b], w[:, H:])):
                    eng.tensor_tensor(heads(rows[:, 0:D]), heads(rows[:, 0:D]), per_head(ws), ALU.mult)
                    last = eng.tensor_tensor(rows[:, D:MSG], rows[:, D:MSG], ws, ALU.mult)
                link(last)
                link(eng.tensor_tensor(row[b][:, 0:MSG], row[b][:, 0:MSG], ext[b][:, 0:MSG], ALU.add))
                link(eng.tensor_scalar(row[b][:, D:MSG], row[b][:, D:MSG], 1e-16, None, ALU.add))
                link(eng.reciprocal(row[b][:, D:MSG], row[b][:, D:MSG]))
                link(eng.tensor_tensor(heads(row[b][:, 0:D]), heads(row[b][:, 0:D]), per_head(row[b][:, D:MSG]),
                                       ALU.mult))
                link(eng.tensor_tensor(row[b][:, 0:D], row[b][:, 0:D], x1[b], ALU.add))
                eng.tensor_copy(acc[:, bass.ds(i, 1), :].rearrange("p o c -> p (o c)"), row[b][:, 0:D])
                link(eng.bn_stats(st6, row[b][:, 0:D]))
                eng.sem_inc(passed, 1)
                eng.bn_aggr(mom, st6).then_inc(mom_ready, 1)
                eng.wait_ge(std_ready, i + 1)
                link(eng.reciprocal(rstd, std))
                if not isinstance(i, int) or i >= 1:
                    eng.wait_ge(xfT_ps, i)
                eng.tensor_scalar(xf, row[b][:, 0:D], mom[:, 0:1], rstd, ALU.subtract, ALU.mult).then_inc(xf_ready, 1)
                eng.wait_ge(gate_ps, i + 1)
                eng.tensor_tensor(cw[:, bass.ds(i, 1), :].rearrange("p o e -> p (o e)"), L[b][:, 0:NE], gb, ALU.add)\
                   .then_inc(logits, 1)
                assert n[0] == STEPS, n

            drive(eng, step)
            eng.wait_ge(logits, NT)
            eng.wait_ge(xfT_kept, NT)
            done = [STEPS * NT]

            def link(ins):
                done[0] += 1
                ins.then_inc(chain, 1)
                eng.wait_ge(chain, done[0])

            def by_tile(ap):
                return ap.rearrange("p (t o) -> p t o", o=1).to_broadcast([P, NT, NE])

            link(eng.tensor_reduce(top, cw, AX, ALU.max))
            eng.tensor_tensor(prob, cw, by_tile(top), ALU.subtract).then_inc(shifted, 1)
            eng.wait_ge(exps, 1)
            link(eng.tensor_reduce(top, prob, AX, ALU.add))
            link(eng.reciprocal(top, top))
            link(eng.tensor_tensor(prob, prob, by_tile(top), ALU.mult))
            lead_t = lead.rearrange("p (o e) -> p o e", o=1).to_broadcast([P, NT, NE])
            link(eng.tensor_copy(two, prob))
            for chosen in (one, two):
                link(eng.tensor_reduce(top, two, AX, ALU.max))
                link(eng.tensor_tensor(hit, two, by_tile(top), ALU.is_equal))
                link(eng.tensor_tensor(rank, hit, lead_t, ALU.mult))
                link(eng.tensor_reduce(top, rank, AX, ALU.max))
                link(eng.tensor_tensor(chosen, rank, by_tile(top), ALU.is_equal))
                if chosen is one:
                    link(eng.scalar_tensor_tensor(two, one, -2.0, prob, ALU.mult, ALU.add))
            link(eng.tensor_tensor(one, one, two, ALU.add))
            eng.tensor_tensor(cw, prob, one, ALU.mult).then_inc(routed, 1)
            eng.wait_ge(routed, 1)

            with eng.Fori(0, MACROS) as m:
                eng.tensor_copy(cwm, cw[:, bass.ds(m * MACRO, MACRO), :]).then_inc(cw_ready, 1)
                eng.wait_ge(cwT_ps, m + 1)
                eng.tensor_copy(cwT[0:NE, 0:4 * P], Y[0][0:NE, :])
                eng.tensor_copy(cwT[0:NE, 4 * P:], Y[1][0:NE, 0:(MACRO - 4) * P]).then_inc(cwT_sb, 1)
                for n in range(YS):
                    e, t = n // MACRO - 1, n % MACRO
                    rows = acc[:, bass.ds(m * MACRO + t, 1), :].rearrange("p o c -> p (o c)")
                    eng.wait_ge(y_ps, YS * m + n + 1)
                    if e < 0:
                        eng.tensor_tensor(rows, Y[n % 4][:, 0:D], rows, ALU.add).then_inc(added, 1)
                    else:
                        eng.wait_ge(added, YS * m + n - MACRO + 1)
                        weight = cw[:, bass.ds(m * MACRO + t, 1), e:e + 1].rearrange("p o e -> p (o e)")
                        eng.scalar_tensor_tensor(rows, Y[n % 4][:, 0:D], weight, rows, ALU.mult, ALU.add)\
                           .then_inc(added, 1)


_INS = ["x", "src", "dst", "edge_attr_256", "L0_gnn_Wq", "L0_gnn_bq", "L0_gnn_Wk", "L0_gnn_bk", "L0_gnn_Wv",
        "L0_gnn_bv", "L0_gnn_We", "L0_gnn_Ws", "L0_gnn_bs", "L0_mix_Wq", "L0_mix_bq", "L0_mix_Wk", "L0_mix_bk",
        "L0_mix_Wv", "L0_mix_bv", "L0_mix_Wo", "L0_mix_bo", "L0_mix_W1", "L0_mix_b1", "L0_mix_W2", "L0_mix_b2",
        "L0_mix_ln1_g", "L0_mix_ln1_b", "L0_mix_ln2_g", "L0_mix_ln2_b", "L0_ffn_gate_w", "L0_ffn_gate_b",
        "L0_ffn_W1", "L0_ffn_b1", "L0_ffn_W2", "L0_ffn_b2"]


def kernel(**inputs):
    import numpy as np
    import concourse.bacc as bacc
    from concourse.bass_utils import run_bass_kernel_spmd

    nc = bacc.Bacc("TRN2", target_bir_lowering=False, num_devices=1)
    arrays, args = {}, {}
    for name in _INS:
        a = np.ascontiguousarray(inputs[name])
        if name == "x":
            a = np.concatenate([a, np.zeros((NP - N, D), a.dtype)])
        elif name == "edge_attr_256":
            a = np.concatenate([a, np.zeros((EP - E, D), a.dtype)])
        elif name == "src":
            a = np.concatenate([a, np.zeros(EP - E, a.dtype)])
        elif name == "dst":
            a = np.concatenate([a, np.full(EP - E, N, a.dtype), np.full(P, N + 1, a.dtype)])
        arrays[f"in_{name}"] = a
        args[name] = nc.dram_tensor(f"in_{name}", a.shape, mybir.dt.from_np(a.dtype), kind="ExternalInput").ap()
    out = nc.dram_tensor("out", [N, D], F32, kind="ExternalOutput").ap()
    build(nc, **args, out=out)
    return run_bass_kernel_spmd(nc, [arrays], core_ids=[0]).results[0]["out"]
```

```python
from contextlib import ExitStack

import concourse.bass as bass
from concourse import mybir

F32 = mybir.dt.float32
I32 = mybir.dt.int32
ALU = mybir.AluOpType
ACT = mybir.ActivationFunctionType
AX = mybir.AxisListType.X

P = 128
N, E, D, H = 6250, 106250, 256, 8
C = D // H
KD = D // P
NT = -(-N // P)
NP = NT * P
LAST = N - (NT - 1) * P
G = 8
PAIRS = G // 2
NG = -(-E // (P * G))
TILES = NG * G
EP = TILES * P
SCALE = float(C) ** -0.5
BIG = 1e30
MSG = D + H
ROW = MSG + H + 1
CHUNKS = -(-TILES // P)
FF = 1024
FC = FF // P
HD = 512
HC = HD // P
NE = 8
MACRO = 7
MACROS = NT // MACRO
SLOTS = (2 * NP + NE * (P - 1)) // P
XROW = D + 2 * NE
KVW = P + H // KD
LN_EPS = 1e-5


class Carve:

    def __init__(self, arena, size):
        self.arena, self.size, self.at = arena, size, 0

    def __call__(self, *shape):
        n = 1
        for s in shape:
            n *= s
        piece = self.arena[:, self.at:self.at + n]
        self.at += n
        assert self.at <= self.size, (self.at, self.size)
        if len(shape) == 2:
            return piece.rearrange("p (a b) -> p a b", a=shape[0])
        if len(shape) == 3:
            return piece.rearrange("p (a b c) -> p a b c", a=shape[0], b=shape[1])
        return piece


def rows_as_tiles(ap):
    return ap.rearrange("(t p) c -> p t c", p=P)


def over_partitions(ap):
    return ap.rearrange("(o n) -> o n", o=1).to_broadcast([P, ap.shape[0]])


def per_channel(ap):
    return ap.rearrange("(k p) -> p k", p=P)


def per_head(ap, tiles=None):
    if tiles is None:
        return ap.rearrange("p (h o) -> p h o", o=1).to_broadcast([P, H, C])
    return ap.rearrange("p t (h o) -> p t h o", o=1).to_broadcast([P, tiles, H, C])


def hold(eng, sem, value, passed):
    eng.wait_ge(sem, value)
    eng.sem_inc(passed, 1)


def heads(ap):
    return ap.rearrange("p (h c) -> p h c", h=H)


def build(nc, x, src, dst, edge_attr_256, L0_gnn_Wq, L0_gnn_bq, L0_gnn_Wk, L0_gnn_bk, L0_gnn_Wv, L0_gnn_bv,
          L0_gnn_We, L0_gnn_Ws, L0_gnn_bs, L0_mix_Wq, L0_mix_bq, L0_mix_Wk, L0_mix_bk, L0_mix_Wv, L0_mix_bv,
          L0_mix_Wo, L0_mix_bo, L0_mix_W1, L0_mix_b1, L0_mix_W2, L0_mix_b2, L0_mix_ln1_g, L0_mix_ln1_b,
          L0_mix_ln2_g, L0_mix_ln2_b, L0_ffn_gate_w, L0_ffn_gate_b, L0_ffn_W1, L0_ffn_b1, L0_ffn_W2, L0_ffn_b2,
          out):
    ctx = ExitStack()
    with ctx:
        def sb(name, shape, dt=F32):
            return ctx.enter_context(nc.sbuf_tensor(name, shape, dt))

        def stage(program, *operands):
            own = []

            def sem(name):
                own.append(nc.alloc_semaphore(name))
                return own[-1]

            program(nc, sem, psum, *operands)
            nc.clear_and_free_semaphores(own)
            nc.all_engine_barrier()

        def dram(name, shape, dt=F32):
            return nc.dram_tensor(name, shape, dt, kind="Internal").ap()

        kv_d = dram("kv_d", [NP, 2 * D])
        q_d = dram("q_d", [NP, D])
        xn_d = dram("xn_d", [NP, D])
        xs_d = dram("xs_d", [NP, D])
        x1_d = dram("x1_d", [NP, D])
        part_d = dram("part_d", [EP, ROW])
        slot_d = dram("slot_d", [SLOTS * P, XROW])
        y_d = dram("y_d", [2 * NP, D])
        extra_d = dram("extra_d", [NP, ROW])

        psum = [ctx.enter_context(nc.psum_tensor(f"bank{i}", [P, 512], F32)) for i in range(8)]
        ident = sb("ident", [P, P])
        eps = sb("eps", [P, 1])
        src_t = sb("src_t", [P, TILES], I32)
        dst_t = sb("dst_t", [P, TILES], I32)
        dst_f = sb("dst_f", [P, TILES])
        state = sb("state", [P, KD, KVW])
        last_i = sb("last_i", [P, NT], I32)
        node_f = sb("node_f", [P, NT])
        ARENA = 49500
        arena = sb("arena", [P, ARENA])

        stage(prepare, ident, eps, src_t, dst_t, dst_f, state, node_f, Carve(arena, ARENA), x, src, dst,
                (L0_gnn_Wk, L0_gnn_Wv, L0_gnn_Wq, L0_gnn_Ws, L0_mix_Wk, L0_mix_Wv),
                (L0_gnn_bk, L0_gnn_bv, L0_gnn_bq, L0_gnn_bs, L0_mix_bk, L0_mix_bv, L0_mix_ln2_b),
                kv_d, q_d, xn_d, xs_d, extra_d)
        stage(edges_and_mix, ident, eps, src_t, dst_t, dst_f, state, Carve(arena, ARENA), dst,
                      edge_attr_256, L0_gnn_We,
                      (L0_mix_Wq, L0_mix_Wo, L0_mix_W1, L0_mix_W2), (L0_mix_bq, L0_mix_b1),
                      (L0_mix_bo, L0_mix_ln1_g, L0_mix_ln1_b, L0_mix_b2, L0_mix_ln2_g),
                      kv_d, q_d, xn_d, xs_d, x1_d, part_d, slot_d)
        stage(merge, ident, dst_f, node_f, last_i, Carve(arena, ARENA), dst, part_d, extra_d)
        stage(experts, ident, eps, node_f, last_i, Carve(arena, ARENA), part_d, extra_d, x1_d,
                L0_ffn_gate_w, L0_ffn_gate_b, L0_ffn_W1, L0_ffn_b1, L0_ffn_W2, L0_ffn_b2, slot_d, y_d, out)


def prepare(nc, sem, psum, ident, eps, src_t, dst_t, dst_f, state, node_f, carve, x, src, dst, weights, biases,
            kv_d, q_d, xn_d, xs_d, extra_d):
    w6 = carve(6, KD, D)
    b6 = carve(7, D)
    xt = [carve(D) for _ in range(2)]
    xn = [carve(D) for _ in range(2)]
    xnT = [carve(KD, P) for _ in range(2)]
    kv = [carve(2 * D) for _ in range(2)]
    qs = [carve(2 * D) for _ in range(2)]
    mk = [carve(D) for _ in range(2)]
    mv = [carve(KD, P + 1) for _ in range(2)]
    neg = [carve(D) for _ in range(2)]
    phi = [carve(D) for _ in range(2)]
    st6 = carve(6)
    mom = [carve(2) for _ in range(2)]
    std = [carve(1) for _ in range(2)]
    rstd = carve(1)
    empty = carve(ROW)
    rows_i = carve(2, CHUNKS, P)
    rows_f = carve(2, CHUNKS, P)
    node_i = carve(NT)

    passed = sem("pa_passed")
    loaded, ident0, made = sem("prep_loaded"), sem("ident_zeroed"), sem("consts_made")
    rows_in, rows_cast, rowT_ps, rowT_sb = sem("rows_in"), sem("rows_cast"), sem("rowT_ps"), sem("rowT_sb")
    x_in = [sem(f"x_in{b}") for b in range(2)]
    stats, mom_ready, std_ready, rstd_ready, xn_ready = (sem(n) for n in (
        "pa_stats", "pa_mom", "pa_std", "pa_rstd", "xn_ready"))
    xnT_ps, xnT_sb, kv_ps, qs_ps, mix_ps, acc_done = (sem(n) for n in (
        "xnT_ps", "xnT_sb", "kv_ps", "qs_ps", "mixkv_ps", "state_added"))
    kv_sb, sum_sb, xs_sb, mk_sb, neg_sb, exp_sb, phi_sb = (sem(n) for n in (
        "kv_sb", "xs_part", "xs_sb", "mixk_sb", "neg_sb", "exp_sb", "phi_sb"))
    stored = [sem(f"pa_stored{b}") for b in range(2)]
    bias_made = sem("bias_made")
    extra_out, state_zero, state_done = sem("extra_out"), sem("state_zeroed"), sem("state_copied")
    T, KV, QS, MX, A0, A1 = psum[0], psum[1], psum[2], psum[3], psum[4], psum[5]
    src_v, dst_v = src.rearrange("(t e) -> t e", e=P), dst.rearrange("(t e) -> t e", e=P)
    full = TILES // P
    rest = TILES - full * P
    NROWS = 4 if rest else 2

    def drive(eng, step):
        for i in range(2):
            step(i, i % 2, i // 2)
        with eng.Fori(0, (NT - 3) // 2) as k:
            step(2 * k + 2, 0, k + 1)
            step(2 * k + 3, 1, k + 1)
        step(NT - 1, (NT - 1) % 2, (NT - 1) // 2)

    assert NT % 2 == 1

    with nc.Block() as block:
        @block.sync
        def _(eng):
            eng.dma_start(xt[0], x[0:P, :]).then_inc(x_in[0], 16)
            eng.dma_start(xt[1], x[P:2 * P, :]).then_inc(x_in[1], 16)
            for w in range(6):
                eng.dma_start(w6[:, w], weights[w].rearrange("(k p) n -> p k n", p=P)).then_inc(loaded, 16)
            for w in range(7):
                eng.dma_start(b6[:, w], over_partitions(biases[w])).then_inc(loaded, 16)
            for a, view in enumerate((src_v, dst_v)):
                eng.dma_start(rows_i[:, a, 0:full].bitcast(I32),
                              view[0:full * P].rearrange("(k p) e -> p k e", p=P)).then_inc(rows_in, 16)
                if rest:
                    eng.dma_start(rows_i[0:rest, a, full].bitcast(I32),
                                  view[full * P:TILES]).then_inc(rows_in, 16)
            eng.wait_ge(made, 6)
            eng.dma_start(rows_as_tiles(extra_d),
                          empty.rearrange("p (o c) -> p o c", o=1).to_broadcast([P, NT, ROW])).then_inc(extra_out, 16)

            def store(i, b, u):
                eng.wait_ge(xn_ready, i + 1)
                eng.dma_start(xn_d[bass.ds(i * P, P), :], xn[b]).then_inc(stored[b], 16)
                eng.wait_ge(kv_sb, i + 1)
                eng.dma_start(kv_d[bass.ds(i * P, P), :], kv[b]).then_inc(stored[b], 16)
                eng.wait_ge(xs_sb, i + 1)
                eng.dma_start(q_d[bass.ds(i * P, P), :], qs[b][:, 0:D]).then_inc(stored[b], 16)
                eng.dma_start(xs_d[bass.ds(i * P, P), :], qs[b][:, D:]).then_inc(stored[b], 16)

            def step(i, b, u):
                store(i, b, u)
                eng.dma_start(xt[b], x[bass.ds((i + 2) * P, P), :]).then_inc(x_in[b], 16)

            step(0, 0, 0)
            with eng.Fori(0, (NT - 3) // 2) as k:
                step(2 * k + 1, 1, k)
                step(2 * k + 2, 0, k + 1)
            for i in (NT - 2, NT - 1):
                store(i, i % 2, i // 2)
            for b in range(2):
                eng.wait_ge(stored[b], 64 * ((NT + 1 - b) // 2))
            eng.wait_ge(extra_out, 16)

        @block.gpsimd
        def _(eng):
            eng.memset(ident[:], 0.0).then_inc(ident0, 1)
            eng.memset(eps[:], LN_EPS).then_inc(made, 1)
            eng.memset(empty[:, 0:MSG], 0.0).then_inc(made, 1)
            eng.memset(empty[:, MSG:ROW], -BIG).then_inc(made, 1)
            for b in range(2):
                eng.memset(mv[b][:, :, P:P + 1], 1.0).then_inc(made, 1)
            eng.wait_ge(ident0, 1)
            eng.affine_select(out=ident[:], in_=ident[:], compare_op=ALU.not_equal, fill=1.0, base=0,
                              pattern=[[-1, P]], channel_multiplier=1).then_inc(made, 1)
            eng.iota(node_i.bitcast(I32), pattern=[[P, NT]], base=0, channel_multiplier=1).then_inc(ident0, 1)
            eng.wait_ge(ident0, 2)
            eng.tensor_copy(node_f[:], node_i.bitcast(I32)).then_inc(made, 1)

        @block.tensor
        def _(eng):
            eng.wait_ge(made, 6)
            for n in range(2 * CHUNKS):
                a, k = divmod(n, CHUNKS)
                rows = P if k < full else rest
                eng.wait_ge(rows_cast, a + 1)
                if n >= 2:
                    eng.wait_ge(rowT_sb, n - 1)
                eng.transpose(psum[6 + n % 2][:, 0:rows], rows_f[0:rows, a, k], ident[0:rows, 0:rows])\
                   .then_inc(rowT_ps, 1)
            eng.wait_ge(loaded, 13 * 16)

            def add_state(i, b, u, first, last):
                rows = LAST if last else P
                eng.wait_ge(phi_sb, i + 1)
                for c, bank in enumerate((A0, A1)):
                    mm = eng.matmul(bank[:, 0:P + 1], phi[b][0:rows, c * P:(c + 1) * P], mv[b][0:rows, c, :],
                                    start=first, stop=last, skip_group_check=True)
                mm.then_inc(acc_done, 1)

            def step(i, b, u):
                eng.wait_ge(xn_ready, i + 1)
                if not isinstance(i, int) or i >= 1:
                    eng.wait_ge(xnT_sb, i)
                for c in range(KD):
                    mm = eng.transpose(T[:, c * P:(c + 1) * P], xn[b][:, c * P:(c + 1) * P], ident[:])
                mm.then_inc(xnT_ps, 1)
                if not isinstance(i, int) or i >= 1:
                    eng.wait_ge(mk_sb, 2 * i)
                eng.wait_ge(xnT_sb, i + 1)
                for n, (bank, done) in enumerate(((KV, kv_ps), (QS, qs_ps), (MX, mix_ps))):
                    for c in range(KD):
                        mm = eng.matmul(bank[:].rearrange("p (w n) -> p w n", w=2), xnT[b][:, c],
                                        w6[:, 2 * n:2 * n + 2, c], start=c == 0, stop=c == KD - 1)
                    mm.then_inc(done, 1)

            step(0, 0, 0)
            step(1, 1, 0)
            add_state(0, 0, 0, True, False)
            with eng.Fori(0, (NT - 3) // 2) as k:
                step(2 * k + 2, 0, k + 1)
                add_state(2 * k + 1, 1, k, False, False)
                step(2 * k + 3, 1, k + 1)
                add_state(2 * k + 2, 0, k + 1, False, False)
            i = NT - 1
            step(i, i % 2, i // 2)
            add_state(i - 1, (i - 1) % 2, (i - 1) // 2, False, False)
            add_state(i, i % 2, i // 2, False, True)

        @block.scalar
        def _(eng):
            eng.wait_ge(made, 6)

            def deviation(i, b):
                eng.wait_ge(mom_ready, i + 1)
                eng.activation(std[b], mom[b][:, 1:2], ACT.Sqrt, bias=eps[:]).then_inc(std_ready, 1)

            def step(i, b, u):
                eng.wait_ge(xnT_ps, i + 1)
                if not isinstance(i, int) or i >= 2:
                    eng.wait_ge(mix_ps, i - 1)
                eng.activation(xnT[b].rearrange("p k n -> p (k n)"), T[:, 0:D], ACT.Copy).then_inc(xnT_sb, 1)
                if not isinstance(i, int) or i < NT - 1:
                    deviation(i + 1, 1 - b)
                eng.wait_ge(neg_sb, i + 1)
                eng.activation(neg[b], neg[b], ACT.Exp).then_inc(exp_sb, 1)

            deviation(0, 0)
            drive(eng, step)

        @block.vector
        def _(eng):
            eng.wait_ge(rows_in, 16 * NROWS)
            for a in range(2):
                eng.tensor_copy(rows_f[:, a, 0:full], rows_i[:, a, 0:full].bitcast(I32))
                last = eng.tensor_copy(rows_f[0:rest, a, full], rows_i[0:rest, a, full].bitcast(I32))
                last.then_inc(rows_cast, 1)
            for n in range(2 * CHUNKS):
                a, k = divmod(n, CHUNKS)
                rows = P if k < full else rest
                eng.wait_ge(rowT_ps, n + 1)
                if a:
                    eng.tensor_copy(dst_f[:, k * P:k * P + rows], psum[6 + n % 2][:, 0:rows])
                eng.tensor_copy((src_t, dst_t)[a][:, k * P:k * P + rows], psum[6 + n % 2][:, 0:rows])\
                   .then_inc(rowT_sb, 1)
            eng.wait_ge(loaded, 13 * 16)
            eng.wait_ge(made, 6)
            eng.tensor_tensor(b6[:, 3], b6[:, 3], b6[:, 6], ALU.add).then_inc(bias_made, 1)
            eng.wait_ge(bias_made, 1)

            def normalise(i, b, u):
                eng.wait_ge(x_in[b], 16 * (u + 1))
                eng.bn_stats(st6, xt[b]).then_inc(stats, 1)
                hold(eng, stats, i + 1, passed)
                eng.bn_aggr(mom[b], st6).then_inc(mom_ready, 1)
                eng.wait_ge(std_ready, i + 1)
                eng.reciprocal(rstd, std[b]).then_inc(rstd_ready, 1)
                eng.wait_ge(rstd_ready, i + 1)
                if not isinstance(i, int) or i >= 2:
                    eng.wait_ge(stored[b], 64 * u)
                eng.tensor_scalar(xn[b], xt[b], mom[b][:, 0:1], rstd, ALU.subtract, ALU.mult).then_inc(xn_ready, 1)

            def add_bias(i, b, u):
                eng.wait_ge(kv_ps, i + 1)
                eng.tensor_tensor(kv[b], KV[:], b6[:, 0:2].rearrange("p w n -> p (w n)"), ALU.add).then_inc(kv_sb, 1)
                eng.wait_ge(qs_ps, i + 1)
                eng.tensor_tensor(qs[b], QS[:], b6[:, 2:4].rearrange("p w n -> p (w n)"), ALU.add).then_inc(sum_sb, 1)
                eng.wait_ge(mix_ps, i + 1)
                if not isinstance(i, int) or i >= 2:
                    eng.wait_ge(acc_done, i - 1)
                eng.tensor_tensor(mk[b], MX[:, 0:D], b6[:, 4], ALU.add).then_inc(mk_sb, 1)
                eng.tensor_tensor(mv[b][:, :, 0:P], MX[:, D:].rearrange("p (k n) -> p k n", k=KD),
                                  b6[:, 5].rearrange("p (k n) -> p k n", k=KD), ALU.add).then_inc(mk_sb, 1)
                eng.wait_ge(sum_sb, i + 1)
                eng.tensor_tensor(qs[b][:, D:], qs[b][:, D:], xt[b], ALU.add).then_inc(xs_sb, 1)
                eng.wait_ge(mk_sb, 2 * i + 1)
                eng.tensor_scalar(neg[b], mk[b], 0.0, None, ALU.min).then_inc(neg_sb, 1)

            def feature(i, b, u):
                eng.wait_ge(exp_sb, i + 1)
                eng.scalar_tensor_tensor(phi[b], mk[b], 0.0, neg[b], ALU.max, ALU.add).then_inc(phi_sb, 1)

            normalise(0, 0, 0)
            pass_two(0, normalise, add_bias, feature)
            with eng.Fori(1, (NT - 1) // 2) as k:
                pass_two(k, normalise, add_bias, feature)
            i = NT - 1
            add_bias(i, i % 2, i // 2)
            feature(i, i % 2, i // 2)
            eng.memset(state[:], 0.0).then_inc(state_zero, 1)
            eng.wait_ge(state_zero, 1)
            eng.wait_ge(acc_done, NT)
            for c, bank in enumerate((A0, A1)):
                for h in range(H // KD):
                    rows = slice(h * C, (h + 1) * C)
                    eng.tensor_copy(state[rows, c, h * C:(h + 1) * C], bank[rows, h * C:(h + 1) * C])
                    last = eng.tensor_copy(state[rows, c, P + h:P + h + 1], bank[rows, P:P + 1])
            last.then_inc(state_done, 1)
            eng.wait_ge(state_done, 1)


def pass_two(k, normalise, add_bias, feature):
    normalise(2 * k + 1, 1, k)
    add_bias(2 * k, 0, k)
    feature(2 * k, 0, k)
    normalise(2 * k + 2, 0, k + 1)
    add_bias(2 * k + 1, 1, k)
    feature(2 * k + 1, 1, k)



def edges_and_mix(nc, sem, psum, ident, eps, src_t, dst_t, dst_f, state, carve, dst, edge_attr, We, mats, columns,
                  rows, kv_d, q_d, xn_d, xs_d, x1_d, part_d, slot_d):
    we = carve(KD, D)
    ea = [carve(G, D) for _ in range(2)]
    kv = [carve(G, 2 * D) for _ in range(2)]
    q = [carve(G, D) for _ in range(2)]
    dst_all = [carve(G, P) for _ in range(2)]
    dst_row = [carve(P) for _ in range(2)]
    eaT = [carve(2 * KD, P) for _ in range(2)]
    kj = [carve(2, D) for _ in range(2)]
    ve = [carve(G, D) for _ in range(2)]
    alpha = [carve(G * H) for _ in range(2)]
    src_c = [carve(G) for _ in range(2)]
    dst_c = [carve(G) for _ in range(2)]
    dst_cf = [carve(G) for _ in range(2)]
    same = [carve(G, P) for _ in range(2)]
    msg = [carve(G, MSG) for _ in range(2)]
    part = [carve(G, ROW) for _ in range(2)]
    keep = carve(P + 1)
    left, peak, diff, prob = carve(P), carve(P), carve(P), carve(P)
    wq, wo, w1, w2 = carve(KD, D), carve(KD, D), carve(KD, FF), carve(FC, D)
    bq, b1, g1c, h1c = carve(KD), carve(FC), carve(KD), carve(KD)
    bo, g1, hb, b2, g2 = (carve(D) for _ in range(5))
    mx_xn, mx_xs, mx_out = carve(D), carve(D), carve(D)
    xnT, qneg, qpos, attn, attnT = carve(KD, P), carve(KD, P), carve(KD, P), carve(D), carve(KD, P)
    den, y, xm, z, x1T, hid = carve(H), carve(D), carve(D), carve(D), carve(KD, P), carve(FC, P)
    m_st6, m_mom, m_std, m_rstd, m_off = carve(6), carve(2), carve(1), carve(1), carve(1)
    no_row = carve(XROW)
    SG = G * H
    T, E_ps, U, S, M = psum[0:2], psum[2:4], psum[4:6], psum[6], psum[7]

    passed = sem("b_passed")
    loaded, edge_made = sem("b_loaded"), sem("b_made")
    ea_in = [sem(f"ea_in{b}") for b in range(2)]
    all_in = [sem(f"dst_all_in{b}") for b in range(2)]
    row_in = [sem(f"dst_row_in{b}") for b in range(2)]
    gathered = [[sem(f"gathered{b}_{j}") for j in range(PAIRS)] for b in range(2)]
    index_ready, eaT_ps, eaT_sb, e_ps = sem("index_ready"), sem("eaT_ps"), sem("eaT_sb"), sem("e_ps")
    kj_ready, ve_ready, prod_ready, alpha_ready = sem("kj_ready"), sem("ve_ready"), sem("prod_ready"), sem("alpha_ready")
    same_row, keep_ready, alphaT_ps, left_ready = sem("same_row"), sem("keep_ready"), sem("alphaT_ps"), sem("left_ready")
    peak_ready, diff_ready, prob_ready, back_ps = sem("peak_ready"), sem("diff_ready"), sem("prob_ready"), sem("back_ps")
    dstc_ready, weights_sb, peaks_sb, same_ready = sem("dstc_ready"), sem("weights_sb"), sem("peaks_sb"), sem("same_ready")
    msg_ready, u_ps, u_sb = sem("msg_ready"), sem("u_ps"), sem("u_sb")
    part_out = [sem(f"part_out{b}") for b in range(2)]
    no_row_made, slots_out = sem("no_row_made"), sem("slots_emptied")
    mx_in, mx_xs_in, mx_stored = sem("mx_in"), sem("mx_xs_in"), sem("mx_stored")
    xnT_ps, q_ps, num_ps, attnT_ps, wo_ps, zT_ps, up0_ps, up1_ps, down_ps = (sem("mx_" + n) for n in (
        "xnT_ps", "q_ps", "num_ps", "attnT_ps", "wo_ps", "zT_ps", "up0_ps", "up1_ps", "down_ps"))
    xnT_sb, q_exp, attnT_sb, x1T_sb, relu0, relu1 = (sem("mx_" + n) for n in (
        "xnT_sb", "q_exp", "attnT_sb", "x1T_sb", "relu0", "relu1"))
    q_min, phi_q, den_eps, den_inv, attn_sb, xb_sb, gained, shifted, summed = (sem("mx_" + n) for n in (
        "q_min", "phi_q", "den_eps", "den_inv", "attn_sb", "xb_sb", "gained", "shifted", "final"))
    y_sb, y_stats, y_mom, y_std, y_rstd, y_off, z_sb = ([sem(f"mx_{n}{m}") for m in range(2)] for n in (
        "y_sb", "y_stats", "y_mom", "y_std", "y_rstd", "y_off", "z_sb"))
    scaled2 = sem("mx_scaled2")

    def seen(v, n=1):
        return not isinstance(v, int) or v >= n

    def exists(g):
        return not isinstance(g, int) or 0 <= g < NG

    def drive(eng, step):
        def two_steps(k):
            step(2 * k + 2, 0, k + 1, (k, 0))
            step(2 * k + 3, 1, k + 1, (k, 8))

        for g in range(2):
            step(g, g, 0, None)
        two_steps(0)
        two_steps(1)
        with eng.Fori(2, NT - 1) as k:
            two_steps(k)
        two_steps(NT - 1)
        for g in range(2 * NT + 2, NG + 2):
            step(g, g % 2, g // 2, (NT, 0) if g == 2 * NT + 2 else None)

    with nc.Block() as block:
        @block.sync
        def _(eng):
            eng.dma_start(we, We.rearrange("(k p) n -> p k n", p=P)).then_inc(loaded, 16)
            edge_rows = rows_as_tiles(edge_attr)
            dst_rows = dst.rearrange("(t e) -> t e", e=P)
            part_rows = rows_as_tiles(part_d)

            def load(g, b):
                if seen(g, 2):
                    hold(eng, eaT_ps, PAIRS * (g - 1), passed)
                eng.dma_start(ea[b], edge_rows[:, bass.ds(g * G, G), :]).then_inc(ea_in[b], 16)
                if seen(g, 2):
                    hold(eng, keep_ready, g - 1, passed)
                    hold(eng, same_ready, g - 1, passed)
                eng.dma_start(dst_row[b][0:SG].bitcast(I32),
                              dst_rows[bass.ds(g * G, G), :].rearrange("t (o e) -> t o e", o=1)
                              .to_broadcast([G, H, P])).then_inc(row_in[b], 16)
                eng.dma_start(dst_all[b].rearrange("p t e -> p (t e)").bitcast(I32),
                              dst[bass.ds(g * G * P, G * P)].rearrange("(o e) -> o e", o=1)
                              .to_broadcast([P, G * P])).then_inc(all_in[b], 16)

            def store(g, b):
                hold(eng, u_sb, G * (g + 1), passed)
                hold(eng, peaks_sb, g + 1, passed)
                eng.dma_start(part_rows[:, bass.ds(g * G, G), :], part[b]).then_inc(part_out[b], 16)

            def empty_slots(t):
                eng.dma_start(slot_d[bass.ds(t * P, P), :], no_row).then_inc(slots_out, 16)

            eng.wait_ge(no_row_made, 2)

            def step(g, b, u, mix):
                if exists(g):
                    load(g, b)
                if exists(g - 3):
                    store(g - 3, 1 - b)
                if exists(g):
                    empty_slots(g)
                if isinstance(g, int) and g == 0:
                    eng.dma_start(mx_xn, xn_d[0:P, :]).then_inc(mx_in, 16)
                    eng.dma_start(mx_xs, xs_d[0:P, :]).then_inc(mx_xs_in, 16)
                    for to, of in ((wq, mats[0]), (wo, mats[1]), (w1, mats[2]), (w2, mats[3])):
                        eng.dma_start(to, of.rearrange("(k p) n -> p k n", p=P)).then_inc(loaded, 16)
                    for to, of in ((bq, columns[0]), (b1, columns[1]), (g1c, rows[1]), (h1c, rows[2])):
                        with nc.allow_non_contiguous_dma("biases, once"):
                            eng.dma_start(to, per_channel(of)).then_inc(loaded, 16)
                    for to, of in zip((bo, g1, hb, b2, g2), rows):
                        eng.dma_start(to, over_partitions(of)).then_inc(loaded, 16)

            drive(eng, step)
            store(NG - 1, (NG - 1) % 2)
            for t in range(NG, SLOTS):
                empty_slots(t)
            eng.wait_ge(slots_out, 16 * SLOTS)
            for b in range(2):
                eng.wait_ge(part_out[b], 16 * (NG // 2))

        LOADS = 14 * 16
        assert NG <= SLOTS

        @block.gpsimd
        def _(eng):
            eng.memset(no_row[:, 0:D + NE], 0.0).then_inc(no_row_made, 1)
            eng.memset(no_row[:, D + NE:], 2.0 * NP).then_inc(no_row_made, 1)

            def step(g, b, u, mix):
                if not exists(g):
                    return
                if seen(g, 2):
                    eng.wait_ge(alpha_ready, PAIRS * (g - 1))
                eng.tensor_copy(src_c[b].bitcast(I32), src_t[:, bass.ds(g * G, G)]).then_inc(index_ready, 1)
                eng.tensor_copy(dst_c[b].bitcast(I32), dst_t[:, bass.ds(g * G, G)]).then_inc(index_ready, 1)
                hold(eng, index_ready, 2 * g + 2, passed)
                for t in range(G):
                    done = gathered[b][t // 2]
                    eng.indirect_dma_start(kv[b][:, t], None, kv_d, bass.IndirectOffsetOnAxis(
                        src_c[b][:, t:t + 1].bitcast(I32), 0), bounds_check=NP - 1, oob_is_err=False).then_inc(done, 16)
                    eng.indirect_dma_start(q[b][:, t], None, q_d, bass.IndirectOffsetOnAxis(
                        dst_c[b][:, t:t + 1].bitcast(I32), 0), bounds_check=NP - 1, oob_is_err=False).then_inc(done, 16)

            drive(eng, step)

        @block.tensor
        def _(eng):
            eng.wait_ge(loaded, 16)

            def mix_slot(mix, s):
                if mix is None:
                    return
                k, s = mix[0], mix[1] + s
                if isinstance(k, int) and k == NT:
                    return
                if s == 0:
                    eng.wait_ge(mx_in, 16 * (k + 1))
                    if seen(k):
                        eng.wait_ge(y_sb[1], k)
                    for c in range(KD):
                        mm = eng.transpose(M[:, c * P:(c + 1) * P], mx_xn[:, c * P:(c + 1) * P], ident[:])
                    mm.then_inc(xnT_ps, 1)
                elif s == 1:
                    eng.wait_ge(xnT_sb, k + 1)
                    for o in range(KD):
                        for c in range(KD):
                            mm = eng.matmul(M[:, o * P:(o + 1) * P], wq[:, c, o * P:(o + 1) * P], xnT[:, c],
                                            start=c == 0, stop=c == KD - 1)
                    mm.then_inc(q_ps, 1)
                elif s == 4:
                    eng.wait_ge(phi_q, k + 1)
                    for c in range(KD):
                        mm = eng.matmul(M[:, c * KVW:(c + 1) * KVW], qneg[:, c], state[:, c], start=True, stop=True)
                    mm.then_inc(num_ps, 1)
                elif s == 5:
                    eng.wait_ge(attn_sb, k + 1)
                    for c in range(KD):
                        mm = eng.transpose(M[:, c * P:(c + 1) * P], attn[:, c * P:(c + 1) * P], ident[:])
                    mm.then_inc(attnT_ps, 1)
                elif s == 6:
                    eng.wait_ge(attnT_sb, k + 1)
                    for c in range(KD):
                        mm = eng.matmul(M[:, 0:D], attnT[:, c], wo[:, c], start=c == 0, stop=c == KD - 1)
                    mm.then_inc(wo_ps, 1)
                elif s == 9:
                    eng.wait_ge(z_sb[0], k + 1)
                    for c in range(KD):
                        mm = eng.transpose(M[:, c * P:(c + 1) * P], z[:, c * P:(c + 1) * P], ident[:])
                    mm.then_inc(zT_ps, 1)
                elif s in (10, 11):
                    first = s == 10
                    eng.wait_ge(x1T_sb if first else relu0, k + 1)
                    for f in range(FC // 2):
                        ff = f if first else FC // 2 + f
                        for c in range(KD):
                            mm = eng.matmul(M[:, f * P:(f + 1) * P], w1[:, c, ff * P:(ff + 1) * P], x1T[:, c],
                                            start=c == 0, stop=c == KD - 1)
                    mm.then_inc(up0_ps if first else up1_ps, 1)
                elif s in (12, 13):
                    eng.wait_ge(relu1, k + 1)
                    half = FC // 2 * (s - 12)
                    for f in range(half, half + FC // 2):
                        mm = eng.matmul(M[:, 0:D], hid[:, f], w2[:, f], start=f == 0, stop=f == FC - 1)
                    if s == 13:
                        mm.then_inc(down_ps, 1)

            def transposes(g, b, u, j):
                n = PAIRS * g + j
                if j == 0:
                    eng.wait_ge(ea_in[b], 16 * (u + 1))
                if seen(n, 2):
                    eng.wait_ge(eaT_sb, n - 1)
                for t in range(2):
                    for c in range(KD):
                        mm = eng.transpose(T[j % 2][:, (t * KD + c) * P:(t * KD + c + 1) * P],
                                           ea[b][:, 2 * j + t, c * P:(c + 1) * P], ident[:])
                mm.then_inc(eaT_ps, 1)

            def project(g, j):
                n = PAIRS * g + j
                eng.wait_ge(eaT_sb, n + 1)
                if seen(n, 2):
                    eng.wait_ge(ve_ready, n - 1)
                for t in range(2):
                    for c in range(KD):
                        mm = eng.matmul(E_ps[j % 2][:, t * D:(t + 1) * D], eaT[j % 2][:, t * KD + c], we[:, c],
                                        start=c == 0, stop=c == KD - 1)
                mm.then_inc(e_ps, 1)

            def scores_to_rows(g, b):
                hold(eng, alpha_ready, PAIRS * (g + 1), passed)
                if seen(g):
                    hold(eng, peaks_sb, g, passed)
                eng.transpose(S[0:SG, 0:P], alpha[b], ident[:]).then_inc(alphaT_ps, 1)

            def rows_back(g):
                hold(eng, prob_ready, g + 1, passed)
                eng.transpose(S[:, P:P + SG], prob[0:SG], ident[0:SG, 0:SG])
                eng.transpose(S[:, P + SG:P + 2 * SG], peak[0:SG], ident[0:SG, 0:SG]).then_inc(back_ps, 1)

            def sum_nodes(g, b, j):
                if not exists(g):
                    return
                eng.wait_ge(msg_ready, PAIRS * g + j + 1)
                for t in (2 * j, 2 * j + 1):
                    n = G * g + t
                    if seen(n, 2):
                        eng.wait_ge(u_sb, n - 1)
                    eng.matmul(U[t % 2][:, 0:MSG], same[b][:, t], msg[b][:, t], start=True, stop=True)\
                       .then_inc(u_ps, 1)

            transposes(0, 0, 0, 0)
            transposes(0, 0, 0, 1)
            project(0, 0)

            def step(g, b, u, mix):
                for j in range(PAIRS):
                    if j < 2 and exists(g):
                        transposes(g, b, u, j + 2)
                    if j >= 2 and exists(g + 1):
                        transposes(g + 1, 1 - b, u + b, j - 2)
                    mix_slot(mix, 2 * j)
                    if j < 3 and exists(g):
                        project(g, j + 1)
                    if j == 3 and exists(g + 1):
                        project(g + 1, 0)
                    if j < 3:
                        sum_nodes(g - 2, b, j + 1)
                    else:
                        sum_nodes(g - 1, 1 - b, 0)
                    if j == 0 and exists(g - 1):
                        scores_to_rows(g - 1, 1 - b)
                    if j == 1 and exists(g - 1):
                        rows_back(g - 1)
                    mix_slot(mix, 2 * j + 1)
                if isinstance(g, int) and g == 1:
                    eng.wait_ge(loaded, LOADS)

            drive(eng, step)

        @block.scalar
        def _(eng):
            def mix_slot(mix, s):
                if mix is None:
                    return
                k, s = mix[0], mix[1] + s
                if s == 2 and seen(k):
                    eng.wait_ge(summed, k)
                    eng.dma_start(x1_d[bass.ds((k - 1) * P, P), :], mx_out).then_inc(mx_stored, 16)
                    if not isinstance(k, int) or k < NT:
                        eng.dma_start(mx_xs, xs_d[bass.ds(k * P, P), :]).then_inc(mx_xs_in, 16)
                if isinstance(k, int) and k == NT:
                    return
                if s == 0:
                    eng.wait_ge(xnT_ps, k + 1)
                    eng.activation(xnT.rearrange("p k n -> p (k n)"), M[:, 0:D], ACT.Copy).then_inc(xnT_sb, 1)
                elif s == 2:
                    eng.wait_ge(q_min, k + 1)
                    for c in range(KD):
                        eng.activation(qpos[:, c], M[:, c * P:(c + 1) * P], ACT.Relu, bias=bq[:, c:c + 1])
                    eng.activation(qneg.rearrange("p k n -> p (k n)"), qneg.rearrange("p k n -> p (k n)"), ACT.Exp)\
                       .then_inc(q_exp, 1)
                elif s == 5:
                    eng.wait_ge(attnT_ps, k + 1)
                    eng.activation(attnT.rearrange("p k n -> p (k n)"), M[:, 0:D], ACT.Copy).then_inc(attnT_sb, 1)
                elif s in (7, 14):
                    m = int(s == 14)
                    eng.wait_ge(y_mom[m], k + 1)
                    eng.activation(m_std, m_mom[:, 1:2], ACT.Sqrt, bias=eps[:]).then_inc(y_std[m], 1)
                    if m == 0 and (not isinstance(k, int) or k < NT - 1):
                        eng.dma_start(mx_xn, xn_d[bass.ds(k * P + P, P), :]).then_inc(mx_in, 16)
                elif s in (8, 15):
                    m = int(s == 15)
                    eng.wait_ge(y_off[m], k + 1)
                    eng.activation(z, y, ACT.Identity, bias=m_off, scale=m_rstd).then_inc(z_sb[m], 1)
                elif s == 9:
                    eng.wait_ge(zT_ps, k + 1)
                    for c in range(KD):
                        last = eng.activation(x1T[:, c], M[:, c * P:(c + 1) * P], ACT.Identity, bias=h1c[:, c:c + 1],
                                              scale=g1c[:, c:c + 1])
                    last.then_inc(x1T_sb, 1)
                elif s in (10, 11):
                    first = s == 10
                    eng.wait_ge(up0_ps if first else up1_ps, k + 1)
                    for f in range(FC // 2):
                        ff = f if first else FC // 2 + f
                        last = eng.activation(hid[:, ff], M[:, f * P:(f + 1) * P], ACT.Relu, bias=b1[:, ff:ff + 1])
                    last.then_inc(relu0 if first else relu1, 1)

            def move(g, j):
                n = PAIRS * g + j
                eng.wait_ge(eaT_ps, n + 1)
                if seen(n, 2):
                    eng.wait_ge(e_ps, n - 1)
                eng.activation(eaT[j % 2].rearrange("p k n -> p (k n)"), T[j % 2][:], ACT.Copy).then_inc(eaT_sb, 1)

            def exponentials(g):
                eng.wait_ge(diff_ready, g + 1)
                if seen(g):
                    eng.wait_ge(back_ps, g)
                eng.activation(prob[0:SG], diff[0:SG], ACT.Exp, scale=SCALE).then_inc(prob_ready, 1)

            def sums_out(g, b, u, j):
                if not exists(g):
                    return
                for t in (2 * j, 2 * j + 1):
                    eng.wait_ge(u_ps, G * g + t + 1)
                    if t == 0 and seen(g, 2):
                        eng.wait_ge(part_out[b], 16 * u)
                    eng.activation(part[b][:, t, 0:MSG], U[t % 2][:, 0:MSG], ACT.Copy).then_inc(u_sb, 1)

            move(0, 0)
            move(0, 1)

            def step(g, b, u, mix):
                for j in range(PAIRS):
                    if j < 2 and exists(g):
                        move(g, j + 2)
                    if j >= 2 and exists(g + 1):
                        move(g + 1, j - 2)
                    if j == 1 and exists(g - 1):
                        exponentials(g - 1)
                    mix_slot(mix, 2 * j)
                    if j < 3:
                        sums_out(g - 2, b, u - 1, j + 1)
                    else:
                        sums_out(g - 1, 1 - b, u - 1 + b, 0)
                    mix_slot(mix, 2 * j + 1)
                if isinstance(g, int) and g == 1:
                    eng.wait_ge(loaded, LOADS)

            drive(eng, step)
            eng.wait_ge(mx_stored, 16 * NT)

        @block.vector
        def _(eng):
            eng.memset(keep[:], -BIG).then_inc(edge_made, 1)
            eng.wait_ge(edge_made, 1)

            def mix_slot(mix, s):
                if mix is None:
                    return
                k, s = mix[0], mix[1] + s
                if s == 0 and seen(k):
                    eng.wait_ge(z_sb[1], k)
                    if seen(k, 2):
                        eng.wait_ge(mx_stored, 16 * (k - 1))
                    eng.tensor_tensor(mx_out, z, g2, ALU.mult).then_inc(scaled2, 1)
                elif s == 1 and seen(k):
                    eng.wait_ge(scaled2, k)
                    eng.wait_ge(mx_xs_in, 16 * k)
                    eng.tensor_tensor(mx_out, mx_out, mx_xs, ALU.add).then_inc(summed, 1)
                if isinstance(k, int) and k == NT:
                    return
                if s == 2:
                    eng.wait_ge(q_ps, k + 1)
                    for c in range(KD):
                        last = eng.tensor_scalar(qneg[:, c], M[:, c * P:(c + 1) * P], bq[:, c:c + 1], 0.0,
                                                 ALU.add, ALU.min)
                    last.then_inc(q_min, 1)
                elif s == 3:
                    eng.wait_ge(q_exp, k + 1)
                    eng.tensor_tensor(qneg, qneg, qpos, ALU.add).then_inc(phi_q, 1)
                elif s == 4:
                    eng.wait_ge(num_ps, k + 1)
                    sums = M[:, 0:KD * KVW].rearrange("p (c w) -> p c w", c=KD)
                    hk = H // KD
                    eng.tensor_scalar(den.rearrange("p (c h) -> p c h", c=KD), sums[:, :, P:KVW], 1e-6, None,
                                      ALU.add).then_inc(den_eps, 1)
                    eng.wait_ge(den_eps, k + 1)
                    eng.reciprocal(den, den).then_inc(den_inv, 1)
                    eng.wait_ge(den_inv, k + 1)
                    for c in range(KD):
                        last = eng.tensor_tensor(
                            attn[:, c * P:(c + 1) * P].rearrange("p (h c) -> p h c", h=hk),
                            M[:, c * KVW:c * KVW + P].rearrange("p (h c) -> p h c", h=hk),
                            den[:, c * hk:(c + 1) * hk].rearrange("p (h o) -> p h o", o=1).to_broadcast([P, hk, C]),
                            ALU.mult)
                    last.then_inc(attn_sb, 1)
                elif s == 5:
                    eng.tensor_tensor(xm, mx_xn, bo, ALU.add).then_inc(xb_sb, 1)
                elif s in (6, 14):
                    m = int(s == 14)
                    eng.wait_ge((wo_ps, down_ps)[m], k + 1)
                    eng.tensor_tensor(y, M[:, 0:D], xm, ALU.add).then_inc(y_sb[m], 1)
                    eng.wait_ge(y_sb[m], k + 1)
                    eng.bn_stats(m_st6, y).then_inc(y_stats[m], 1)
                    hold(eng, y_stats[m], k + 1, passed)
                    eng.bn_aggr(m_mom, m_st6).then_inc(y_mom[m], 1)
                elif s in (7, 15):
                    m = int(s == 15)
                    eng.wait_ge(y_std[m], k + 1)
                    eng.reciprocal(m_rstd, m_std).then_inc(y_rstd[m], 1)
                    eng.wait_ge(y_rstd[m], k + 1)
                    eng.tensor_scalar(m_off, m_mom[:, 0:1], m_rstd, -1.0, ALU.mult, ALU.mult).then_inc(y_off[m], 1)
                elif s == 9:
                    eng.wait_ge(z_sb[0], k + 1)
                    eng.tensor_tensor(xm, z, g1, ALU.mult).then_inc(gained, 1)
                elif s == 10:
                    eng.wait_ge(gained, k + 1)
                    eng.tensor_tensor(xm, xm, hb, ALU.add).then_inc(shifted, 1)

            def keys_and_values(g, b, u, j):
                n = PAIRS * g + j
                e2 = E_ps[j % 2][:].rearrange("p (t c) -> p t c", t=2)
                eng.wait_ge(gathered[b][j], 64 * (u + 1))
                eng.wait_ge(e_ps, n + 1)
                eng.tensor_tensor(kj[j % 2], kv[b][:, 2 * j:2 * j + 2, 0:D], e2, ALU.add).then_inc(kj_ready, 1)
                eng.tensor_tensor(ve[b][:, 2 * j:2 * j + 2], kv[b][:, 2 * j:2 * j + 2, D:], e2, ALU.add)\
                   .then_inc(ve_ready, 1)
                eng.wait_ge(kj_ready, n + 1)
                eng.tensor_tensor(kj[j % 2], kj[j % 2], q[b][:, 2 * j:2 * j + 2], ALU.mult).then_inc(prod_ready, 1)

            def score(g, b, j):
                eng.wait_ge(prod_ready, PAIRS * g + j + 1)
                eng.tensor_reduce(alpha[b][:, 2 * j * H:2 * (j + 1) * H],
                                  kj[j % 2].rearrange("p t (h c) -> p (t h) c", h=H), AX, ALU.add)\
                   .then_inc(alpha_ready, 1)

            def neighbours(g, b, u):
                eng.wait_ge(row_in[b], 16 * (u + 1))
                row = dst_row[b][0:SG].bitcast(I32)
                eng.tensor_tensor(keep[0:SG, 1:P], row[:, 1:P], row[:, 0:P - 1], ALU.is_equal).then_inc(same_row, 1)
                eng.tensor_copy(dst_cf[b], dst_f[:, bass.ds(g * G, G)]).then_inc(dstc_ready, 1)
                eng.wait_ge(same_row, g + 1)
                eng.tensor_scalar(keep[0:SG, 1:P], keep[0:SG, 1:P], 1.0, BIG, ALU.subtract, ALU.mult)\
                   .then_inc(keep_ready, 1)

            def same_nodes(g, b, u):
                eng.wait_ge(dstc_ready, g + 1)
                eng.wait_ge(all_in[b], 16 * (u + 1))
                if seen(g, 2):
                    eng.wait_ge(u_ps, G * (g - 1))
                eng.tensor_tensor(same[b], dst_all[b].bitcast(I32),
                                  dst_cf[b].rearrange("p (t o) -> p t o", o=1).to_broadcast([P, G, P]),
                                  ALU.is_equal).then_inc(same_ready, 1)

            def maxima(g):
                eng.wait_ge(keep_ready, g + 1)
                eng.wait_ge(alphaT_ps, g + 1)
                if seen(g):
                    eng.wait_ge(back_ps, g)
                eng.tensor_tensor_scan(left[0:SG], keep[0:SG, 0:P], S[0:SG, 0:P], -BIG, ALU.add, ALU.max)\
                   .then_inc(left_ready, 1)
                eng.wait_ge(left_ready, g + 1)
                eng.tensor_tensor_scan(peak[0:SG, ::-1], keep[0:SG, 1:P + 1][:, ::-1], left[0:SG, ::-1], -BIG,
                                       ALU.add, ALU.max).then_inc(peak_ready, 1)
                eng.wait_ge(peak_ready, g + 1)
                if seen(g):
                    eng.wait_ge(prob_ready, g)
                eng.tensor_tensor(diff[0:SG], S[0:SG, 0:P], peak[0:SG], ALU.subtract).then_inc(diff_ready, 1)

            def weights_in(g, b, u):
                eng.wait_ge(back_ps, g + 1)
                eng.tensor_copy(msg[b][:, :, D:MSG], S[:, P:P + SG].rearrange("p (t h) -> p t h", t=G))\
                   .then_inc(weights_sb, 1)
                if seen(g, 2):
                    eng.wait_ge(part_out[b], 16 * u)
                eng.tensor_copy(part[b][:, :, MSG + H], dst_cf[b])
                eng.tensor_copy(part[b][:, :, MSG:MSG + H], S[:, P + SG:P + 2 * SG].rearrange("p (t h) -> p t h", t=G))\
                   .then_inc(peaks_sb, 1)
                eng.wait_ge(weights_sb, g + 1)

            def messages(g, b, j):
                if not exists(g):
                    return
                t = slice(2 * j, 2 * j + 2)
                eng.tensor_tensor(msg[b][:, t, 0:D].rearrange("p t (h c) -> p t h c", h=H),
                                  ve[b][:, t].rearrange("p t (h c) -> p t h c", h=H),
                                  per_head(msg[b][:, t, D:MSG], 2), ALU.mult).then_inc(msg_ready, 1)

            def step(g, b, u, mix):
                h, c, w = g - 1, 1 - b, u - 1 + b
                for j in range(PAIRS):
                    if exists(g):
                        keys_and_values(g, b, u, j)
                    if j == 0 and exists(h):
                        neighbours(h, c, w)
                    mix_slot(mix, 2 * j)
                    if j == 2 and exists(h):
                        weights_in(h, c, w)
                    if j < 2:
                        messages(g - 2, b, j + 2)
                    else:
                        messages(h, c, j - 2)
                    if exists(g):
                        score(g, b, j)
                    if j == 0 and exists(h):
                        maxima(h)
                    if j == 1 and exists(h):
                        same_nodes(h, c, w)
                    mix_slot(mix, 2 * j + 1)
                if isinstance(g, int) and g == 1:
                    eng.wait_ge(loaded, LOADS)
                    eng.tensor_tensor(hb, hb, b2, ALU.add).then_inc(edge_made, 1)
                    eng.wait_ge(edge_made, 2)

            drive(eng, step)


def merge(nc, sem, psum, ident, dst_f, node_f, last_i, carve, dst, part_d, extra_d):
    MR = 104
    MC = TILES // MR
    assert MR * MC == TILES
    FAR = 100000.0
    pick, ends, hits = carve(P), carve(TILES), carve(TILES)
    tile_f, tile_i, cnt = carve(NT), carve(NT), carve(NT)
    lots = [carve(P) for _ in range(2)]
    at = [carve(1) for _ in range(2)]
    row, ext, res = carve(ROW), carve(ROW), carve(ROW)
    nxt, prev, own1 = carve(1), carve(1), carve(1)
    own1_i = carve(1)
    over, first, key, to_f, to_i, from_i = (carve(1) for _ in range(6))
    keys, keysT, same = carve(MR), carve(MR), carve(MR)
    keep, left, peak = carve(MR + 1), carve(MR), carve(MR)
    d, w = carve(2 * H), carve(2 * H)
    ends_ps, K, S, Sum = psum[0:2], psum[2], psum[3], psum[4]

    passed = sem("mg_passed")
    made, pick0 = sem("mg_made"), sem("pick0")
    ends_done, chain = sem("ends_ps"), sem("mg_dve")
    tiles_found, at_ready = sem("tiles_found"), sem("at_ready")
    lots_in = [sem(f"lots_in{b}") for b in range(2)]
    counted, found = sem("counted"), sem("last_found")
    mg_in, index_made, keys_made, ext_in = sem("mg_in"), sem("mg_index"), sem("mg_keys"), sem("ext_in")
    keyT_ps, peakT, weights, scaled, sum_ps, res_ready, res_out = (sem(n) for n in (
        "keyT_ps", "peakT", "mg_weights", "mg_scaled", "mg_sum_ps", "res_ready", "res_out"))
    peaks_made, diffs = sem("mg_peaks"), sem("mg_diffs")
    dst_rows = dst.rearrange("(t e) -> t e", e=P)
    parts = part_d.rearrange("(t e) w -> t e w", e=P)

    def chunk_rows(eng, c):
        STEPS = 12
        n = [0]

        def link(ins):
            n[0] += 1
            ins.then_inc(chain, 1)
            eng.wait_ge(chain, NT + 2 + STEPS * c + n[0])

        r = slice(0, MR)
        node = row[r, MSG + H:ROW]
        eng.wait_ge(mg_in, 48 * (c + 1))
        link(eng.tensor_tensor(over[r], node, nxt[r].bitcast(I32), ALU.is_equal))
        link(eng.tensor_tensor(first[r], node, prev[r].bitcast(I32), ALU.not_equal))
        link(eng.scalar_tensor_tensor(key[r], node, own1[r], over[r], ALU.add, ALU.mult))
        link(eng.tensor_tensor(key[r], key[r], own1[r], ALU.subtract))
        eng.tensor_copy(keys[r], key[r].to_broadcast([MR, MR])).then_inc(keys_made, 1)
        link(eng.tensor_tensor(first[r], first[r], over[r], ALU.mult))
        link(eng.scalar_tensor_tensor(to_f[r], node, FAR, first[r], ALU.subtract, ALU.mult))
        if later(c):
            eng.wait_ge(res_out, 16 * c)
        eng.tensor_scalar(to_i[r].bitcast(I32), to_f[r], FAR, None, ALU.add).then_inc(index_made, 1)
        eng.tensor_copy(from_i[r].bitcast(I32), node).then_inc(index_made, 1)
        eng.wait_ge(keyT_ps, c + 1)
        link(eng.tensor_copy(keysT[r], K[r, 0:MR]))
        eng.tensor_scalar(same[r], keysT[r], key[r], None, ALU.is_equal).then_inc(scaled, 1)
        link(eng.tensor_tensor(keep[0:H, 1:MR], keysT[0:H, 1:MR], keysT[0:H, 0:MR - 1], ALU.is_equal))
        link(eng.tensor_scalar(keep[0:H, 1:MR], keep[0:H, 1:MR], 1.0, BIG, ALU.subtract, ALU.mult))
        link(eng.tensor_tensor_scan(left[0:H], keep[0:H, 0:MR], S[0:H, 0:MR], -BIG, ALU.add, ALU.max))
        eng.tensor_tensor_scan(peak[0:H, ::-1], keep[0:H, 1:MR + 1][:, ::-1], left[0:H, ::-1], -BIG,
                               ALU.add, ALU.max).then_inc(peaks_made, 1)
        eng.wait_ge(peakT, c + 1)
        eng.wait_ge(ext_in, 16 * (c + 1))
        link(eng.tensor_tensor(res[r, MSG:MSG + H], S[r, P:P + H], ext[r, MSG:MSG + H], ALU.max))
        eng.tensor_tensor(d[r, 0:H], row[r, MSG:MSG + H], res[r, MSG:MSG + H], ALU.subtract).then_inc(diffs, 1)
        eng.tensor_tensor(d[r, H:], ext[r, MSG:MSG + H], res[r, MSG:MSG + H], ALU.subtract).then_inc(diffs, 1)
        eng.wait_ge(weights, c + 1)

        def weigh(rows, ws):
            eng.tensor_tensor(heads(rows[r, 0:D]), heads(rows[r, 0:D]),
                              ws.rearrange("p (h o) -> p h o", o=1).to_broadcast([MR, H, C]), ALU.mult)
            return eng.tensor_tensor(rows[r, D:MSG], rows[r, D:MSG], ws, ALU.mult)

        weigh(row, w[r, 0:H]).then_inc(scaled, 1)
        link(weigh(ext, w[r, H:]))
        eng.tensor_copy(res[r, MSG + H:ROW], node)
        eng.wait_ge(sum_ps, c + 1)
        eng.tensor_tensor(res[r, 0:MSG], ext[r, 0:MSG], Sum[r, 0:MSG], ALU.add).then_inc(res_ready, 1)
        assert n[0] == STEPS, n

    def later(c):
        return not isinstance(c, int) or c >= 1

    def drive(eng, chunk):
        chunk(0)
        with eng.Fori(1, MC) as c:
            chunk(c)

    with nc.Block() as block:
        @block.sync
        def _(eng):
            eng.wait_ge(made, 4)

            def chunk(c):
                if later(c):
                    eng.wait_ge(res_ready, c)
                with nc.allow_non_contiguous_dma("one number of a tile"):
                    eng.dma_start(row[0:MR], parts[bass.ds(c * MR, MR), P - 1, :]).then_inc(mg_in, 16)
                    eng.dma_start(nxt[0:MR].bitcast(I32), dst_rows[bass.ds(c * MR + 1, MR), 0:1]).then_inc(mg_in, 16)
                    eng.dma_start(prev[1:MR].bitcast(I32), dst_rows[bass.ds(c * MR, MR - 1), P - 1:P])\
                       .then_inc(mg_in, 16)

            drive(eng, chunk)

        @block.gpsimd
        def _(eng):
            eng.memset(pick, 0.0).then_inc(pick0, 1)
            eng.memset(prev.bitcast(I32), -1).then_inc(made, 1)
            eng.memset(keep, -BIG).then_inc(made, 1)
            eng.iota(own1_i.bitcast(I32), pattern=[[0, 1]], base=1, channel_multiplier=1).then_inc(pick0, 1)
            eng.wait_ge(pick0, 2)
            eng.affine_select(out=pick, in_=pick, compare_op=ALU.not_equal, fill=1.0, base=-(P - 1),
                              pattern=[[0, P]], channel_multiplier=1).then_inc(made, 1)
            eng.tensor_copy(own1, own1_i.bitcast(I32)).then_inc(made, 1)

            eng.wait_ge(tiles_found, 1)

            def look_up(i, b, u):
                if not isinstance(i, int) or i >= 2:
                    eng.wait_ge(counted, i - 1)
                eng.tensor_copy(at[b].bitcast(I32), tile_i[:, bass.ds(i, 1)].bitcast(I32)).then_inc(at_ready, 1)
                hold(eng, at_ready, i + 1, passed)
                eng.indirect_dma_start(lots[b].bitcast(I32), None, dst_rows, bass.IndirectOffsetOnAxis(
                    at[b].bitcast(I32), 0), bounds_check=TILES - 1, oob_is_err=False).then_inc(lots_in[b], 16)

            for i in range(3):
                look_up(i, i % 2, i // 2)
            with eng.Fori(1, (NT - 1) // 2) as k:
                look_up(2 * k + 1, 1, k)
                look_up(2 * k + 2, 0, k + 1)

            def chunk(c):
                eng.wait_ge(index_made, 2 * c + 2)
                if later(c):
                    hold(eng, res_out, 16 * c, passed)
                eng.indirect_dma_start(ext[0:MR], None, extra_d, bass.IndirectOffsetOnAxis(
                    from_i[0:MR].bitcast(I32), 0), bounds_check=NP - 1, oob_is_err=False).then_inc(ext_in, 16)
                hold(eng, res_ready, c + 1, passed)
                eng.indirect_dma_start(extra_d, bass.IndirectOffsetOnAxis(to_i[0:MR].bitcast(I32), 0),
                                       res[0:MR], None, bounds_check=NP - 1, oob_is_err=False).then_inc(res_out, 16)

            drive(eng, chunk)
            eng.wait_ge(res_out, 16 * MC)

        @block.tensor
        def _(eng):
            eng.wait_ge(made, 4)
            half = TILES // 2
            for n in range(2):
                mm = eng.matmul(ends_ps[n][:, 0:half], pick, dst_f[:, n * half:(n + 1) * half], start=True, stop=True)
            mm.then_inc(ends_done, 1)
            with eng.Fori(0, MC) as c:
                hold(eng, keys_made, c + 1, passed)
                eng.transpose(K[0:MR, 0:MR], keys[0:MR], ident[0:MR, 0:MR])
                eng.transpose(S[0:H, 0:MR], row[0:MR, MSG:MSG + H], ident[0:MR, 0:MR]).then_inc(keyT_ps, 1)
                hold(eng, peaks_made, c + 1, passed)
                eng.transpose(S[0:MR, P:P + H], peak[0:H], ident[0:H, 0:H]).then_inc(peakT, 1)
                hold(eng, scaled, 2 * c + 2, passed)
                eng.matmul(Sum[0:MR, 0:MSG], same[0:MR], row[0:MR, 0:MSG], start=True, stop=True).then_inc(sum_ps, 1)

        @block.scalar
        def _(eng):
            with eng.Fori(0, MC) as c:
                eng.wait_ge(diffs, 2 * c + 2)
                eng.activation(w[0:MR], d[0:MR], ACT.Exp, scale=SCALE).then_inc(weights, 1)

        @block.vector
        def _(eng):
            eng.wait_ge(made, 4)
            eng.wait_ge(ends_done, 1)
            half = TILES // 2
            for n in range(2):
                last = eng.tensor_copy(ends[:, n * half:(n + 1) * half], ends_ps[n][:, 0:half])
            last.then_inc(chain, 1)
            eng.wait_ge(chain, 1)
            with eng.Fori(0, NT) as i:
                eng.tensor_scalar(hits, ends, node_f[:, bass.ds(i, 1)], 0.0, ALU.is_le, ALU.add,
                                  accum_out=tile_f[:, bass.ds(i, 1)]).then_inc(chain, 1)
                eng.wait_ge(chain, i + 2)
            eng.tensor_scalar(tile_f, tile_f, float(TILES - 1), None, ALU.min).then_inc(chain, 1)
            eng.wait_ge(chain, NT + 2)
            eng.tensor_copy(tile_i.bitcast(I32), tile_f).then_inc(tiles_found, 1)

            def count(i, b, u):
                eng.wait_ge(lots_in[b], 16 * (u + 1))
                eng.tensor_scalar(hits[:, 0:P], lots[b].bitcast(I32), node_f[:, bass.ds(i, 1)], 0.0, ALU.is_le,
                                  ALU.add, accum_out=cnt[:, bass.ds(i, 1)]).then_inc(counted, 1)
                eng.wait_ge(counted, i + 1)

            count(0, 0, 0)
            with eng.Fori(0, (NT - 1) // 2) as k:
                count(2 * k + 1, 1, k)
                count(2 * k + 2, 0, k + 1)
            eng.scalar_tensor_tensor(tile_f, tile_f, float(P), cnt, ALU.mult, ALU.add).then_inc(found, 1)
            eng.wait_ge(found, 1)
            eng.tensor_scalar(last_i[:], tile_f, -1.0, 0.0, ALU.add, ALU.max).then_inc(found, 1)

            drive(eng, lambda c: chunk_rows(eng, c))


def experts(nc, sem, psum, ident, eps, node_f, last_i, carve, part_d, extra_d, x1_d, gate_w, gate_b, W1, b1, W2,
            b2, slot_d, y_d, out):
    w1 = carve(NE * KD, HD)
    w2 = carve(NE * HC, D)
    b1r, b2r = carve(NE, HD), carve(NE, D)
    acc = carve(NT, D)
    gw, gb = carve(KD, NE), carve(NE)
    expert_i = carve(SLOTS)
    rows_at = carve.at
    xs = carve(NT, XROW)
    end = carve.at
    early = Carve(carve.arena, end)
    has, off, peak = early(MACRO), early(MACRO), early(MACRO, H)
    d, w = early(MACRO, 2 * H), early(MACRO, 2 * H)
    st6, mom = early(MACRO, 6), early(MACRO, 2)
    at = [early(MACRO) for _ in range(2)]
    moments, std, rstd = early(NT, 2), early(NT), early(NT)
    xf = [early(D) for _ in range(2)]
    xfT = [early(KD, P) for _ in range(2)]
    lead, lead_i = early(NE), early(NE)
    cw, prob, hit, rank, one, two = (early(NT, NE) for _ in range(6))
    top, zeros = early(NT), early(NT)
    ones, before = early(P), early(P)
    incl, more = early(NE, NT), early(NE, NT)
    step_i, step_f, slot_i, slot_f = early(NT), early(NT), early(SLOTS), early(SLOTS)
    tiles, ends, starts, passed_e, expert_f = early(NE), early(NE), early(NE), early(SLOTS, NE), early(SLOTS)
    assert early.at <= NE * KD * HD
    early.at = NE * KD * HD
    row = [early(MACRO, ROW) for _ in range(2)]
    ext = [early(MACRO, ROW) for _ in range(2)]
    x1 = [early(MACRO, D) for _ in range(2)]
    assert early.at <= rows_at - NT * D
    w2_at = NE * KD * HD
    sends = Carve(carve.arena, w2_at + NE * HC * D)
    sends.at = w2_at
    to_i = sends(NT, 2)
    send = [sends(XROW) for _ in range(4)]
    send_at = [sends(2) for _ in range(4)]
    results = Carve(carve.arena, w2_at)
    yy = [results(MACRO, 2 * D) for _ in range(2)]
    work = Carve(carve.arena, end)
    work.at = rows_at
    slot = [work(XROW) for _ in range(4)]
    xT = [work(KD, P) for _ in range(2)]
    hs = [work(HD) for _ in range(2)]
    act = [work(HD) for _ in range(2)]
    hT = [work(HC, P) for _ in range(2)]
    ys = [work(D) for _ in range(4)]
    y_at = [work(1) for _ in range(4)]

    passed = sem("ex_passed")
    made, lead0, loaded, gates_in = sem("ex_made"), sem("lead0"), sem("ex_loaded"), sem("gates_in")
    at_ready = sem("ex_at")
    row_in = [sem(f"main_in{b}") for b in range(2)]
    ext_in = [sem(f"extra_in{b}") for b in range(2)]
    chain, diffs, weights, mom_ready, std_ready = (sem(n) for n in (
        "ex_dve", "ex_diffs", "ex_weights", "ex_mom", "ex_std"))
    summed, rstd_ready, xf_kept, sel_ready, counts_ps = sem("ex_summed"), sem("ex_rstd"), sem("xf_kept"), sem("selected"), sem("counts_ps")
    xf_ready, xfT_ps, xfT_sb, gate_ps, logits = (sem(n) for n in ("xf_ready", "xfT_ps", "xfT_sb", "gate_ps", "logits"))
    shifted, exps, routed = sem("gates_shifted"), sem("gates_exp"), sem("routed")
    staged = sem("row_staged")
    sent = [sem(f"row_sent{b}") for b in range(4)]
    slot_in = [sem(f"slot_in{b}") for b in range(4)]
    y_out = [sem(f"y_out{b}") for b in range(4)]
    xT_ps, xT_sb, h_ps, h_sum, act_ready, hT_ps, hT_sb, y_ps, y_sum, y_ready, y_at_ready = (sem("sl_" + n) for n in (
        "xT_ps", "xT_sb", "h_ps", "h_sum", "act", "hT_ps", "hT_sb", "y_ps", "y_sum", "y_ready", "y_at"))
    yy_in = [sem(f"yy_in{b}") for b in range(2)]
    first_added, added = sem("first_added"), sem("added")
    out_done = sem("out_done")
    T, L = psum[0:2], psum[2:4]
    XT, HP, HT, YP = psum[0:2], psum[2:4], psum[4:6], psum[6:8]
    TURNS = SLOTS + 2

    def drive(eng, step, count):
        for i in range(3):
            step(i, i % 2, i // 2)
        with eng.Fori(1, (count - 1) // 2) as k:
            step(2 * k + 1, 1, k)
            step(2 * k + 2, 0, k + 1)

    def drive_slots(eng, turn, count=TURNS, peeled=1):
        for s in range(4 * peeled):
            turn(s, s % 4, s // 4)
        with eng.Fori(peeled, count // 4) as k:
            for j in range(4):
                turn(4 * k + j, j, k)
        for s in range(4 * (count // 4), count):
            turn(s, s % 4, s // 4)

    def seen(v, n=1):
        return not isinstance(v, int) or v >= n

    def is_tile(i):
        return not isinstance(i, int) or i < NT

    def is_slot(s):
        return not isinstance(s, int) or 0 <= s < SLOTS

    def expert_of(eng, s):
        return eng.value_load(expert_i[0:1, bass.ds(s, 1)].bitcast(I32), min_val=0, max_val=NE - 1)

    with nc.Block() as block:
        @block.sync
        def _(eng):
            eng.dma_start(gw, gate_w.rearrange("(k p) n -> p k n", p=P)).then_inc(gates_in, 16)
            eng.dma_start(gb, over_partitions(gate_b)).then_inc(gates_in, 16)

            def step(m, b, u):
                if seen(m, 2):
                    eng.wait_ge(summed, m - 1)
                eng.dma_start(ext[b], rows_as_tiles(extra_d)[:, bass.ds(m * MACRO, MACRO), :]).then_inc(ext_in[b], 16)
                eng.dma_start(x1[b], rows_as_tiles(x1_d)[:, bass.ds(m * MACRO, MACRO), :]).then_inc(ext_in[b], 16)

            drive(eng, step, MACROS)
            eng.wait_ge(routed, 1)
            eng.dma_start(w1, W1.rearrange("e (k p) n -> p (e k) n", p=P)).then_inc(loaded, 16)
            eng.dma_start(b1r.rearrange("p e n -> p (e n)"), over_partitions(b1.rearrange("e n -> (e n)")))\
               .then_inc(loaded, 16)
            eng.dma_start(b2r.rearrange("p e n -> p (e n)"), over_partitions(b2.rearrange("e n -> (e n)")))\
               .then_inc(loaded, 16)
            for b in range(4):
                eng.wait_ge(sent[b], 32 * ((NT + 3 - b) // 4))
            eng.dma_start(w2, W2.rearrange("e (k p) n -> p (e k) n", p=P)).then_inc(loaded, 16)
            slots = rows_as_tiles(slot_d)

            def turn(s, b, u):
                if seen(s, 4):
                    hold(eng, y_ready, s - 3, passed)
                    hold(eng, y_at_ready, s - 3, passed)
                eng.dma_start(slot[b], slot_d[bass.ds(s * P, P), :]).then_inc(slot_in[b], 16)

            drive_slots(eng, turn, SLOTS)
            for b in range(4):
                eng.wait_ge(y_out[b], 16 * ((SLOTS + 3 - b) // 4))
            pairs = y_d[0:2 * NP, :].rearrange("(t p w) c -> p t (w c)", p=P, w=2)
            rows = out[0:(NT - 1) * P, :].rearrange("(t p) c -> p t c", p=P)
            for m in range(MACROS):
                if m >= 2:
                    eng.wait_ge(added, m - 1)
                eng.dma_start(yy[m % 2], pairs[:, m * MACRO:(m + 1) * MACRO, :]).then_inc(yy_in[m % 2], 16)
                if m:
                    eng.wait_ge(added, m)
                    eng.dma_start(rows[:, (m - 1) * MACRO:m * MACRO, :], acc[:, (m - 1) * MACRO:m * MACRO, :])\
                       .then_inc(out_done, 16)
            eng.wait_ge(added, MACROS)
            first = NT - MACRO
            eng.dma_start(rows[:, first:NT - 1, :], acc[:, first:NT - 1, :]).then_inc(out_done, 16)
            eng.dma_start(out[(NT - 1) * P:N, :], acc[0:LAST, NT - 1, :]).then_inc(out_done, 16)
            eng.wait_ge(out_done, 16 * (MACROS + 1))

        @block.gpsimd
        def _(eng):
            eng.iota(lead_i.bitcast(I32), pattern=[[-1, NE]], base=NE, channel_multiplier=0).then_inc(lead0, 1)
            eng.wait_ge(lead0, 1)
            eng.tensor_copy(lead, lead_i.bitcast(I32)).then_inc(made, 1)
            eng.memset(zeros, 0.0).then_inc(made, 1)
            eng.memset(ones, 1.0).then_inc(made, 1)
            eng.wait_ge(made, 3)
            eng.affine_select(out=before, in_=ones, compare_op=ALU.is_gt, fill=0.0, base=0, pattern=[[1, P]],
                              channel_multiplier=-1).then_inc(made, 1)
            eng.iota(step_i.bitcast(I32), pattern=[[P, NT]], base=0, channel_multiplier=0).then_inc(lead0, 1)
            eng.iota(slot_i.bitcast(I32), pattern=[[1, SLOTS]], base=0, channel_multiplier=0).then_inc(lead0, 1)
            eng.wait_ge(lead0, 3)
            eng.tensor_copy(step_f, step_i.bitcast(I32)).then_inc(made, 1)
            eng.tensor_copy(slot_f, slot_i.bitcast(I32)).then_inc(made, 1)

            def step(m, b, u):
                if seen(m, 2):
                    eng.wait_ge(summed, m - 1)
                eng.tensor_copy(at[b].bitcast(I32), last_i[:, bass.ds(m * MACRO, MACRO)]).then_inc(at_ready, 1)
                hold(eng, at_ready, m + 1, passed)
                for t in range(MACRO):
                    eng.indirect_dma_start(row[b][:, t], None, part_d, bass.IndirectOffsetOnAxis(
                        at[b][:, t:t + 1].bitcast(I32), 0), bounds_check=EP - 1, oob_is_err=False)\
                       .then_inc(row_in[b], 16)

            drive(eng, step, MACROS)

            def scatter(i, b, u):
                hold(eng, staged, i + 1, passed)
                for n in range(2):
                    eng.indirect_dma_start(slot_d, bass.IndirectOffsetOnAxis(send_at[b][:, n:n + 1].bitcast(I32), 0),
                                           send[b], None, bounds_check=SLOTS * P - 1, oob_is_err=False)\
                       .then_inc(sent[b], 16)

            drive_slots(eng, scatter, NT)

            def turn(s, b, u):
                hold(eng, y_ready, s + 1, passed)
                hold(eng, y_at_ready, s + 1, passed)
                eng.indirect_dma_start(y_d, bass.IndirectOffsetOnAxis(y_at[b].bitcast(I32), 0), ys[b], None,
                                       bounds_check=2 * NP - 1, oob_is_err=False).then_inc(y_out[b], 16)

            drive_slots(eng, turn, SLOTS)

        @block.tensor
        def _(eng):
            eng.wait_ge(gates_in, 32)

            def gates(i, b):
                eng.wait_ge(xfT_sb, i + 1)
                if seen(i, 2):
                    eng.wait_ge(logits, i - 1)
                for c in range(KD):
                    mm = eng.matmul(L[b][:, 0:NE], xfT[b][:, c], gw[:, c], start=c == 0, stop=c == KD - 1)
                mm.then_inc(gate_ps, 1)

            def step(i, b, u):
                if is_tile(i):
                    eng.wait_ge(xf_ready, i + 1)
                    if seen(i, 2):
                        eng.wait_ge(xfT_sb, i - 1)
                    for c in range(KD):
                        mm = eng.transpose(T[b][:, c * P:(c + 1) * P], xf[b][:, c * P:(c + 1) * P], ident[:])
                    mm.then_inc(xfT_ps, 1)
                if seen(i):
                    gates(i - 1, 1 - b)

            drive(eng, step, NT)
            step(NT, NT % 2, NT // 2)
            eng.wait_ge(made, 6)
            eng.wait_ge(sel_ready, 1)
            picked = hit.rearrange("p t e -> p (t e)")
            eng.matmul(HT[0][:, 0:NT * NE], ones, picked, start=True, stop=True)
            eng.matmul(HT[1][:, 0:NT * NE], before, picked, start=True, stop=True).then_inc(counts_ps, 1)
            eng.wait_ge(routed, 1)
            eng.wait_ge(loaded, 64)

            def columns(s, b, u):
                eng.wait_ge(slot_in[b], 16 * (u + 1))
                if seen(s, 2):
                    eng.wait_ge(xT_sb, s - 1)
                for c in range(KD):
                    mm = eng.transpose(XT[b % 2][:, c * P:(c + 1) * P], slot[b][:, c * P:(c + 1) * P], ident[:])
                mm.then_inc(xT_ps, 1)

            def up(s, b):
                e = expert_of(eng, s)
                eng.wait_ge(xT_sb, s + 1)
                if seen(s, 2):
                    eng.wait_ge(h_sum, s - 1)
                for c in range(KD):
                    mm = eng.matmul(HP[b % 2][:], xT[b % 2][:, c], w1[:, bass.ds(e * KD + c, 1), :]
                                    .rearrange("p o n -> p (o n)"), start=c == 0, stop=c == KD - 1)
                mm.then_inc(h_ps, 1)

            def hidden_columns(s, b):
                eng.wait_ge(act_ready, s + 1)
                if seen(s, 2):
                    eng.wait_ge(hT_sb, s - 1)
                for j in range(HC):
                    mm = eng.transpose(HT[b % 2][:, j * P:(j + 1) * P], act[b % 2][:, j * P:(j + 1) * P], ident[:])
                mm.then_inc(hT_ps, 1)

            def down(s, b):
                e = expert_of(eng, s)
                eng.wait_ge(hT_sb, s + 1)
                if seen(s, 2):
                    eng.wait_ge(y_sum, s - 1)
                for j in range(HC):
                    mm = eng.matmul(YP[b % 2][:, 0:D], hT[b % 2][:, j], w2[:, bass.ds(e * HC + j, 1), :]
                                    .rearrange("p o n -> p (o n)"), start=j == 0, stop=j == HC - 1)
                mm.then_inc(y_ps, 1)

            columns(0, 0, 0)

            def turn(s, b, u):
                before_it, after_it = (b + 3) % 4, (b + 1) % 4
                if seen(s) and is_slot(s - 1):
                    hidden_columns(s - 1, before_it)
                if is_slot(s):
                    up(s, b)
                if seen(s) and is_slot(s - 1):
                    down(s - 1, before_it)
                if is_slot(s + 1):
                    columns(s + 1, after_it, u + (b == 3))

            drive_slots(eng, turn)

        @block.scalar
        def _(eng):
            def weigh_parts(m, b, u):
                eng.wait_ge(diffs, 2 * m + 2)
                eng.activation(w.rearrange("p t h -> p (t h)"), d.rearrange("p t h -> p (t h)"), ACT.Exp, scale=SCALE)\
                   .then_inc(weights, 1)

            drive(eng, weigh_parts, MACROS)
            eng.wait_ge(mom_ready, 1)
            eng.activation(std, moments[:, :, 1], ACT.Sqrt, bias=eps[:]).then_inc(std_ready, 1)

            def step(i, b, u):
                eng.wait_ge(xfT_ps, i + 1)
                if seen(i, 2):
                    eng.wait_ge(gate_ps, i - 1)
                eng.activation(xfT[b].rearrange("p k n -> p (k n)"), T[b][:, 0:D], ACT.Copy).then_inc(xfT_sb, 1)

            drive(eng, step, NT)
            eng.wait_ge(shifted, 1)
            eng.activation(prob.rearrange("p t e -> p (t e)"), prob.rearrange("p t e -> p (t e)"), ACT.Exp)\
               .then_inc(exps, 1)

            def columns(s, b):
                eng.wait_ge(xT_ps, s + 1)
                if seen(s, 2):
                    eng.wait_ge(h_ps, s - 1)
                eng.activation(xT[b % 2].rearrange("p k n -> p (k n)"), XT[b % 2][:, 0:D], ACT.Copy).then_inc(xT_sb, 1)

            def gelu(s, b):
                eng.wait_ge(h_sum, s + 1)
                if seen(s, 2):
                    eng.wait_ge(hT_ps, s - 1)
                eng.activation(act[b % 2], hs[b % 2], ACT.Gelu).then_inc(act_ready, 1)

            def hidden_columns(s, b):
                eng.wait_ge(hT_ps, s + 1)
                if seen(s, 2):
                    eng.wait_ge(y_ps, s - 1)
                eng.activation(hT[b % 2].rearrange("p k n -> p (k n)"), HT[b % 2][:], ACT.Copy).then_inc(hT_sb, 1)

            columns(0, 0)

            def turn(s, b, u):
                if seen(s) and is_slot(s - 1):
                    hidden_columns(s - 1, (b + 3) % 4)
                if is_slot(s):
                    gelu(s, b)
                if is_slot(s + 1):
                    columns(s + 1, (b + 1) % 4)

            drive_slots(eng, turn)

        @block.vector
        def _(eng):
            eng.wait_ge(gates_in, 32)
            eng.wait_ge(made, 6)
            STEPS = 16

            def add_up(m, b, u):
                n = [0]

                def link(ins):
                    n[0] += 1
                    ins.then_inc(chain, 1)
                    eng.wait_ge(chain, STEPS * m + n[0])

                def each(ap, width):
                    return ap.rearrange("p (t o) -> p t o", o=1).to_broadcast([P, MACRO, width])

                def messages(rows):
                    return rows[:, :, 0:D].rearrange("p t (h c) -> p t h c", h=H)

                rows, more = row[b], ext[b]
                top_of = slice(MSG, MSG + H)
                eng.wait_ge(row_in[b], 16 * MACRO * (u + 1))
                eng.wait_ge(ext_in[b], 32 * (u + 1))
                link(eng.tensor_tensor(has, rows[:, :, MSG + H], node_f[:, bass.ds(m * MACRO, MACRO)], ALU.is_equal))
                link(eng.tensor_scalar(off, has, 1.0, BIG, ALU.subtract, ALU.mult))
                link(eng.tensor_tensor(rows[:, :, top_of], rows[:, :, top_of], each(has, H), ALU.mult))
                link(eng.tensor_tensor(rows[:, :, top_of], rows[:, :, top_of], each(off, H), ALU.add))
                link(eng.tensor_tensor(peak, rows[:, :, top_of], more[:, :, top_of], ALU.max))
                if seen(m):
                    eng.wait_ge(weights, m)
                eng.tensor_tensor(d[:, :, 0:H], rows[:, :, top_of], peak, ALU.subtract).then_inc(diffs, 1)
                eng.tensor_tensor(d[:, :, H:], more[:, :, top_of], peak, ALU.subtract).then_inc(diffs, 1)
                eng.wait_ge(weights, m + 1)
                link(eng.tensor_tensor(w[:, :, 0:H], w[:, :, 0:H], each(has, H), ALU.mult))
                for part, ws in ((rows, w[:, :, 0:H]), (more, w[:, :, H:])):
                    eng.tensor_tensor(messages(part), messages(part), per_head(ws, MACRO), ALU.mult)
                    last = eng.tensor_tensor(part[:, :, D:MSG], part[:, :, D:MSG], ws, ALU.mult)
                link(last)
                link(eng.tensor_tensor(rows[:, :, 0:MSG], rows[:, :, 0:MSG], more[:, :, 0:MSG], ALU.add))
                link(eng.tensor_scalar(rows[:, :, D:MSG], rows[:, :, D:MSG], 1e-16, None, ALU.add))
                link(eng.reciprocal(rows[:, :, D:MSG], rows[:, :, D:MSG]))
                link(eng.tensor_tensor(messages(rows), messages(rows), per_head(rows[:, :, D:MSG], MACRO), ALU.mult))
                link(eng.tensor_tensor(rows[:, :, 0:D], rows[:, :, 0:D], x1[b], ALU.add))
                for t in range(MACRO):
                    last = eng.bn_stats(st6[:, t], rows[:, t, 0:D])
                link(last)
                eng.sem_inc(passed, 1)
                for t in range(MACRO):
                    last = eng.bn_aggr(mom[:, t], st6[:, t])
                link(last)
                link(eng.tensor_copy(moments[:, bass.ds(m * MACRO, MACRO), :], mom))
                link(eng.tensor_copy(acc[:, bass.ds(m * MACRO, MACRO), :], rows[:, :, 0:D]))
                eng.sem_inc(summed, 1)
                assert n[0] == STEPS, n

            drive(eng, add_up, MACROS)
            eng.sem_inc(mom_ready, 1)
            eng.wait_ge(std_ready, 1)
            eng.reciprocal(rstd, std).then_inc(rstd_ready, 1)
            eng.wait_ge(rstd_ready, 1)

            def normalise(i, b, u):
                if is_tile(i):
                    if seen(i, 2):
                        eng.wait_ge(xfT_ps, i - 1)
                    rows = acc[:, bass.ds(i, 1), :].rearrange("p o c -> p (o c)")
                    mean, scale = moments[:, bass.ds(i, 1), 0], rstd[:, bass.ds(i, 1)]
                    eng.tensor_scalar(xf[b], rows, mean, scale, ALU.subtract, ALU.mult).then_inc(xf_ready, 1)
                    eng.tensor_scalar(xs[:, bass.ds(i, 1), 0:D].rearrange("p o c -> p (o c)"), rows, mean, scale,
                                      ALU.subtract, ALU.mult).then_inc(xf_kept, 1)
                if seen(i, 2):
                    eng.wait_ge(gate_ps, i - 1)
                    eng.tensor_tensor(cw[:, bass.ds(i - 2, 1), :].rearrange("p o e -> p (o e)"), L[b][:, 0:NE],
                                      gb, ALU.add).then_inc(logits, 1)

            drive(eng, normalise, NT)
            for i in (NT, NT + 1):
                normalise(i, i % 2, i // 2)
            eng.wait_ge(logits, NT)
            eng.wait_ge(xf_kept, NT)
            done = [STEPS * MACROS]

            def link(ins):
                done[0] += 1
                ins.then_inc(chain, 1)
                eng.wait_ge(chain, done[0])

            def by_tile(ap):
                return ap.rearrange("p (t o) -> p t o", o=1).to_broadcast([P, NT, NE])

            link(eng.tensor_reduce(top, cw, AX, ALU.max))
            eng.tensor_tensor(prob, cw, by_tile(top), ALU.subtract).then_inc(shifted, 1)
            eng.wait_ge(exps, 1)
            link(eng.tensor_reduce(top, prob, AX, ALU.add))
            link(eng.reciprocal(top, top))
            link(eng.tensor_tensor(prob, prob, by_tile(top), ALU.mult))
            lead_t = lead.rearrange("p (o e) -> p o e", o=1).to_broadcast([P, NT, NE])
            link(eng.tensor_copy(two, prob))
            for chosen in (one, two):
                link(eng.tensor_reduce(top, two, AX, ALU.max))
                link(eng.tensor_tensor(hit, two, by_tile(top), ALU.is_equal))
                link(eng.tensor_tensor(rank, hit, lead_t, ALU.mult))
                link(eng.tensor_reduce(top, rank, AX, ALU.max))
                link(eng.tensor_tensor(chosen, rank, by_tile(top), ALU.is_equal))
                if chosen is one:
                    link(eng.scalar_tensor_tensor(two, one, -2.0, prob, ALU.mult, ALU.add))
            eng.tensor_tensor(hit, one, two, ALU.add).then_inc(sel_ready, 1)
            eng.wait_ge(sel_ready, 1)
            eng.tensor_tensor(xs[:, :, D:D + NE], prob, hit, ALU.mult)
            nodes = node_f[:].rearrange("p (t o) -> p t o", o=1).to_broadcast([P, NT, NE])
            eng.scalar_tensor_tensor(xs[:, :, D + NE:], nodes, 2.0, two, ALU.mult, ALU.add)
            eng.wait_ge(counts_ps, 1)
            here = HT[0][:, 0:NT * NE].rearrange("p (t e) -> p e t", e=NE)
            ahead = HT[1][:, 0:NT * NE].rearrange("p (t e) -> p e t", e=NE)
            for e in range(NE):
                last = eng.tensor_tensor_scan(incl[:, e], zeros, here[:, e], 0.0, ALU.add, ALU.add)
            link(last)
            link(eng.tensor_tensor(more, incl[:, :, NT - 1:NT].to_broadcast([P, NE, NT]),
                                   step_f.rearrange("p (o t) -> p o t", o=1).to_broadcast([P, NE, NT]), ALU.is_gt))
            link(eng.tensor_reduce(tiles, more, AX, ALU.add))
            link(eng.tensor_tensor_scan(ends, zeros[:, 0:NE], tiles, 0.0, ALU.add, ALU.add))
            link(eng.tensor_tensor(starts, ends, tiles, ALU.subtract))
            link(eng.scalar_tensor_tensor(incl, starts.rearrange("p (e o) -> p e o", o=1).to_broadcast([P, NE, NT]),
                                          float(P), incl, ALU.mult, ALU.add))
            link(eng.tensor_tensor(incl, incl, here, ALU.subtract))
            link(eng.tensor_tensor(incl, incl, ahead, ALU.add))
            places = incl.rearrange("p e t -> p t e")
            for n, chosen in enumerate((one, two)):
                link(eng.tensor_tensor(rank, chosen, places, ALU.mult))
                link(eng.tensor_reduce(top, rank, AX, ALU.add))
                link(eng.tensor_copy(to_i[:, :, n].bitcast(I32), top))
            link(eng.tensor_tensor(passed_e, slot_f.rearrange("p (s o) -> p s o", o=1).to_broadcast([P, SLOTS, NE]),
                                   ends.rearrange("p (o e) -> p o e", o=1).to_broadcast([P, SLOTS, NE]), ALU.is_ge))
            link(eng.tensor_reduce(expert_f, passed_e, AX, ALU.add))
            link(eng.tensor_scalar(expert_f, expert_f, float(NE - 1), None, ALU.min))
            eng.tensor_copy(expert_i.bitcast(I32), expert_f).then_inc(routed, 1)
            eng.wait_ge(routed, 1)

            def stage_rows(i, b, u):
                if seen(i, 4):
                    eng.wait_ge(sent[b], 32 * u)
                eng.tensor_copy(send[b], xs[:, bass.ds(i, 1), :].rearrange("p o c -> p (o c)"))
                eng.tensor_copy(send_at[b].bitcast(I32), to_i[:, bass.ds(i, 1), :].rearrange("p o n -> p (o n)")
                                .bitcast(I32)).then_inc(staged, 1)

            drive_slots(eng, stage_rows, NT)
            eng.wait_ge(loaded, 64)

            def add_first_bias(s, b):
                e = expert_of(eng, s)
                eng.wait_ge(h_ps, s + 1)
                if seen(s, 2):
                    eng.wait_ge(act_ready, s - 1)
                eng.tensor_tensor(hs[b % 2], HP[b % 2][:], b1r[:, bass.ds(e, 1), :].rearrange("p o n -> p (o n)"),
                                  ALU.add).then_inc(h_sum, 1)

            def weigh(s, b, u):
                e = expert_of(eng, s)
                eng.wait_ge(y_ps, s + 1)
                if seen(s, 4):
                    eng.wait_ge(y_out[b], 16 * u)
                eng.tensor_copy(y_at[b].bitcast(I32), slot[b][:, bass.ds(e + (D + NE), 1)]).then_inc(y_at_ready, 1)
                eng.tensor_tensor(ys[b], YP[b % 2][:, 0:D], b2r[:, bass.ds(e, 1), :].rearrange("p o n -> p (o n)"),
                                  ALU.add).then_inc(y_sum, 1)
                eng.wait_ge(y_sum, s + 1)
                eng.tensor_scalar(ys[b], ys[b], slot[b][:, bass.ds(e + D, 1)], None, ALU.mult).then_inc(y_ready, 1)

            def turn(s, b, u):
                if is_slot(s):
                    add_first_bias(s, b)
                if seen(s) and is_slot(s - 1):
                    weigh(s - 1, (b + 3) % 4, u - (b == 0))

            drive_slots(eng, turn, peeled=2)

            for m in range(MACROS):
                eng.wait_ge(yy_in[m % 2], 16 * (m // 2 + 1))
                rows = acc[:, m * MACRO:(m + 1) * MACRO, :]
                eng.tensor_tensor(rows, rows, yy[m % 2][:, :, 0:D], ALU.add).then_inc(first_added, 1)
                eng.wait_ge(first_added, m + 1)
                eng.tensor_tensor(rows, rows, yy[m % 2][:, :, D:], ALU.add).then_inc(added, 1)


_INS = ["x", "src", "dst", "edge_attr_256", "L0_gnn_Wq", "L0_gnn_bq", "L0_gnn_Wk", "L0_gnn_bk", "L0_gnn_Wv",
        "L0_gnn_bv", "L0_gnn_We", "L0_gnn_Ws", "L0_gnn_bs", "L0_mix_Wq", "L0_mix_bq", "L0_mix_Wk", "L0_mix_bk",
        "L0_mix_Wv", "L0_mix_bv", "L0_mix_Wo", "L0_mix_bo", "L0_mix_W1", "L0_mix_b1", "L0_mix_W2", "L0_mix_b2",
        "L0_mix_ln1_g", "L0_mix_ln1_b", "L0_mix_ln2_g", "L0_mix_ln2_b", "L0_ffn_gate_w", "L0_ffn_gate_b",
        "L0_ffn_W1", "L0_ffn_b1", "L0_ffn_W2", "L0_ffn_b2"]


def kernel(**inputs):
    import numpy as np
    import concourse.bacc as bacc
    from concourse.bass_utils import run_bass_kernel_spmd

    nc = bacc.Bacc("TRN2", target_bir_lowering=False, num_devices=1)
    arrays, args = {}, {}
    for name in _INS:
        a = np.ascontiguousarray(inputs[name])
        if name == "x":
            a = np.concatenate([a, np.zeros((NP - N, D), a.dtype)])
        elif name == "edge_attr_256":
            a = np.concatenate([a, np.zeros((EP - E, D), a.dtype)])
        elif name == "src":
            a = np.concatenate([a, np.zeros(EP - E, a.dtype)])
        elif name == "dst":
            a = np.concatenate([a, np.full(EP - E, N, a.dtype), np.full(P, N + 1, a.dtype)])
        arrays[f"in_{name}"] = a
        args[name] = nc.dram_tensor(f"in_{name}", a.shape, mybir.dt.from_np(a.dtype), kind="ExternalInput").ap()
    out = nc.dram_tensor("out", [N, D], F32, kind="ExternalOutput").ap()
    build(nc, **args, out=out)
    return run_bass_kernel_spmd(nc, [arrays], core_ids=[0]).results[0]["out"]
```

```python
from contextlib import ExitStack

import concourse.bass as bass
from concourse import mybir

F32 = mybir.dt.float32
I32 = mybir.dt.int32
ALU = mybir.AluOpType
ACT = mybir.ActivationFunctionType
AX = mybir.AxisListType.X

P = 128
N, E, D, H = 6250, 106250, 256, 8
C = D // H
KD = D // P
NT = -(-N // P)
NP = NT * P
LAST = N - (NT - 1) * P
G = 8
PAIRS = G // 2
NG = -(-E // (P * G))
TILES = NG * G
EP = TILES * P
SCALE = float(C) ** -0.5
BIG = 1e30
MSG = D + H
ROW = MSG + H + 1
CHUNKS = -(-TILES // P)
FF = 1024
FC = FF // P
HD = 512
HC = HD // P
NE = 8
MACRO = 7
MACROS = NT // MACRO
SLOTS = (2 * NP + NE * (P - 1)) // P
XROW = D + 2 * NE
KVW = P + H // KD
LN_EPS = 1e-5


class Carve:

    def __init__(self, arena, size):
        self.arena, self.size, self.at = arena, size, 0

    def __call__(self, *shape):
        n = 1
        for s in shape:
            n *= s
        piece = self.arena[:, self.at:self.at + n]
        self.at += n
        assert self.at <= self.size, (self.at, self.size)
        if len(shape) == 2:
            return piece.rearrange("p (a b) -> p a b", a=shape[0])
        if len(shape) == 3:
            return piece.rearrange("p (a b c) -> p a b c", a=shape[0], b=shape[1])
        return piece


def rows_as_tiles(ap):
    return ap.rearrange("(t p) c -> p t c", p=P)


def over_partitions(ap):
    return ap.rearrange("(o n) -> o n", o=1).to_broadcast([P, ap.shape[0]])


def per_channel(ap):
    return ap.rearrange("(k p) -> p k", p=P)


def per_head(ap, tiles=None):
    if tiles is None:
        return ap.rearrange("p (h o) -> p h o", o=1).to_broadcast([P, H, C])
    return ap.rearrange("p t (h o) -> p t h o", o=1).to_broadcast([P, tiles, H, C])


def hold(eng, sem, value, passed):
    eng.wait_ge(sem, value)
    eng.sem_inc(passed, 1)


def heads(ap):
    return ap.rearrange("p (h c) -> p h c", h=H)


def build(nc, x, src, dst, edge_attr_256, L0_gnn_Wq, L0_gnn_bq, L0_gnn_Wk, L0_gnn_bk, L0_gnn_Wv, L0_gnn_bv,
          L0_gnn_We, L0_gnn_Ws, L0_gnn_bs, L0_mix_Wq, L0_mix_bq, L0_mix_Wk, L0_mix_bk, L0_mix_Wv, L0_mix_bv,
          L0_mix_Wo, L0_mix_bo, L0_mix_W1, L0_mix_b1, L0_mix_W2, L0_mix_b2, L0_mix_ln1_g, L0_mix_ln1_b,
          L0_mix_ln2_g, L0_mix_ln2_b, L0_ffn_gate_w, L0_ffn_gate_b, L0_ffn_W1, L0_ffn_b1, L0_ffn_W2, L0_ffn_b2,
          out):
    ctx = ExitStack()
    with ctx:
        def sb(name, shape, dt=F32):
            return ctx.enter_context(nc.sbuf_tensor(name, shape, dt))

        def stage(program, *operands):
            own = []

            def sem(name):
                own.append(nc.alloc_semaphore(name))
                return own[-1]

            program(nc, sem, psum, *operands)
            nc.clear_and_free_semaphores(own)
            nc.all_engine_barrier()

        def dram(name, shape, dt=F32):
            return nc.dram_tensor(name, shape, dt, kind="Internal").ap()

        kv_d = dram("kv_d", [NP, 2 * D])
        q_d = dram("q_d", [NP, D])
        xn_d = dram("xn_d", [NP, D])
        xs_d = dram("xs_d", [NP, D])
        x1_d = dram("x1_d", [NP, D])
        part_d = dram("part_d", [EP, ROW])
        slot_d = dram("slot_d", [SLOTS * P, XROW])
        y_d = dram("y_d", [2 * NP, D])
        extra_d = dram("extra_d", [NP, ROW])

        psum = [ctx.enter_context(nc.psum_tensor(f"bank{i}", [P, 512], F32)) for i in range(8)]
        ident = sb("ident", [P, P])
        eps = sb("eps", [P, 1])
        src_t = sb("src_t", [P, TILES], I32)
        dst_t = sb("dst_t", [P, TILES], I32)
        dst_f = sb("dst_f", [P, TILES])
        state = sb("state", [P, KD, KVW])
        last_i = sb("last_i", [P, NT], I32)
        node_f = sb("node_f", [P, NT])
        ARENA = 49500
        arena = sb("arena", [P, ARENA])

        stage(prepare, ident, eps, src_t, dst_t, dst_f, state, node_f, last_i, Carve(arena, ARENA), x, src, dst,
                (L0_gnn_Wk, L0_gnn_Wv, L0_gnn_Wq, L0_gnn_Ws, L0_mix_Wk, L0_mix_Wv),
                (L0_gnn_bk, L0_gnn_bv, L0_gnn_bq, L0_gnn_bs, L0_mix_bk, L0_mix_bv, L0_mix_ln2_b),
                kv_d, q_d, xn_d, xs_d, extra_d)
        stage(edges_and_mix, ident, eps, src_t, dst_t, dst_f, state, Carve(arena, ARENA), dst,
                      edge_attr_256, L0_gnn_We,
                      (L0_mix_Wq, L0_mix_Wo, L0_mix_W1, L0_mix_W2), (L0_mix_bq, L0_mix_b1),
                      (L0_mix_bo, L0_mix_ln1_g, L0_mix_ln1_b, L0_mix_b2, L0_mix_ln2_g),
                      kv_d, q_d, xn_d, xs_d, x1_d, part_d, slot_d)
        stage(merge, ident, Carve(arena, ARENA), dst, part_d, extra_d)
        stage(experts, ident, eps, node_f, last_i, Carve(arena, ARENA), part_d, extra_d, x1_d,
                L0_ffn_gate_w, L0_ffn_gate_b, L0_ffn_W1, L0_ffn_b1, L0_ffn_W2, L0_ffn_b2, slot_d, y_d, out)


def prepare(nc, sem, psum, ident, eps, src_t, dst_t, dst_f, state, node_f, last_i, carve, x, src, dst, weights, biases,
            kv_d, q_d, xn_d, xs_d, extra_d):
    w6 = carve(6, KD, D)
    b6 = carve(7, D)
    xt = [carve(D) for _ in range(2)]
    xb = [carve(D) for _ in range(2)]
    xn = [carve(D) for _ in range(2)]
    xnT = [carve(KD, P) for _ in range(2)]
    kv = [carve(2 * D) for _ in range(2)]
    qs = [carve(2 * D) for _ in range(2)]
    mk = [carve(D) for _ in range(2)]
    mv = [carve(KD, P + 1) for _ in range(2)]
    neg = [carve(D) for _ in range(2)]
    phi = [carve(D) for _ in range(2)]
    st6 = carve(6)
    mom = [carve(2) for _ in range(2)]
    std = [carve(1) for _ in range(2)]
    rstd = carve(1)
    empty = carve(ROW)
    rows_i = carve(2, CHUNKS, P)
    rows_f = carve(2, CHUNKS, P)
    node_i = carve(NT)
    pick, ends = carve(P), carve(TILES)
    hits = [carve(TILES) for _ in range(2)]
    nodes_of = [carve(P) for _ in range(2)]
    count_hits = [carve(P) for _ in range(2)]
    at = [carve(1) for _ in range(2)]
    tile_f, cnt = carve(NT), carve(NT)

    passed = sem("pa_passed")
    loaded, ident0, made = sem("prep_loaded"), sem("ident_zeroed"), sem("consts_made")
    rows_in, rows_cast, rowT_ps, rowT_sb = sem("rows_in"), sem("rows_cast"), sem("rowT_ps"), sem("rowT_sb")
    x_in = [sem(f"x_in{b}") for b in range(2)]
    stats, mom_ready, std_ready, rstd_ready, xn_ready = (sem(n) for n in (
        "pa_stats", "pa_mom", "pa_std", "pa_rstd", "xn_ready"))
    xnT_ps, xnT_sb, kv_ps, qs_ps, mix_ps, acc_done = (sem(n) for n in (
        "xnT_ps", "xnT_sb", "kv_ps", "qs_ps", "mixkv_ps", "state_added"))
    kv_sb, xb_ready, xs_sb, mk_sb, neg_sb, exp_sb, phi_sb = (sem(n) for n in (
        "kv_sb", "xb_ready", "xs_sb", "mixk_sb", "neg_sb", "exp_sb", "phi_sb"))
    stored = [sem(f"pa_stored{b}") for b in range(2)]
    bias_made = sem("bias_made")
    extra_out, state_zero, state_done = sem("extra_out"), sem("state_zeroed"), sem("state_copied")
    pick0, pick_made, ends_ps, ends_sb = sem("pick0"), sem("pick_made"), sem("ends_ps"), sem("ends_sb")
    tile_found, at_ready, counted, last_found = (sem(n) for n in (
        "tile_found", "tile_at", "edges_counted", "last_found"))
    nodes_in = [sem(f"nodes_in{b}") for b in range(2)]
    T, KV, QS, MX, A0, A1 = (psum[0], psum[6]), psum[1], psum[2], psum[3], psum[4], psum[5]
    HALF = TILES // 2
    src_v, dst_v = src.rearrange("(t e) -> t e", e=P), dst.rearrange("(t e) -> t e", e=P)
    full = TILES // P
    rest = TILES - full * P
    NROWS = 4 if rest else 2

    def drive(eng, step):
        for i in range(2):
            step(i, i % 2, i // 2)
        with eng.Fori(0, (NT - 3) // 2) as k:
            step(2 * k + 2, 0, k + 1)
            step(2 * k + 3, 1, k + 1)
        step(NT - 1, (NT - 1) % 2, (NT - 1) // 2)

    assert NT % 2 == 1

    with nc.Block() as block:
        @block.sync
        def _(eng):
            for a, view in enumerate((src_v, dst_v)):
                eng.dma_start(rows_i[:, a, 0:full].bitcast(I32),
                              view[0:full * P].rearrange("(k p) e -> p k e", p=P)).then_inc(rows_in, 16)
                if rest:
                    eng.dma_start(rows_i[0:rest, a, full].bitcast(I32),
                                  view[full * P:TILES]).then_inc(rows_in, 16)
            eng.dma_start(xt[0], x[0:P, :]).then_inc(x_in[0], 16)
            eng.dma_start(xt[1], x[P:2 * P, :]).then_inc(x_in[1], 16)
            for w in range(6):
                eng.dma_start(w6[:, w], weights[w].rearrange("(k p) n -> p k n", p=P)).then_inc(loaded, 16)
            for w in range(7):
                eng.dma_start(b6[:, w], over_partitions(biases[w])).then_inc(loaded, 16)
            eng.wait_ge(made, 6)
            eng.dma_start(rows_as_tiles(extra_d),
                          empty.rearrange("p (o c) -> p o c", o=1).to_broadcast([P, NT, ROW])).then_inc(extra_out, 16)

            def store(i, b, u):
                eng.wait_ge(xn_ready, i + 1)
                eng.dma_start(xn_d[bass.ds(i * P, P), :], xn[b]).then_inc(stored[b], 16)
                if not isinstance(i, int) or i < NT - 2:
                    hold(eng, xb_ready, i + 1, passed)
                    eng.dma_start(xt[b], x[bass.ds((i + 2) * P, P), :]).then_inc(x_in[b], 16)
                eng.wait_ge(kv_sb, i + 1)
                eng.dma_start(kv_d[bass.ds(i * P, P), :], kv[b]).then_inc(stored[b], 16)
                eng.wait_ge(xs_sb, i + 1)
                eng.dma_start(q_d[bass.ds(i * P, P), :], qs[b][:, 0:D]).then_inc(stored[b], 16)
                eng.dma_start(xs_d[bass.ds(i * P, P), :], qs[b][:, D:]).then_inc(stored[b], 16)

            store(0, 0, 0)
            with eng.Fori(0, (NT - 3) // 2) as k:
                store(2 * k + 1, 1, k)
                store(2 * k + 2, 0, k + 1)
            for i in (NT - 2, NT - 1):
                store(i, i % 2, i // 2)
            for b in range(2):
                eng.wait_ge(stored[b], 64 * ((NT + 1 - b) // 2))
            eng.wait_ge(extra_out, 16)

        @block.gpsimd
        def _(eng):
            eng.memset(ident[:], 0.0).then_inc(ident0, 1)
            eng.memset(eps[:], LN_EPS).then_inc(made, 1)
            eng.memset(empty[:, 0:MSG], 0.0).then_inc(made, 1)
            eng.memset(empty[:, MSG:ROW], -BIG).then_inc(made, 1)
            for b in range(2):
                eng.memset(mv[b][:, :, P:P + 1], 1.0).then_inc(made, 1)
            eng.wait_ge(ident0, 1)
            eng.affine_select(out=ident[:], in_=ident[:], compare_op=ALU.not_equal, fill=1.0, base=0,
                              pattern=[[-1, P]], channel_multiplier=1).then_inc(made, 1)
            eng.iota(node_i.bitcast(I32), pattern=[[P, NT]], base=0, channel_multiplier=1).then_inc(ident0, 1)
            eng.wait_ge(ident0, 2)
            eng.tensor_copy(node_f[:], node_i.bitcast(I32)).then_inc(made, 1)
            eng.memset(pick, 0.0).then_inc(pick0, 1)
            eng.wait_ge(pick0, 1)
            eng.affine_select(out=pick, in_=pick, compare_op=ALU.not_equal, fill=1.0, base=-(P - 1),
                              pattern=[[0, P]], channel_multiplier=1).then_inc(pick_made, 1)

            def look_up(i, b, u):
                if not isinstance(i, int) or i >= 2:
                    eng.wait_ge(counted, i - 1)
                hold(eng, at_ready, i + 1, passed)
                eng.indirect_dma_start(nodes_of[b].bitcast(I32), None, dst_v, bass.IndirectOffsetOnAxis(
                    at[b].bitcast(I32), 0), bounds_check=TILES - 1, oob_is_err=False).then_inc(nodes_in[b], 16)

            def add_x(i, b, u):
                eng.wait_ge(x_in[b], 16 * (u + 1))
                if not isinstance(i, int) or i >= 2:
                    hold(eng, xs_sb, i - 1, passed)
                eng.tensor_tensor(xb[b], xt[b], b6[:, 3], ALU.add).then_inc(xb_ready, 1)

            def step(i, b, u):
                if not isinstance(i, int) or i < NT - 1:
                    add_x(i + 1, 1 - b, u + b)
                look_up(i, b, u)

            eng.wait_ge(bias_made, 1)
            add_x(0, 0, 0)
            drive(eng, step)

        @block.tensor
        def _(eng):
            eng.wait_ge(made, 6)
            for n in range(2 * CHUNKS):
                a, k = divmod(n, CHUNKS)
                rows = P if k < full else rest
                eng.wait_ge(rows_cast, a + 1)
                if n >= 2:
                    eng.wait_ge(rowT_sb, n - 1)
                eng.transpose(psum[6 + n % 2][:, 0:rows], rows_f[0:rows, a, k], ident[0:rows, 0:rows])\
                   .then_inc(rowT_ps, 1)
            eng.wait_ge(rowT_sb, 2 * CHUNKS)
            eng.wait_ge(pick_made, 1)
            for n in range(2):
                mm = eng.matmul(psum[6 + n][:, 0:HALF], pick, dst_f[:, n * HALF:(n + 1) * HALF], start=True, stop=True)
            mm.then_inc(ends_ps, 1)
            eng.wait_ge(loaded, 13 * 16)
            eng.wait_ge(ends_sb, 1)

            def add_state(i, b, u, first, last):
                rows = LAST if last else P
                eng.wait_ge(phi_sb, i + 1)
                for c, bank in enumerate((A0, A1)):
                    mm = eng.matmul(bank[:, 0:P + 1], phi[b][0:rows, c * P:(c + 1) * P], mv[b][0:rows, c, :],
                                    start=first, stop=last, skip_group_check=True)
                mm.then_inc(acc_done, 1)

            def columns(i, b):
                eng.wait_ge(xn_ready, i + 1)
                if not isinstance(i, int) or i >= 2:
                    eng.wait_ge(xnT_sb, i - 1)
                for c in range(KD):
                    mm = eng.transpose(T[b][:, c * P:(c + 1) * P], xn[b][:, c * P:(c + 1) * P], ident[:])
                mm.then_inc(xnT_ps, 1)

            def products(i, b):
                eng.wait_ge(xnT_sb, i + 1)
                for n, (bank, done, out_of) in enumerate(((KV, kv_ps, kv_sb), (QS, qs_ps, xs_sb), (MX, mix_ps, mk_sb))):
                    if not isinstance(i, int) or i >= 1:
                        eng.wait_ge(out_of, 2 * i if bank is MX else i)
                    for c in range(KD):
                        mm = eng.matmul(bank[:].rearrange("p (w n) -> p w n", w=2), xnT[b][:, c],
                                        w6[:, 2 * n:2 * n + 2, c], start=c == 0, stop=c == KD - 1)
                    mm.then_inc(done, 1)

            def step(i, b, u):
                products(i, b)
                if not isinstance(i, int) or i < NT - 1:
                    columns(i + 1, 1 - b)

            columns(0, 0)
            step(0, 0, 0)
            step(1, 1, 0)
            add_state(0, 0, 0, True, False)
            with eng.Fori(0, (NT - 3) // 2) as k:
                step(2 * k + 2, 0, k + 1)
                add_state(2 * k + 1, 1, k, False, False)
                step(2 * k + 3, 1, k + 1)
                add_state(2 * k + 2, 0, k + 1, False, False)
            i = NT - 1
            step(i, i % 2, i // 2)
            add_state(i - 1, (i - 1) % 2, (i - 1) // 2, False, False)
            add_state(i, i % 2, i // 2, False, True)

        @block.scalar
        def _(eng):
            eng.wait_ge(made, 6)

            def deviation(i, b):
                eng.wait_ge(mom_ready, i + 1)
                eng.activation(std[b], mom[b][:, 1:2], ACT.Sqrt, bias=eps[:]).then_inc(std_ready, 1)

            def columns(i, b):
                eng.wait_ge(xnT_ps, i + 1)
                if not isinstance(i, int) or i >= 2:
                    eng.wait_ge(mix_ps, i - 1)
                eng.activation(xnT[b].rearrange("p k n -> p (k n)"), T[b][:, 0:D], ACT.Copy).then_inc(xnT_sb, 1)

            def step(i, b, u):
                if not isinstance(i, int) or i < NT - 1:
                    deviation(i + 1, 1 - b)
                    columns(i + 1, 1 - b)
                eng.wait_ge(neg_sb, i + 1)
                eng.activation(neg[b], neg[b], ACT.Exp).then_inc(exp_sb, 1)

            deviation(0, 0)
            columns(0, 0)
            drive(eng, step)

        @block.vector
        def _(eng):
            eng.wait_ge(rows_in, 16 * NROWS)
            for a in range(2):
                eng.tensor_copy(rows_f[:, a, 0:full], rows_i[:, a, 0:full].bitcast(I32))
                last = eng.tensor_copy(rows_f[0:rest, a, full], rows_i[0:rest, a, full].bitcast(I32))
                last.then_inc(rows_cast, 1)
            for n in range(2 * CHUNKS):
                a, k = divmod(n, CHUNKS)
                rows = P if k < full else rest
                eng.wait_ge(rowT_ps, n + 1)
                if a:
                    eng.tensor_copy(dst_f[:, k * P:k * P + rows], psum[6 + n % 2][:, 0:rows])
                eng.tensor_copy((src_t, dst_t)[a][:, k * P:k * P + rows], psum[6 + n % 2][:, 0:rows])\
                   .then_inc(rowT_sb, 1)
            eng.wait_ge(loaded, 13 * 16)
            eng.wait_ge(made, 7)
            eng.wait_ge(ends_ps, 1)
            for n in range(2):
                last = eng.tensor_copy(ends[:, n * HALF:(n + 1) * HALF], psum[6 + n][:, 0:HALF])
            last.then_inc(ends_sb, 1)
            eng.wait_ge(ends_sb, 1)
            eng.tensor_tensor(b6[:, 3], b6[:, 3], b6[:, 6], ALU.add).then_inc(bias_made, 1)
            eng.wait_ge(bias_made, 1)

            def normalise(i, b, u):
                eng.wait_ge(x_in[b], 16 * (u + 1))
                eng.bn_stats(st6, xt[b]).then_inc(stats, 1)
                hold(eng, stats, i + 1, passed)
                eng.bn_aggr(mom[b], st6).then_inc(mom_ready, 1)
                eng.wait_ge(std_ready, i + 1)
                eng.reciprocal(rstd, std[b]).then_inc(rstd_ready, 1)
                eng.wait_ge(rstd_ready, i + 1)
                if not isinstance(i, int) or i >= 2:
                    eng.wait_ge(stored[b], 64 * u)
                eng.tensor_scalar(xn[b], xt[b], mom[b][:, 0:1], rstd, ALU.subtract, ALU.mult).then_inc(xn_ready, 1)

            def add_bias(i, b, u):
                eng.wait_ge(kv_ps, i + 1)
                eng.tensor_tensor(kv[b], KV[:], b6[:, 0:2].rearrange("p w n -> p (w n)"), ALU.add).then_inc(kv_sb, 1)
                eng.wait_ge(qs_ps, i + 1)
                eng.wait_ge(xb_ready, i + 1)
                eng.tensor_tensor(qs[b][:, 0:D], QS[:, 0:D], b6[:, 2], ALU.add)
                eng.tensor_tensor(qs[b][:, D:], QS[:, D:], xb[b], ALU.add).then_inc(xs_sb, 1)
                eng.wait_ge(mix_ps, i + 1)
                if not isinstance(i, int) or i >= 2:
                    eng.wait_ge(acc_done, i - 1)
                eng.tensor_tensor(mk[b], MX[:, 0:D], b6[:, 4], ALU.add).then_inc(mk_sb, 1)
                eng.tensor_tensor(mv[b][:, :, 0:P], MX[:, D:].rearrange("p (k n) -> p k n", k=KD),
                                  b6[:, 5].rearrange("p (k n) -> p k n", k=KD), ALU.add).then_inc(mk_sb, 1)
                eng.wait_ge(mk_sb, 2 * i + 1)
                eng.tensor_scalar(neg[b], mk[b], 0.0, None, ALU.min).then_inc(neg_sb, 1)

            def feature(i, b, u):
                eng.wait_ge(exp_sb, i + 1)
                eng.scalar_tensor_tensor(phi[b], mk[b], 0.0, neg[b], ALU.max, ALU.add).then_inc(phi_sb, 1)

            def find_tile(i, b):
                eng.tensor_scalar(hits[b], ends, node_f[:, bass.ds(i, 1)], 0.0, ALU.is_le, ALU.add,
                                  accum_out=tile_f[:, bass.ds(i, 1)]).then_inc(tile_found, 1)

            def name_tile(i, b):
                eng.wait_ge(tile_found, i + 1)
                if not isinstance(i, int) or i >= 2:
                    eng.wait_ge(counted, i - 1)
                eng.tensor_scalar(at[b].bitcast(I32), tile_f[:, bass.ds(i, 1)], float(TILES - 1), None, ALU.min)\
                   .then_inc(at_ready, 1)

            def count_edges(i, b, u):
                eng.wait_ge(nodes_in[b], 16 * (u + 1))
                eng.tensor_scalar(count_hits[b], nodes_of[b].bitcast(I32), node_f[:, bass.ds(i, 1)], 0.0, ALU.is_le,
                                  ALU.add, accum_out=cnt[:, bass.ds(i, 1)]).then_inc(counted, 1)

            def step(i, b, u):
                if not isinstance(i, int) or i < NT - 1:
                    normalise(i + 1, 1 - b, u + b)
                if not isinstance(i, int) or i >= 1:
                    count_edges(i - 1, 1 - b, u - 1 + b)
                add_bias(i, b, u)
                find_tile(i, b)
                feature(i, b, u)
                name_tile(i, b)

            normalise(0, 0, 0)
            drive(eng, step)
            eng.memset(state[:], 0.0).then_inc(state_zero, 1)
            eng.wait_ge(state_zero, 1)
            eng.wait_ge(acc_done, NT)
            for c, bank in enumerate((A0, A1)):
                for h in range(H // KD):
                    rows = slice(h * C, (h + 1) * C)
                    eng.tensor_copy(state[rows, c, h * C:(h + 1) * C], bank[rows, h * C:(h + 1) * C])
                    last = eng.tensor_copy(state[rows, c, P + h:P + h + 1], bank[rows, P:P + 1])
            last.then_inc(state_done, 1)
            eng.wait_ge(state_done, 1)
            i = NT - 1
            count_edges(i, i % 2, i // 2)
            eng.tensor_scalar(tile_f, tile_f, float(TILES - 1), None, ALU.min).then_inc(last_found, 1)
            eng.wait_ge(last_found, 1)
            eng.wait_ge(counted, NT)
            eng.scalar_tensor_tensor(tile_f, tile_f, float(P), cnt, ALU.mult, ALU.add).then_inc(last_found, 1)
            eng.wait_ge(last_found, 2)
            eng.tensor_scalar(last_i[:], tile_f, -1.0, 0.0, ALU.add, ALU.max).then_inc(last_found, 1)
            eng.wait_ge(last_found, 3)


def edges_and_mix(nc, sem, psum, ident, eps, src_t, dst_t, dst_f, state, carve, dst, edge_attr, We, mats, columns,
                  rows, kv_d, q_d, xn_d, xs_d, x1_d, part_d, slot_d):
    we = carve(KD, D)
    ea = [carve(G, D) for _ in range(2)]
    kv = [carve(G, 2 * D) for _ in range(2)]
    q = [carve(G, D) for _ in range(2)]
    dst_all = [carve(G, P) for _ in range(2)]
    dst_row = [carve(P) for _ in range(2)]
    eaT = [carve(2 * KD, P) for _ in range(2)]
    kj = [carve(2, D) for _ in range(2)]
    ve = [carve(G, D) for _ in range(2)]
    alpha = [carve(G * H) for _ in range(2)]
    src_c = [carve(G) for _ in range(2)]
    dst_c = [carve(G) for _ in range(2)]
    dst_cf = [carve(G) for _ in range(2)]
    same = [carve(G, P) for _ in range(2)]
    msg = [carve(G, MSG) for _ in range(2)]
    part = [carve(G, ROW) for _ in range(2)]
    keep = carve(P + 1)
    left, peak, diff, prob = carve(P), carve(P), carve(P), carve(P)
    wq, wo, w1, w2 = carve(KD, D), carve(KD, D), carve(KD, FF), carve(FC, D)
    bq, b1, g1c, h1c = carve(KD), carve(FC), carve(KD), carve(KD)
    bo, g1, hb, b2, g2 = (carve(D) for _ in range(5))
    mx_xn, mx_xs, mx_out = carve(D), carve(D), carve(D)
    xnT, qneg, qpos, attn, attnT = carve(KD, P), carve(KD, P), carve(KD, P), carve(D), carve(KD, P)
    den, y, xm, z, x1T, hid = carve(H), carve(D), carve(D), carve(D), carve(KD, P), carve(FC, P)
    m_st6, m_mom, m_std, m_rstd, m_off = carve(6), carve(2), carve(1), carve(1), carve(1)
    no_row = carve(XROW)
    SG = G * H
    T, E_ps, U, S, M = psum[0:2], psum[2:4], psum[4:6], psum[6], psum[7]

    passed = sem("b_passed")
    loaded, edge_made = sem("b_loaded"), sem("b_made")
    ea_in = [sem(f"ea_in{b}") for b in range(2)]
    all_in = [sem(f"dst_all_in{b}") for b in range(2)]
    row_in = [sem(f"dst_row_in{b}") for b in range(2)]
    gathered = [[sem(f"gathered{b}_{j}") for j in range(PAIRS)] for b in range(2)]
    index_ready, eaT_ps, eaT_sb, e_ps = sem("index_ready"), sem("eaT_ps"), sem("eaT_sb"), sem("e_ps")
    kj_ready, ve_ready, prod_ready, alpha_ready = sem("kj_ready"), sem("ve_ready"), sem("prod_ready"), sem("alpha_ready")
    same_row, keep_ready, alphaT_ps, left_ready = sem("same_row"), sem("keep_ready"), sem("alphaT_ps"), sem("left_ready")
    peak_ready, diff_ready, prob_ready, back_ps = sem("peak_ready"), sem("diff_ready"), sem("prob_ready"), sem("back_ps")
    dstc_ready, weights_sb, peaks_sb, same_ready = sem("dstc_ready"), sem("weights_sb"), sem("peaks_sb"), sem("same_ready")
    msg_ready, u_ps, u_sb = sem("msg_ready"), sem("u_ps"), sem("u_sb")
    part_out = [sem(f"part_out{b}") for b in range(2)]
    no_row_made, slots_out = sem("no_row_made"), sem("slots_emptied")
    mx_in, mx_xs_in, mx_stored = sem("mx_in"), sem("mx_xs_in"), sem("mx_stored")
    xnT_ps, q_ps, num_ps, attnT_ps, wo_ps, zT_ps, up0_ps, up1_ps, down_ps = (sem("mx_" + n) for n in (
        "xnT_ps", "q_ps", "num_ps", "attnT_ps", "wo_ps", "zT_ps", "up0_ps", "up1_ps", "down_ps"))
    xnT_sb, q_exp, attnT_sb, x1T_sb, relu0, relu1 = (sem("mx_" + n) for n in (
        "xnT_sb", "q_exp", "attnT_sb", "x1T_sb", "relu0", "relu1"))
    q_min, phi_q, den_eps, den_inv, attn_sb, xb_sb, gained, shifted, summed = (sem("mx_" + n) for n in (
        "q_min", "phi_q", "den_eps", "den_inv", "attn_sb", "xb_sb", "gained", "shifted", "final"))
    y_sb, y_stats, y_mom, y_std, y_rstd, y_off, z_sb = ([sem(f"mx_{n}{m}") for m in range(2)] for n in (
        "y_sb", "y_stats", "y_mom", "y_std", "y_rstd", "y_off", "z_sb"))
    scaled2 = sem("mx_scaled2")

    def seen(v, n=1):
        return not isinstance(v, int) or v >= n

    def is_tile(k):
        return not isinstance(k, int) or k < NT

    def exists(g):
        return not isinstance(g, int) or 0 <= g < NG

    def drive(eng, step):
        def two_steps(k):
            step(2 * k + 2, 0, k + 1, (k, 0))
            step(2 * k + 3, 1, k + 1, (k, 8))

        for g in range(2):
            step(g, g, 0, None)
        two_steps(0)
        two_steps(1)
        with eng.Fori(2, NT - 1) as k:
            two_steps(k)
        two_steps(NT - 1)
        for g in range(2 * NT + 2, NG + 2):
            step(g, g % 2, g // 2, (NT, 0) if g == 2 * NT + 2 else None)

    with nc.Block() as block:
        @block.sync
        def _(eng):
            eng.dma_start(we, We.rearrange("(k p) n -> p k n", p=P)).then_inc(loaded, 16)
            edge_rows = rows_as_tiles(edge_attr)
            dst_rows = dst.rearrange("(t e) -> t e", e=P)
            part_rows = rows_as_tiles(part_d)

            def load(g, b):
                if seen(g, 2):
                    hold(eng, eaT_ps, PAIRS * (g - 1), passed)
                eng.dma_start(ea[b], edge_rows[:, bass.ds(g * G, G), :]).then_inc(ea_in[b], 16)
                if seen(g, 2):
                    hold(eng, keep_ready, g - 1, passed)
                    hold(eng, same_ready, g - 1, passed)
                eng.dma_start(dst_row[b][0:SG].bitcast(I32),
                              dst_rows[bass.ds(g * G, G), :].rearrange("t (o e) -> t o e", o=1)
                              .to_broadcast([G, H, P])).then_inc(row_in[b], 16)
                eng.dma_start(dst_all[b].rearrange("p t e -> p (t e)").bitcast(I32),
                              dst[bass.ds(g * G * P, G * P)].rearrange("(o e) -> o e", o=1)
                              .to_broadcast([P, G * P])).then_inc(all_in[b], 16)

            def store(g, b):
                hold(eng, u_sb, G * (g + 1), passed)
                hold(eng, peaks_sb, g + 1, passed)
                eng.dma_start(part_rows[:, bass.ds(g * G, G), :], part[b]).then_inc(part_out[b], 16)

            def empty_slots(t):
                eng.dma_start(slot_d[bass.ds(t * P, P), :], no_row).then_inc(slots_out, 16)

            eng.wait_ge(no_row_made, 2)

            def step(g, b, u, mix):
                if exists(g):
                    load(g, b)
                if exists(g - 3):
                    store(g - 3, 1 - b)
                if exists(g):
                    empty_slots(g)
                if isinstance(g, int) and g == 0:
                    eng.dma_start(mx_xn, xn_d[0:P, :]).then_inc(mx_in, 16)
                    eng.dma_start(mx_xs, xs_d[0:P, :]).then_inc(mx_xs_in, 16)
                    for to, of in ((wq, mats[0]), (wo, mats[1]), (w1, mats[2]), (w2, mats[3])):
                        eng.dma_start(to, of.rearrange("(k p) n -> p k n", p=P)).then_inc(loaded, 16)
                    for to, of in ((bq, columns[0]), (b1, columns[1]), (g1c, rows[1]), (h1c, rows[2])):
                        with nc.allow_non_contiguous_dma("biases, once"):
                            eng.dma_start(to, per_channel(of)).then_inc(loaded, 16)
                    for to, of in zip((bo, g1, hb, b2, g2), rows):
                        eng.dma_start(to, over_partitions(of)).then_inc(loaded, 16)

            drive(eng, step)
            store(NG - 1, (NG - 1) % 2)
            for t in range(NG, SLOTS):
                empty_slots(t)
            eng.wait_ge(slots_out, 16 * SLOTS)
            for b in range(2):
                eng.wait_ge(part_out[b], 16 * (NG // 2))

        LOADS = 14 * 16
        assert NG <= SLOTS

        @block.gpsimd
        def _(eng):
            eng.memset(no_row[:, 0:D + NE], 0.0).then_inc(no_row_made, 1)
            eng.memset(no_row[:, D + NE:], 2.0 * NP).then_inc(no_row_made, 1)

            def step(g, b, u, mix):
                if not exists(g):
                    return
                if seen(g, 2):
                    eng.wait_ge(alpha_ready, PAIRS * (g - 1))
                eng.tensor_copy(src_c[b].bitcast(I32), src_t[:, bass.ds(g * G, G)]).then_inc(index_ready, 1)
                eng.tensor_copy(dst_c[b].bitcast(I32), dst_t[:, bass.ds(g * G, G)]).then_inc(index_ready, 1)
                hold(eng, index_ready, 2 * g + 2, passed)
                for t in range(G):
                    done = gathered[b][t // 2]
                    eng.indirect_dma_start(kv[b][:, t], None, kv_d, bass.IndirectOffsetOnAxis(
                        src_c[b][:, t:t + 1].bitcast(I32), 0), bounds_check=NP - 1, oob_is_err=False).then_inc(done, 16)
                    eng.indirect_dma_start(q[b][:, t], None, q_d, bass.IndirectOffsetOnAxis(
                        dst_c[b][:, t:t + 1].bitcast(I32), 0), bounds_check=NP - 1, oob_is_err=False).then_inc(done, 16)

            drive(eng, step)

        @block.tensor
        def _(eng):
            eng.wait_ge(loaded, 16)

            def mix_slot(mix, s):
                if mix is None:
                    return
                k, s = mix[0], mix[1] + s
                if not is_tile(k):
                    return
                if s == 0:
                    eng.wait_ge(mx_in, 16 * (k + 1))
                    if seen(k):
                        eng.wait_ge(y_sb[1], k)
                    for c in range(KD):
                        mm = eng.transpose(M[:, c * P:(c + 1) * P], mx_xn[:, c * P:(c + 1) * P], ident[:])
                    mm.then_inc(xnT_ps, 1)
                elif s == 1:
                    eng.wait_ge(xnT_sb, k + 1)
                    for o in range(KD):
                        for c in range(KD):
                            mm = eng.matmul(M[:, o * P:(o + 1) * P], wq[:, c, o * P:(o + 1) * P], xnT[:, c],
                                            start=c == 0, stop=c == KD - 1)
                    mm.then_inc(q_ps, 1)
                elif s == 4:
                    eng.wait_ge(phi_q, k + 1)
                    for c in range(KD):
                        mm = eng.matmul(M[:, c * KVW:(c + 1) * KVW], qneg[:, c], state[:, c], start=True, stop=True)
                    mm.then_inc(num_ps, 1)
                elif s == 5:
                    eng.wait_ge(attn_sb, k + 1)
                    for c in range(KD):
                        mm = eng.transpose(M[:, c * P:(c + 1) * P], attn[:, c * P:(c + 1) * P], ident[:])
                    mm.then_inc(attnT_ps, 1)
                elif s == 6:
                    eng.wait_ge(attnT_sb, k + 1)
                    for c in range(KD):
                        mm = eng.matmul(M[:, 0:D], attnT[:, c], wo[:, c], start=c == 0, stop=c == KD - 1)
                    mm.then_inc(wo_ps, 1)
                elif s == 9:
                    eng.wait_ge(z_sb[0], k + 1)
                    for c in range(KD):
                        mm = eng.transpose(M[:, c * P:(c + 1) * P], z[:, c * P:(c + 1) * P], ident[:])
                    mm.then_inc(zT_ps, 1)
                elif s in (10, 11):
                    first = s == 10
                    eng.wait_ge(x1T_sb if first else relu0, k + 1)
                    for f in range(FC // 2):
                        ff = f if first else FC // 2 + f
                        for c in range(KD):
                            mm = eng.matmul(M[:, f * P:(f + 1) * P], w1[:, c, ff * P:(ff + 1) * P], x1T[:, c],
                                            start=c == 0, stop=c == KD - 1)
                    mm.then_inc(up0_ps if first else up1_ps, 1)
                elif s in (12, 13):
                    eng.wait_ge(relu1, k + 1)
                    half = FC // 2 * (s - 12)
                    for f in range(half, half + FC // 2):
                        mm = eng.matmul(M[:, 0:D], hid[:, f], w2[:, f], start=f == 0, stop=f == FC - 1)
                    if s == 13:
                        mm.then_inc(down_ps, 1)

            def transposes(g, b, u, j):
                n = PAIRS * g + j
                if j == 0:
                    eng.wait_ge(ea_in[b], 16 * (u + 1))
                if seen(n, 2):
                    eng.wait_ge(eaT_sb, n - 1)
                for t in range(2):
                    for c in range(KD):
                        mm = eng.transpose(T[j % 2][:, (t * KD + c) * P:(t * KD + c + 1) * P],
                                           ea[b][:, 2 * j + t, c * P:(c + 1) * P], ident[:])
                mm.then_inc(eaT_ps, 1)

            def project(g, j):
                n = PAIRS * g + j
                eng.wait_ge(eaT_sb, n + 1)
                if seen(n, 2):
                    eng.wait_ge(ve_ready, n - 1)
                for t in range(2):
                    for c in range(KD):
                        mm = eng.matmul(E_ps[j % 2][:, t * D:(t + 1) * D], eaT[j % 2][:, t * KD + c], we[:, c],
                                        start=c == 0, stop=c == KD - 1)
                mm.then_inc(e_ps, 1)

            def scores_to_rows(g, b):
                hold(eng, alpha_ready, PAIRS * (g + 1), passed)
                if seen(g):
                    hold(eng, peaks_sb, g, passed)
                eng.transpose(S[0:SG, 0:P], alpha[b], ident[:]).then_inc(alphaT_ps, 1)

            def rows_back(g):
                hold(eng, prob_ready, g + 1, passed)
                eng.transpose(S[:, P:P + SG], prob[0:SG], ident[0:SG, 0:SG])
                eng.transpose(S[:, P + SG:P + 2 * SG], peak[0:SG], ident[0:SG, 0:SG]).then_inc(back_ps, 1)

            def sum_nodes(g, b, j):
                if not exists(g):
                    return
                eng.wait_ge(msg_ready, PAIRS * g + j + 1)
                for t in (2 * j, 2 * j + 1):
                    n = G * g + t
                    if seen(n, 2):
                        eng.wait_ge(u_sb, n - 1)
                    eng.matmul(U[t % 2][:, 0:MSG], same[b][:, t], msg[b][:, t], start=True, stop=True)\
                       .then_inc(u_ps, 1)

            transposes(0, 0, 0, 0)
            transposes(0, 0, 0, 1)
            project(0, 0)

            def step(g, b, u, mix):
                for j in range(PAIRS):
                    if j < 2 and exists(g):
                        transposes(g, b, u, j + 2)
                    if j >= 2 and exists(g + 1):
                        transposes(g + 1, 1 - b, u + b, j - 2)
                    if j < 3 and exists(g):
                        project(g, j + 1)
                    if j == 3 and exists(g + 1):
                        project(g + 1, 0)
                    mix_slot(mix, 2 * j)
                    if j == 2:
                        mix_slot(mix, 2 * j + 1)
                    if j < 3:
                        sum_nodes(g - 2, b, j + 1)
                    else:
                        sum_nodes(g - 1, 1 - b, 0)
                    if j == 0 and exists(g - 1):
                        scores_to_rows(g - 1, 1 - b)
                    if j == 1 and exists(g - 1):
                        rows_back(g - 1)
                    if j != 2:
                        mix_slot(mix, 2 * j + 1)
                if isinstance(g, int) and g == 1:
                    eng.wait_ge(loaded, LOADS)

            drive(eng, step)

        @block.scalar
        def _(eng):
            def normalised(k, m):
                eng.wait_ge(y_off[m], k + 1)
                eng.activation(z, y, ACT.Identity, bias=m_off, scale=m_rstd).then_inc(z_sb[m], 1)

            def mix_slot(mix, s):
                if mix is None:
                    return
                k, s = mix[0], mix[1] + s
                if s == 3 and seen(k):
                    eng.wait_ge(summed, k)
                    eng.dma_start(x1_d[bass.ds((k - 1) * P, P), :], mx_out).then_inc(mx_stored, 16)
                    if is_tile(k):
                        eng.dma_start(mx_xs, xs_d[bass.ds(k * P, P), :]).then_inc(mx_xs_in, 16)
                if s == 0 and is_tile(k):
                    eng.wait_ge(xnT_ps, k + 1)
                    eng.activation(xnT.rearrange("p k n -> p (k n)"), M[:, 0:D], ACT.Copy).then_inc(xnT_sb, 1)
                if s == 0 and seen(k):
                    normalised(k - 1, 1)
                if not is_tile(k):
                    return
                if s == 2:
                    eng.wait_ge(q_min, k + 1)
                    for c in range(KD):
                        eng.activation(qpos[:, c], M[:, c * P:(c + 1) * P], ACT.Relu, bias=bq[:, c:c + 1])
                    eng.activation(qneg.rearrange("p k n -> p (k n)"), qneg.rearrange("p k n -> p (k n)"), ACT.Exp)\
                       .then_inc(q_exp, 1)
                elif s == 5:
                    eng.wait_ge(attnT_ps, k + 1)
                    eng.activation(attnT.rearrange("p k n -> p (k n)"), M[:, 0:D], ACT.Copy).then_inc(attnT_sb, 1)
                elif s in (7, 14):
                    m = int(s == 14)
                    eng.wait_ge(y_mom[m], k + 1)
                    eng.activation(m_std, m_mom[:, 1:2], ACT.Sqrt, bias=eps[:]).then_inc(y_std[m], 1)
                    if m == 0 and (not isinstance(k, int) or k < NT - 1):
                        eng.dma_start(mx_xn, xn_d[bass.ds(k * P + P, P), :]).then_inc(mx_in, 16)
                elif s == 8:
                    normalised(k, 0)
                elif s == 9:
                    eng.wait_ge(zT_ps, k + 1)
                    for c in range(KD):
                        last = eng.activation(x1T[:, c], M[:, c * P:(c + 1) * P], ACT.Identity, bias=h1c[:, c:c + 1],
                                              scale=g1c[:, c:c + 1])
                    last.then_inc(x1T_sb, 1)
                elif s in (10, 11):
                    first = s == 10
                    eng.wait_ge(up0_ps if first else up1_ps, k + 1)
                    for f in range(FC // 2):
                        ff = f if first else FC // 2 + f
                        last = eng.activation(hid[:, ff], M[:, f * P:(f + 1) * P], ACT.Relu, bias=b1[:, ff:ff + 1])
                    last.then_inc(relu0 if first else relu1, 1)

            def move(g, j):
                n = PAIRS * g + j
                eng.wait_ge(eaT_ps, n + 1)
                if seen(n, 2):
                    eng.wait_ge(e_ps, n - 1)
                eng.activation(eaT[j % 2].rearrange("p k n -> p (k n)"), T[j % 2][:], ACT.Copy).then_inc(eaT_sb, 1)

            def exponentials(g):
                eng.wait_ge(diff_ready, g + 1)
                if seen(g):
                    eng.wait_ge(back_ps, g)
                eng.activation(prob[0:SG], diff[0:SG], ACT.Exp, scale=SCALE).then_inc(prob_ready, 1)

            def sums_out(g, b, u, j):
                if not exists(g):
                    return
                for t in (2 * j, 2 * j + 1):
                    eng.wait_ge(u_ps, G * g + t + 1)
                    if t == 0 and seen(g, 2):
                        eng.wait_ge(part_out[b], 16 * u)
                    eng.activation(part[b][:, t, 0:MSG], U[t % 2][:, 0:MSG], ACT.Copy).then_inc(u_sb, 1)

            move(0, 0)
            move(0, 1)

            def step(g, b, u, mix):
                for j in range(PAIRS):
                    if j < 2 and exists(g):
                        move(g, j + 2)
                    if j >= 2 and exists(g + 1):
                        move(g + 1, j - 2)
                    if j == 1 and exists(g - 1):
                        exponentials(g - 1)
                    mix_slot(mix, 2 * j)
                    if j < 3:
                        sums_out(g - 2, b, u - 1, j + 1)
                    else:
                        sums_out(g - 1, 1 - b, u - 1 + b, 0)
                    mix_slot(mix, 2 * j + 1)
                if isinstance(g, int) and g == 1:
                    eng.wait_ge(loaded, LOADS)

            drive(eng, step)
            eng.wait_ge(mx_stored, 16 * NT)

        @block.vector
        def _(eng):
            eng.memset(keep[:], -BIG).then_inc(edge_made, 1)
            eng.wait_ge(edge_made, 1)

            def scale_and_offset(k, m):
                eng.wait_ge(y_std[m], k + 1)
                eng.reciprocal(m_rstd, m_std).then_inc(y_rstd[m], 1)
                eng.wait_ge(y_rstd[m], k + 1)
                eng.tensor_scalar(m_off, m_mom[:, 0:1], m_rstd, -1.0, ALU.mult, ALU.mult).then_inc(y_off[m], 1)

            def mix_slot(mix, s):
                if mix is None:
                    return
                k, s = mix[0], mix[1] + s
                if s == 0 and seen(k):
                    scale_and_offset(k - 1, 1)
                elif s == 1 and seen(k):
                    eng.wait_ge(z_sb[1], k)
                    if seen(k, 2):
                        eng.wait_ge(mx_stored, 16 * (k - 1))
                    eng.tensor_tensor(mx_out, z, g2, ALU.mult).then_inc(scaled2, 1)
                elif s == 2 and seen(k):
                    eng.wait_ge(scaled2, k)
                    eng.wait_ge(mx_xs_in, 16 * k)
                    eng.tensor_tensor(mx_out, mx_out, mx_xs, ALU.add).then_inc(summed, 1)
                if not is_tile(k):
                    return
                if s == 2:
                    eng.wait_ge(q_ps, k + 1)
                    for c in range(KD):
                        last = eng.tensor_scalar(qneg[:, c], M[:, c * P:(c + 1) * P], bq[:, c:c + 1], 0.0,
                                                 ALU.add, ALU.min)
                    last.then_inc(q_min, 1)
                elif s == 3:
                    eng.wait_ge(q_exp, k + 1)
                    eng.tensor_tensor(qneg, qneg, qpos, ALU.add).then_inc(phi_q, 1)
                elif s == 4:
                    eng.wait_ge(num_ps, k + 1)
                    sums = M[:, 0:KD * KVW].rearrange("p (c w) -> p c w", c=KD)
                    hk = H // KD
                    eng.tensor_scalar(den.rearrange("p (c h) -> p c h", c=KD), sums[:, :, P:KVW], 1e-6, None,
                                      ALU.add).then_inc(den_eps, 1)
                    eng.wait_ge(den_eps, k + 1)
                    eng.reciprocal(den, den).then_inc(den_inv, 1)
                    eng.wait_ge(den_inv, k + 1)
                    for c in range(KD):
                        last = eng.tensor_tensor(
                            attn[:, c * P:(c + 1) * P].rearrange("p (h c) -> p h c", h=hk),
                            M[:, c * KVW:c * KVW + P].rearrange("p (h c) -> p h c", h=hk),
                            den[:, c * hk:(c + 1) * hk].rearrange("p (h o) -> p h o", o=1).to_broadcast([P, hk, C]),
                            ALU.mult)
                    last.then_inc(attn_sb, 1)
                elif s == 5:
                    eng.tensor_tensor(xm, mx_xn, bo, ALU.add).then_inc(xb_sb, 1)
                elif s in (6, 14):
                    m = int(s == 14)
                    eng.wait_ge((wo_ps, down_ps)[m], k + 1)
                    eng.tensor_tensor(y, M[:, 0:D], xm, ALU.add).then_inc(y_sb[m], 1)
                    eng.wait_ge(y_sb[m], k + 1)
                    eng.bn_stats(m_st6, y).then_inc(y_stats[m], 1)
                    hold(eng, y_stats[m], k + 1, passed)
                    eng.bn_aggr(m_mom, m_st6).then_inc(y_mom[m], 1)
                elif s == 7:
                    scale_and_offset(k, 0)
                elif s == 9:
                    eng.wait_ge(z_sb[0], k + 1)
                    eng.tensor_tensor(xm, z, g1, ALU.mult).then_inc(gained, 1)
                elif s == 10:
                    eng.wait_ge(gained, k + 1)
                    eng.tensor_tensor(xm, xm, hb, ALU.add).then_inc(shifted, 1)

            def keys_and_values(g, b, u, j):
                n = PAIRS * g + j
                e2 = E_ps[j % 2][:].rearrange("p (t c) -> p t c", t=2)
                eng.wait_ge(gathered[b][j], 64 * (u + 1))
                eng.wait_ge(e_ps, n + 1)
                eng.tensor_tensor(kj[j % 2], kv[b][:, 2 * j:2 * j + 2, 0:D], e2, ALU.add).then_inc(kj_ready, 1)
                eng.tensor_tensor(ve[b][:, 2 * j:2 * j + 2], kv[b][:, 2 * j:2 * j + 2, D:], e2, ALU.add)\
                   .then_inc(ve_ready, 1)
                eng.wait_ge(kj_ready, n + 1)
                eng.tensor_tensor(kj[j % 2], kj[j % 2], q[b][:, 2 * j:2 * j + 2], ALU.mult).then_inc(prod_ready, 1)

            def score(g, b, j):
                eng.wait_ge(prod_ready, PAIRS * g + j + 1)
                eng.tensor_reduce(alpha[b][:, 2 * j * H:2 * (j + 1) * H],
                                  kj[j % 2].rearrange("p t (h c) -> p (t h) c", h=H), AX, ALU.add)\
                   .then_inc(alpha_ready, 1)

            def neighbours(g, b, u):
                eng.wait_ge(row_in[b], 16 * (u + 1))
                row = dst_row[b][0:SG].bitcast(I32)
                eng.tensor_tensor(keep[0:SG, 1:P], row[:, 1:P], row[:, 0:P - 1], ALU.is_equal).then_inc(same_row, 1)
                eng.tensor_copy(dst_cf[b], dst_f[:, bass.ds(g * G, G)]).then_inc(dstc_ready, 1)
                eng.wait_ge(same_row, g + 1)
                eng.tensor_scalar(keep[0:SG, 1:P], keep[0:SG, 1:P], 1.0, BIG, ALU.subtract, ALU.mult)\
                   .then_inc(keep_ready, 1)

            def same_nodes(g, b, u):
                eng.wait_ge(dstc_ready, g + 1)
                eng.wait_ge(all_in[b], 16 * (u + 1))
                if seen(g, 2):
                    eng.wait_ge(u_ps, G * (g - 1))
                eng.tensor_tensor(same[b], dst_all[b].bitcast(I32),
                                  dst_cf[b].rearrange("p (t o) -> p t o", o=1).to_broadcast([P, G, P]),
                                  ALU.is_equal).then_inc(same_ready, 1)

            def maxima(g):
                eng.wait_ge(keep_ready, g + 1)
                eng.wait_ge(alphaT_ps, g + 1)
                if seen(g):
                    eng.wait_ge(back_ps, g)
                eng.tensor_tensor_scan(left[0:SG], keep[0:SG, 0:P], S[0:SG, 0:P], -BIG, ALU.add, ALU.max)\
                   .then_inc(left_ready, 1)
                eng.wait_ge(left_ready, g + 1)
                eng.tensor_tensor_scan(peak[0:SG, ::-1], keep[0:SG, 1:P + 1][:, ::-1], left[0:SG, ::-1], -BIG,
                                       ALU.add, ALU.max).then_inc(peak_ready, 1)
                eng.wait_ge(peak_ready, g + 1)
                if seen(g):
                    eng.wait_ge(prob_ready, g)
                eng.tensor_tensor(diff[0:SG], S[0:SG, 0:P], peak[0:SG], ALU.subtract).then_inc(diff_ready, 1)

            def weights_in(g, b, u):
                eng.wait_ge(back_ps, g + 1)
                eng.tensor_copy(msg[b][:, :, D:MSG], S[:, P:P + SG].rearrange("p (t h) -> p t h", t=G))\
                   .then_inc(weights_sb, 1)
                if seen(g, 2):
                    eng.wait_ge(part_out[b], 16 * u)
                eng.tensor_copy(part[b][:, :, MSG + H], dst_cf[b])
                eng.tensor_copy(part[b][:, :, MSG:MSG + H], S[:, P + SG:P + 2 * SG].rearrange("p (t h) -> p t h", t=G))\
                   .then_inc(peaks_sb, 1)
                eng.wait_ge(weights_sb, g + 1)

            def messages(g, b, j):
                if not exists(g):
                    return
                t = slice(2 * j, 2 * j + 2)
                eng.tensor_tensor(msg[b][:, t, 0:D].rearrange("p t (h c) -> p t h c", h=H),
                                  ve[b][:, t].rearrange("p t (h c) -> p t h c", h=H),
                                  per_head(msg[b][:, t, D:MSG], 2), ALU.mult).then_inc(msg_ready, 1)

            def step(g, b, u, mix):
                h, c, w = g - 1, 1 - b, u - 1 + b
                for j in range(PAIRS):
                    if j == 2:
                        mix_slot(mix, 2 * j)
                    if exists(g):
                        keys_and_values(g, b, u, j)
                    if j == 0 and exists(h):
                        neighbours(h, c, w)
                    if j != 2:
                        mix_slot(mix, 2 * j)
                    if j == 2 and exists(h):
                        weights_in(h, c, w)
                    if j < 2:
                        messages(g - 2, b, j + 2)
                    else:
                        messages(h, c, j - 2)
                    if exists(g):
                        score(g, b, j)
                    if j == 0 and exists(h):
                        maxima(h)
                    mix_slot(mix, 2 * j + 1)
                    if j == 1 and exists(h):
                        same_nodes(h, c, w)
                if isinstance(g, int) and g == 1:
                    eng.wait_ge(loaded, LOADS)
                    eng.tensor_tensor(hb, hb, b2, ALU.add).then_inc(edge_made, 1)
                    eng.wait_ge(edge_made, 2)

            drive(eng, step)


def merge(nc, sem, psum, ident, carve, dst, part_d, extra_d):
    MR = 104
    MC = TILES // MR
    assert MR * MC == TILES
    FAR = 100000.0
    row_of, nxt_of, prev_of = ([carve(n) for _ in range(2)] for n in (ROW, 1, 1))
    ext, res, own1 = carve(ROW), carve(ROW), carve(1)
    own1_i = carve(1)
    over, first, key, to_f, to_i, from_i = (carve(1) for _ in range(6))
    keys, keysT, same = carve(MR), carve(MR), carve(MR)
    keep, left, peak = carve(MR + 1), carve(MR), carve(MR)
    d, w = carve(2 * H), carve(2 * H)
    K, S, Sum = psum[2], psum[3], psum[4]

    passed = sem("mg_passed")
    made, own_made, chain = sem("mg_made"), sem("own_made"), sem("mg_dve")
    mg_in = [sem(f"mg_in{b}") for b in range(2)]
    index_made, keys_made, ext_in = sem("mg_index"), sem("mg_keys"), sem("ext_in")
    keyT_ps, peakT, weights, scaled, sum_ps, res_ready, res_out = (sem(n) for n in (
        "keyT_ps", "peakT", "mg_weights", "mg_scaled", "mg_sum_ps", "res_ready", "res_out"))
    peaks_made, diffs = sem("mg_peaks"), sem("mg_diffs")
    dst_rows = dst.rearrange("(t e) -> t e", e=P)
    parts = part_d.rearrange("(t e) w -> t e w", e=P)

    def chunk_rows(eng, c, b, u):
        row, nxt, prev = row_of[b], nxt_of[b], prev_of[b]
        STEPS = 12
        n = [0]

        def link(ins):
            n[0] += 1
            ins.then_inc(chain, 1)
            eng.wait_ge(chain, STEPS * c + n[0])

        r = slice(0, MR)
        node = row[r, MSG + H:ROW]
        eng.wait_ge(mg_in[b], 48 * (u + 1))
        link(eng.tensor_tensor(over[r], node, nxt[r].bitcast(I32), ALU.is_equal))
        link(eng.tensor_tensor(first[r], node, prev[r].bitcast(I32), ALU.not_equal))
        link(eng.scalar_tensor_tensor(key[r], node, own1[r], over[r], ALU.add, ALU.mult))
        link(eng.tensor_tensor(key[r], key[r], own1[r], ALU.subtract))
        eng.tensor_copy(keys[r], key[r].to_broadcast([MR, MR])).then_inc(keys_made, 1)
        link(eng.tensor_tensor(first[r], first[r], over[r], ALU.mult))
        link(eng.scalar_tensor_tensor(to_f[r], node, FAR, first[r], ALU.subtract, ALU.mult))
        if later(c):
            eng.wait_ge(res_out, 16 * c)
        eng.tensor_scalar(to_i[r].bitcast(I32), to_f[r], FAR, None, ALU.add).then_inc(index_made, 1)
        eng.tensor_copy(from_i[r].bitcast(I32), node).then_inc(index_made, 1)
        eng.wait_ge(keyT_ps, c + 1)
        link(eng.tensor_copy(keysT[r], K[r, 0:MR]))
        eng.tensor_scalar(same[r], keysT[r], key[r], None, ALU.is_equal).then_inc(scaled, 1)
        link(eng.tensor_tensor(keep[0:H, 1:MR], keysT[0:H, 1:MR], keysT[0:H, 0:MR - 1], ALU.is_equal))
        link(eng.tensor_scalar(keep[0:H, 1:MR], keep[0:H, 1:MR], 1.0, BIG, ALU.subtract, ALU.mult))
        link(eng.tensor_tensor_scan(left[0:H], keep[0:H, 0:MR], S[0:H, 0:MR], -BIG, ALU.add, ALU.max))
        eng.tensor_tensor_scan(peak[0:H, ::-1], keep[0:H, 1:MR + 1][:, ::-1], left[0:H, ::-1], -BIG,
                               ALU.add, ALU.max).then_inc(peaks_made, 1)
        eng.wait_ge(peakT, c + 1)
        eng.wait_ge(ext_in, 16 * (c + 1))
        link(eng.tensor_tensor(res[r, MSG:MSG + H], S[r, P:P + H], ext[r, MSG:MSG + H], ALU.max))
        eng.tensor_tensor(d[r, 0:H], row[r, MSG:MSG + H], res[r, MSG:MSG + H], ALU.subtract).then_inc(diffs, 1)
        eng.tensor_tensor(d[r, H:], ext[r, MSG:MSG + H], res[r, MSG:MSG + H], ALU.subtract).then_inc(diffs, 1)
        eng.wait_ge(weights, c + 1)

        def weigh(rows, ws):
            eng.tensor_tensor(heads(rows[r, 0:D]), heads(rows[r, 0:D]),
                              ws.rearrange("p (h o) -> p h o", o=1).to_broadcast([MR, H, C]), ALU.mult)
            return eng.tensor_tensor(rows[r, D:MSG], rows[r, D:MSG], ws, ALU.mult)

        weigh(row, w[r, 0:H]).then_inc(scaled, 1)
        link(weigh(ext, w[r, H:]))
        eng.tensor_copy(res[r, MSG + H:ROW], node)
        eng.wait_ge(sum_ps, c + 1)
        eng.tensor_tensor(res[r, 0:MSG], ext[r, 0:MSG], Sum[r, 0:MSG], ALU.add).then_inc(res_ready, 1)
        assert n[0] == STEPS, n

    def later(c, n=1):
        return not isinstance(c, int) or c >= n

    def drive(eng, chunk):
        for c in range(2):
            chunk(c, c, 0)
        with eng.Fori(1, MC // 2) as k:
            chunk(2 * k, 0, k)
            chunk(2 * k + 1, 1, k)

    assert MC % 2 == 0

    with nc.Block() as block:
        @block.sync
        def _(eng):
            eng.wait_ge(made, 4)

            def chunk(c, b, u):
                if later(c, 2):
                    eng.wait_ge(res_ready, c - 1)
                first, rows = c * MR, slice(0, MR)
                with nc.allow_non_contiguous_dma("one number of a tile"):
                    eng.dma_start(row_of[b][rows], parts[bass.ds(first, MR), P - 1, :]).then_inc(mg_in[b], 16)
                    eng.dma_start(nxt_of[b][rows].bitcast(I32), dst_rows[bass.ds(first + 1, MR), 0:1])\
                       .then_inc(mg_in[b], 16)
                    eng.dma_start(prev_of[b][1:MR].bitcast(I32), dst_rows[bass.ds(first, MR - 1), P - 1:P])\
                       .then_inc(mg_in[b], 16)

            drive(eng, chunk)

        @block.gpsimd
        def _(eng):
            for b in range(2):
                eng.memset(prev_of[b].bitcast(I32), -1).then_inc(made, 1)
            eng.memset(keep, -BIG).then_inc(made, 1)
            eng.iota(own1_i.bitcast(I32), pattern=[[0, 1]], base=1, channel_multiplier=1).then_inc(own_made, 1)
            eng.wait_ge(own_made, 1)
            eng.tensor_copy(own1, own1_i.bitcast(I32)).then_inc(made, 1)

            def chunk(c, b, u):
                eng.wait_ge(index_made, 2 * c + 2)
                if later(c):
                    hold(eng, res_out, 16 * c, passed)
                eng.indirect_dma_start(ext[0:MR], None, extra_d, bass.IndirectOffsetOnAxis(
                    from_i[0:MR].bitcast(I32), 0), bounds_check=NP - 1, oob_is_err=False).then_inc(ext_in, 16)
                hold(eng, res_ready, c + 1, passed)
                eng.indirect_dma_start(extra_d, bass.IndirectOffsetOnAxis(to_i[0:MR].bitcast(I32), 0),
                                       res[0:MR], None, bounds_check=NP - 1, oob_is_err=False).then_inc(res_out, 16)

            drive(eng, chunk)
            eng.wait_ge(res_out, 16 * MC)

        @block.tensor
        def _(eng):
            eng.wait_ge(made, 4)
            def chunk(c, b, u):
                row = row_of[b]
                hold(eng, keys_made, c + 1, passed)
                eng.transpose(K[0:MR, 0:MR], keys[0:MR], ident[0:MR, 0:MR])
                eng.transpose(S[0:H, 0:MR], row[0:MR, MSG:MSG + H], ident[0:MR, 0:MR]).then_inc(keyT_ps, 1)
                hold(eng, peaks_made, c + 1, passed)
                eng.transpose(S[0:MR, P:P + H], peak[0:H], ident[0:H, 0:H]).then_inc(peakT, 1)
                hold(eng, scaled, 2 * c + 2, passed)
                eng.matmul(Sum[0:MR, 0:MSG], same[0:MR], row[0:MR, 0:MSG], start=True, stop=True).then_inc(sum_ps, 1)

            drive(eng, chunk)

        @block.scalar
        def _(eng):
            with eng.Fori(0, MC) as c:
                eng.wait_ge(diffs, 2 * c + 2)
                eng.activation(w[0:MR], d[0:MR], ACT.Exp, scale=SCALE).then_inc(weights, 1)

        @block.vector
        def _(eng):
            eng.wait_ge(made, 4)
            drive(eng, lambda c, b, u: chunk_rows(eng, c, b, u))


def experts(nc, sem, psum, ident, eps, node_f, last_i, carve, part_d, extra_d, x1_d, gate_w, gate_b, W1, b1, W2,
            b2, slot_d, y_d, out):
    w1 = carve(NE * KD, HD)
    w2 = carve(NE * HC, D)
    b1c, b2r = carve(NE * HC), carve(NE, D)
    acc = carve(NT, D)
    gw, gb = carve(KD, NE), carve(NE)
    expert_i = carve(SLOTS)
    rows_at = carve.at
    xs = carve(NT, XROW)
    end = carve.at
    early = Carve(carve.arena, end)
    has, off, peak = early(MACRO), early(MACRO), early(MACRO, H)
    d, w = early(MACRO, 2 * H), early(MACRO, 2 * H)
    st6, mom = early(MACRO, 6), early(MACRO, 2)
    at = [early(MACRO) for _ in range(2)]
    moments, std, rstd = early(NT, 2), early(NT), early(NT)
    xf = [early(D) for _ in range(2)]
    xfT = [early(KD, P) for _ in range(2)]
    lead, lead_i = early(NE), early(NE)
    cw, prob, hit, rank, one, two = (early(NT, NE) for _ in range(6))
    top, zeros = early(NT), early(NT)
    ones, before = early(P), early(P)
    incl, more = early(NE, NT), early(NE, NT)
    step_i, step_f, slot_i, slot_f = early(NT), early(NT), early(SLOTS), early(SLOTS)
    tiles, ends, starts, passed_e, expert_f = early(NE), early(NE), early(NE), early(SLOTS, NE), early(SLOTS)
    assert early.at <= NE * KD * HD
    early.at = rows_at
    row = [early(MACRO, ROW) for _ in range(2)]
    ext = [early(MACRO, ROW) for _ in range(2)]
    x1 = [early(MACRO, D) for _ in range(2)]
    b2_at = NE * (KD * HD + HC * D + HC)
    sends = Carve(carve.arena, b2_at + NE * D)
    sends.at = b2_at
    to_i = sends(NT, 2)
    send = [sends(XROW) for _ in range(4)]
    send_at = [sends(2) for _ in range(4)]
    results = Carve(carve.arena, NE * KD * HD)
    yy = [results(MACRO, 2 * D) for _ in range(2)]
    work = Carve(carve.arena, end)
    work.at = rows_at
    slot = [work(XROW) for _ in range(4)]
    xT = [work(KD, P) for _ in range(2)]
    w1s = [work(KD, HD) for _ in range(2)]
    hid = [work(HC, P) for _ in range(2)]
    ys = [work(D) for _ in range(4)]
    y_at = [work(1) for _ in range(4)]

    passed = sem("ex_passed")
    made, lead0, loaded, gates_in = sem("ex_made"), sem("lead0"), sem("ex_loaded"), sem("gates_in")
    at_ready = sem("ex_at")
    row_in = [sem(f"main_in{b}") for b in range(2)]
    ext_in = [sem(f"extra_in{b}") for b in range(2)]
    chain, diffs, weights, mom_ready, std_ready = (sem(n) for n in (
        "ex_dve", "ex_diffs", "ex_weights", "ex_mom", "ex_std"))
    x2_ready, kept, rstd_ready, xf_kept, sel_ready, counts_ps = (sem(n) for n in (
        "x2_ready", "x2_kept", "ex_rstd", "xf_kept", "selected", "counts_ps"))
    xf_ready, xfT_ps, xfT_sb, gate_ps, logits = (sem(n) for n in ("xf_ready", "xfT_ps", "xfT_sb", "gate_ps", "logits"))
    shifted, exps, routed = sem("gates_shifted"), sem("gates_exp"), sem("routed")
    staged = sem("row_staged")
    sent = [sem(f"row_sent{b}") for b in range(4)]
    slot_in = [sem(f"slot_in{b}") for b in range(4)]
    y_out = [sem(f"y_out{b}") for b in range(4)]
    xT_ps, xT_sb, w1_ready, h_ps, hid_ready, y_ps, y_sum, y_ready, y_at_ready = (sem("sl_" + n) for n in (
        "xT_ps", "xT_sb", "w1_ready", "h_ps", "hid_ready", "y_ps", "y_sum", "y_ready", "y_at"))
    yy_in = [sem(f"yy_in{b}") for b in range(2)]
    first_added, added = sem("first_added"), sem("added")
    out_done = sem("out_done")
    T, L = psum[0:2], psum[2:4]
    XT, HP, counts, YP = psum[0:2], psum[2:4], psum[4:6], psum[6:8]
    TURNS = SLOTS + 1
    STEPS = 15
    LOADS = 16 * (2 * NE + 2)

    def drive(eng, step, count):
        for i in range(3):
            step(i, i % 2, i // 2)
        with eng.Fori(1, (count - 1) // 2) as k:
            step(2 * k + 1, 1, k)
            step(2 * k + 2, 0, k + 1)

    def drive_slots(eng, turn, count=TURNS, peeled=1):
        for s in range(4 * peeled):
            turn(s, s % 4, s // 4)
        with eng.Fori(peeled, count // 4) as k:
            for j in range(4):
                turn(4 * k + j, j, k)
        for s in range(4 * (count // 4), count):
            turn(s, s % 4, s // 4)

    def seen(v, n=1):
        return not isinstance(v, int) or v >= n

    def is_tile(i):
        return not isinstance(i, int) or i < NT

    def is_slot(s):
        return not isinstance(s, int) or 0 <= s < SLOTS

    def expert_of(eng, s):
        return eng.value_load(expert_i[0:1, bass.ds(s, 1)].bitcast(I32), min_val=0, max_val=NE - 1)

    with nc.Block() as block:
        @block.sync
        def _(eng):
            eng.dma_start(gw, gate_w.rearrange("(k p) n -> p k n", p=P)).then_inc(gates_in, 16)
            eng.dma_start(gb, over_partitions(gate_b)).then_inc(gates_in, 16)

            def step(m, b, u):
                if seen(m, 2):
                    eng.wait_ge(chain, STEPS * (m - 1))
                    eng.wait_ge(kept, m - 1)
                eng.dma_start(ext[b], rows_as_tiles(extra_d)[:, bass.ds(m * MACRO, MACRO), :]).then_inc(ext_in[b], 16)
                eng.dma_start(x1[b], rows_as_tiles(x1_d)[:, bass.ds(m * MACRO, MACRO), :]).then_inc(ext_in[b], 16)

            drive(eng, step, MACROS)
            eng.wait_ge(routed, 1)
            for e in range(NE):
                eng.wait_ge(staged, e * (NT // NE) + 1)
                eng.dma_start(w1[:, e * KD:(e + 1) * KD], W1[e].rearrange("(k p) n -> p k n", p=P))\
                   .then_inc(loaded, 16)
                eng.dma_start(w2[:, e * HC:(e + 1) * HC], W2[e].rearrange("(k p) n -> p k n", p=P))\
                   .then_inc(loaded, 16)
            with nc.allow_non_contiguous_dma("biases, once"):
                eng.dma_start(b1c, b1.rearrange("e (k p) -> p (e k)", p=P)).then_inc(loaded, 16)
            for b in range(4):
                eng.wait_ge(sent[b], 32 * ((NT + 3 - b) // 4))
            eng.dma_start(b2r.rearrange("p e n -> p (e n)"), over_partitions(b2.rearrange("e n -> (e n)")))\
               .then_inc(loaded, 16)

            def turn(s, b, u):
                if seen(s, 4):
                    hold(eng, y_ready, s - 3, passed)
                    hold(eng, y_at_ready, s - 3, passed)
                eng.dma_start(slot[b], slot_d[bass.ds(s * P, P), :]).then_inc(slot_in[b], 16)

            drive_slots(eng, turn, SLOTS)
            for b in range(4):
                eng.wait_ge(y_out[b], 16 * ((SLOTS + 3 - b) // 4))
            pairs = y_d[0:2 * NP, :].rearrange("(t p w) c -> p t (w c)", p=P, w=2)
            rows = out[0:(NT - 1) * P, :].rearrange("(t p) c -> p t c", p=P)
            for m in range(MACROS):
                if m >= 2:
                    eng.wait_ge(added, m - 1)
                eng.dma_start(yy[m % 2], pairs[:, m * MACRO:(m + 1) * MACRO, :]).then_inc(yy_in[m % 2], 16)
                if m:
                    eng.wait_ge(added, m)
                    eng.dma_start(rows[:, (m - 1) * MACRO:m * MACRO, :], acc[:, (m - 1) * MACRO:m * MACRO, :])\
                       .then_inc(out_done, 16)
            eng.wait_ge(added, MACROS)
            first = NT - MACRO
            eng.dma_start(rows[:, first:NT - 1, :], acc[:, first:NT - 1, :]).then_inc(out_done, 16)
            eng.dma_start(out[(NT - 1) * P:N, :], acc[0:LAST, NT - 1, :]).then_inc(out_done, 16)
            eng.wait_ge(out_done, 16 * (MACROS + 1))

        @block.gpsimd
        def _(eng):
            eng.iota(lead_i.bitcast(I32), pattern=[[-1, NE]], base=NE, channel_multiplier=0).then_inc(lead0, 1)
            eng.wait_ge(lead0, 1)
            eng.tensor_copy(lead, lead_i.bitcast(I32)).then_inc(made, 1)
            eng.memset(zeros, 0.0).then_inc(made, 1)
            eng.memset(ones, 1.0).then_inc(made, 1)
            eng.wait_ge(made, 3)
            eng.affine_select(out=before, in_=ones, compare_op=ALU.is_gt, fill=0.0, base=0, pattern=[[1, P]],
                              channel_multiplier=-1).then_inc(made, 1)
            eng.iota(step_i.bitcast(I32), pattern=[[P, NT]], base=0, channel_multiplier=0).then_inc(lead0, 1)
            eng.iota(slot_i.bitcast(I32), pattern=[[1, SLOTS]], base=0, channel_multiplier=0).then_inc(lead0, 1)
            eng.wait_ge(lead0, 3)
            eng.tensor_copy(step_f, step_i.bitcast(I32)).then_inc(made, 1)
            eng.tensor_copy(slot_f, slot_i.bitcast(I32)).then_inc(made, 1)

            def step(m, b, u):
                if seen(m, 2):
                    eng.wait_ge(chain, STEPS * (m - 1))
                    eng.wait_ge(kept, m - 1)
                eng.tensor_copy(at[b].bitcast(I32), last_i[:, bass.ds(m * MACRO, MACRO)]).then_inc(at_ready, 1)
                hold(eng, at_ready, m + 1, passed)
                for t in range(MACRO):
                    eng.indirect_dma_start(row[b][:, t], None, part_d, bass.IndirectOffsetOnAxis(
                        at[b][:, t:t + 1].bitcast(I32), 0), bounds_check=EP - 1, oob_is_err=False)\
                       .then_inc(row_in[b], 16)

            drive(eng, step, MACROS)

            def scatter(i, b, u):
                hold(eng, staged, i + 1, passed)
                for n in range(2):
                    eng.indirect_dma_start(slot_d, bass.IndirectOffsetOnAxis(send_at[b][:, n:n + 1].bitcast(I32), 0),
                                           send[b], None, bounds_check=SLOTS * P - 1, oob_is_err=False)\
                       .then_inc(sent[b], 16)

            drive_slots(eng, scatter, NT)

            def turn(s, b, u):
                hold(eng, y_ready, s + 1, passed)
                hold(eng, y_at_ready, s + 1, passed)
                eng.indirect_dma_start(y_d, bass.IndirectOffsetOnAxis(y_at[b].bitcast(I32), 0), ys[b], None,
                                       bounds_check=2 * NP - 1, oob_is_err=False).then_inc(y_out[b], 16)

            drive_slots(eng, turn, SLOTS)

        @block.tensor
        def _(eng):
            eng.wait_ge(gates_in, 32)

            def gates(i, b):
                eng.wait_ge(xfT_sb, i + 1)
                if seen(i, 2):
                    eng.wait_ge(logits, i - 1)
                for c in range(KD):
                    mm = eng.matmul(L[b][:, 0:NE], xfT[b][:, c], gw[:, c], start=c == 0, stop=c == KD - 1)
                mm.then_inc(gate_ps, 1)

            def step(i, b, u):
                if is_tile(i):
                    eng.wait_ge(xf_ready, i + 1)
                    if seen(i, 2):
                        eng.wait_ge(xfT_sb, i - 1)
                    for c in range(KD):
                        mm = eng.transpose(T[b][:, c * P:(c + 1) * P], xf[b][:, c * P:(c + 1) * P], ident[:])
                    mm.then_inc(xfT_ps, 1)
                if seen(i):
                    gates(i - 1, 1 - b)

            drive(eng, step, NT)
            step(NT, NT % 2, NT // 2)
            eng.wait_ge(made, 6)
            eng.wait_ge(sel_ready, 1)
            picked = hit.rearrange("p t e -> p (t e)")
            eng.matmul(counts[0][:, 0:NT * NE], ones, picked, start=True, stop=True)
            eng.matmul(counts[1][:, 0:NT * NE], before, picked, start=True, stop=True).then_inc(counts_ps, 1)
            eng.wait_ge(routed, 1)
            eng.wait_ge(loaded, LOADS)

            def columns(s, b, u):
                eng.wait_ge(slot_in[b], 16 * (u + 1))
                if seen(s, 2):
                    eng.wait_ge(xT_sb, s - 1)
                for c in range(KD):
                    mm = eng.transpose(XT[b % 2][:, c * P:(c + 1) * P], slot[b][:, c * P:(c + 1) * P], ident[:])
                mm.then_inc(xT_ps, 1)

            def up(s, b):
                eng.wait_ge(w1_ready, s + 1)
                eng.wait_ge(xT_sb, s + 1)
                if seen(s, 2):
                    eng.wait_ge(hid_ready, s - 1)
                for j in range(HC):
                    for c in range(KD):
                        mm = eng.matmul(HP[b % 2][:, j * P:(j + 1) * P], w1s[b % 2][:, c, j * P:(j + 1) * P],
                                        xT[b % 2][:, c], start=c == 0, stop=c == KD - 1)
                mm.then_inc(h_ps, 1)

            def down(s, b, e):
                eng.wait_ge(hid_ready, s + 1)
                if seen(s, 2):
                    eng.wait_ge(y_sum, s - 1)
                for j in range(HC):
                    mm = eng.matmul(YP[b % 2][:, 0:D], hid[b % 2][:, j], w2[:, bass.ds(e * HC + j, 1), :]
                                    .rearrange("p o n -> p (o n)"), start=j == 0, stop=j == HC - 1)
                mm.then_inc(y_ps, 1)

            columns(0, 0, 0)

            def turn(s, b, u):
                before_it, after_it = (b + 3) % 4, (b + 1) % 4
                if seen(s) and is_slot(s - 1):
                    e_before = expert_of(eng, s - 1)
                if is_slot(s):
                    up(s, b)
                if is_slot(s + 1):
                    columns(s + 1, after_it, u + (b == 3))
                if seen(s) and is_slot(s - 1):
                    down(s - 1, before_it, e_before)

            drive_slots(eng, turn)

        @block.scalar
        def _(eng):
            def keep_rows(m, b):
                eng.wait_ge(x2_ready, m + 1)
                eng.activation(acc[:, bass.ds(m * MACRO, MACRO), :], row[b][:, :, 0:D], ACT.Copy).then_inc(kept, 1)

            def weigh_parts(m, b, u):
                eng.wait_ge(diffs, 2 * m + 2)
                eng.activation(w.rearrange("p t h -> p (t h)"), d.rearrange("p t h -> p (t h)"), ACT.Exp, scale=SCALE)\
                   .then_inc(weights, 1)
                if seen(m):
                    keep_rows(m - 1, 1 - b)

            drive(eng, weigh_parts, MACROS)
            keep_rows(MACROS - 1, (MACROS - 1) % 2)
            eng.wait_ge(mom_ready, 1)
            eng.activation(std, moments[:, :, 1], ACT.Sqrt, bias=eps[:]).then_inc(std_ready, 1)

            def step(i, b, u):
                eng.wait_ge(xfT_ps, i + 1)
                if seen(i, 2):
                    eng.wait_ge(gate_ps, i - 1)
                eng.activation(xfT[b].rearrange("p k n -> p (k n)"), T[b][:, 0:D], ACT.Copy).then_inc(xfT_sb, 1)

            drive(eng, step, NT)
            eng.wait_ge(shifted, 1)
            eng.activation(prob.rearrange("p t e -> p (t e)"), prob.rearrange("p t e -> p (t e)"), ACT.Exp)\
               .then_inc(exps, 1)

            def columns(s, b):
                eng.wait_ge(xT_ps, s + 1)
                if seen(s, 2):
                    eng.wait_ge(h_ps, s - 1)
                eng.activation(xT[b % 2].rearrange("p k n -> p (k n)"), XT[b % 2][:, 0:D], ACT.Copy).then_inc(xT_sb, 1)

            def gelu(s, b):
                e = expert_of(eng, s)
                eng.wait_ge(h_ps, s + 1)
                if seen(s, 2):
                    eng.wait_ge(y_ps, s - 1)
                for j in range(HC):
                    last = eng.activation(hid[b % 2][:, j], HP[b % 2][:, j * P:(j + 1) * P], ACT.Gelu,
                                          bias=b1c[:, bass.ds(e * HC + j, 1)])
                last.then_inc(hid_ready, 1)

            eng.wait_ge(loaded, LOADS)
            columns(0, 0)

            def turn(s, b, u):
                if is_slot(s + 1):
                    columns(s + 1, (b + 1) % 4)
                if is_slot(s):
                    gelu(s, b)

            drive_slots(eng, turn)

        @block.vector
        def _(eng):
            eng.wait_ge(gates_in, 32)
            eng.wait_ge(made, 6)

            def add_up(m, b, u):
                n = [0]

                def link(ins):
                    n[0] += 1
                    ins.then_inc(chain, 1)
                    eng.wait_ge(chain, STEPS * m + n[0])

                def each(ap, width):
                    return ap.rearrange("p (t o) -> p t o", o=1).to_broadcast([P, MACRO, width])

                def messages(rows):
                    return rows[:, :, 0:D].rearrange("p t (h c) -> p t h c", h=H)

                rows, more = row[b], ext[b]
                top_of = slice(MSG, MSG + H)
                eng.wait_ge(row_in[b], 16 * MACRO * (u + 1))
                eng.wait_ge(ext_in[b], 32 * (u + 1))
                link(eng.tensor_tensor(has, rows[:, :, MSG + H], node_f[:, bass.ds(m * MACRO, MACRO)], ALU.is_equal))
                link(eng.tensor_scalar(off, has, 1.0, BIG, ALU.subtract, ALU.mult))
                link(eng.tensor_tensor(rows[:, :, top_of], rows[:, :, top_of], each(has, H), ALU.mult))
                link(eng.tensor_tensor(rows[:, :, top_of], rows[:, :, top_of], each(off, H), ALU.add))
                link(eng.tensor_tensor(peak, rows[:, :, top_of], more[:, :, top_of], ALU.max))
                if seen(m):
                    eng.wait_ge(weights, m)
                eng.tensor_tensor(d[:, :, 0:H], rows[:, :, top_of], peak, ALU.subtract).then_inc(diffs, 1)
                eng.tensor_tensor(d[:, :, H:], more[:, :, top_of], peak, ALU.subtract).then_inc(diffs, 1)
                eng.wait_ge(weights, m + 1)
                link(eng.tensor_tensor(w[:, :, 0:H], w[:, :, 0:H], each(has, H), ALU.mult))
                for part, ws in ((rows, w[:, :, 0:H]), (more, w[:, :, H:])):
                    eng.tensor_tensor(messages(part), messages(part), per_head(ws, MACRO), ALU.mult)
                    last = eng.tensor_tensor(part[:, :, D:MSG], part[:, :, D:MSG], ws, ALU.mult)
                link(last)
                link(eng.tensor_tensor(rows[:, :, 0:MSG], rows[:, :, 0:MSG], more[:, :, 0:MSG], ALU.add))
                link(eng.tensor_scalar(rows[:, :, D:MSG], rows[:, :, D:MSG], 1e-16, None, ALU.add))
                link(eng.reciprocal(rows[:, :, D:MSG], rows[:, :, D:MSG]))
                link(eng.tensor_tensor(messages(rows), messages(rows), per_head(rows[:, :, D:MSG], MACRO), ALU.mult))
                link(eng.tensor_tensor(rows[:, :, 0:D], rows[:, :, 0:D], x1[b], ALU.add))
                eng.sem_inc(x2_ready, 1)
                for t in range(MACRO):
                    last = eng.bn_stats(st6[:, t], rows[:, t, 0:D])
                link(last)
                eng.sem_inc(passed, 1)
                for t in range(MACRO):
                    last = eng.bn_aggr(mom[:, t], st6[:, t])
                link(last)
                link(eng.tensor_copy(moments[:, bass.ds(m * MACRO, MACRO), :], mom))
                assert n[0] == STEPS, n

            drive(eng, add_up, MACROS)
            eng.wait_ge(kept, MACROS)
            eng.sem_inc(mom_ready, 1)
            eng.wait_ge(std_ready, 1)
            eng.reciprocal(rstd, std).then_inc(rstd_ready, 1)
            eng.wait_ge(rstd_ready, 1)

            def normalise(i, b, u):
                if is_tile(i):
                    if seen(i, 2):
                        eng.wait_ge(xfT_ps, i - 1)
                    rows = acc[:, bass.ds(i, 1), :].rearrange("p o c -> p (o c)")
                    mean, scale = moments[:, bass.ds(i, 1), 0], rstd[:, bass.ds(i, 1)]
                    eng.tensor_scalar(xf[b], rows, mean, scale, ALU.subtract, ALU.mult).then_inc(xf_ready, 1)
                    eng.tensor_scalar(xs[:, bass.ds(i, 1), 0:D].rearrange("p o c -> p (o c)"), rows, mean, scale,
                                      ALU.subtract, ALU.mult).then_inc(xf_kept, 1)
                if seen(i, 2):
                    eng.wait_ge(gate_ps, i - 1)
                    eng.tensor_tensor(cw[:, bass.ds(i - 2, 1), :].rearrange("p o e -> p (o e)"), L[b][:, 0:NE],
                                      gb, ALU.add).then_inc(logits, 1)

            drive(eng, normalise, NT)
            for i in (NT, NT + 1):
                normalise(i, i % 2, i // 2)
            eng.wait_ge(logits, NT)
            eng.wait_ge(xf_kept, NT)
            done = [STEPS * MACROS]

            def link(ins):
                done[0] += 1
                ins.then_inc(chain, 1)
                eng.wait_ge(chain, done[0])

            def by_tile(ap):
                return ap.rearrange("p (t o) -> p t o", o=1).to_broadcast([P, NT, NE])

            link(eng.tensor_reduce(top, cw, AX, ALU.max))
            eng.tensor_tensor(prob, cw, by_tile(top), ALU.subtract).then_inc(shifted, 1)
            eng.wait_ge(exps, 1)
            link(eng.tensor_reduce(top, prob, AX, ALU.add))
            link(eng.reciprocal(top, top))
            link(eng.tensor_tensor(prob, prob, by_tile(top), ALU.mult))
            lead_t = lead.rearrange("p (o e) -> p o e", o=1).to_broadcast([P, NT, NE])
            link(eng.tensor_copy(two, prob))
            for chosen in (one, two):
                link(eng.tensor_reduce(top, two, AX, ALU.max))
                link(eng.tensor_tensor(hit, two, by_tile(top), ALU.is_equal))
                link(eng.tensor_tensor(rank, hit, lead_t, ALU.mult))
                link(eng.tensor_reduce(top, rank, AX, ALU.max))
                link(eng.tensor_tensor(chosen, rank, by_tile(top), ALU.is_equal))
                if chosen is one:
                    link(eng.scalar_tensor_tensor(two, one, -2.0, prob, ALU.mult, ALU.add))
            eng.tensor_tensor(hit, one, two, ALU.add).then_inc(sel_ready, 1)
            eng.wait_ge(sel_ready, 1)
            eng.tensor_tensor(xs[:, :, D:D + NE], prob, hit, ALU.mult)
            nodes = node_f[:].rearrange("p (t o) -> p t o", o=1).to_broadcast([P, NT, NE])
            eng.scalar_tensor_tensor(xs[:, :, D + NE:], nodes, 2.0, two, ALU.mult, ALU.add)
            eng.wait_ge(counts_ps, 1)
            here = counts[0][:, 0:NT * NE].rearrange("p (t e) -> p e t", e=NE)
            ahead = counts[1][:, 0:NT * NE].rearrange("p (t e) -> p e t", e=NE)
            for e in range(NE):
                last = eng.tensor_tensor_scan(incl[:, e], zeros, here[:, e], 0.0, ALU.add, ALU.add)
            link(last)
            link(eng.tensor_tensor(more, incl[:, :, NT - 1:NT].to_broadcast([P, NE, NT]),
                                   step_f.rearrange("p (o t) -> p o t", o=1).to_broadcast([P, NE, NT]), ALU.is_gt))
            link(eng.tensor_reduce(tiles, more, AX, ALU.add))
            link(eng.tensor_tensor_scan(ends, zeros[:, 0:NE], tiles, 0.0, ALU.add, ALU.add))
            link(eng.tensor_tensor(starts, ends, tiles, ALU.subtract))
            link(eng.scalar_tensor_tensor(incl, starts.rearrange("p (e o) -> p e o", o=1).to_broadcast([P, NE, NT]),
                                          float(P), incl, ALU.mult, ALU.add))
            link(eng.tensor_tensor(incl, incl, here, ALU.subtract))
            link(eng.tensor_tensor(incl, incl, ahead, ALU.add))
            places = incl.rearrange("p e t -> p t e")
            for n, chosen in enumerate((one, two)):
                link(eng.tensor_tensor(rank, chosen, places, ALU.mult))
                link(eng.tensor_reduce(top, rank, AX, ALU.add))
                link(eng.tensor_copy(to_i[:, :, n].bitcast(I32), top))
            link(eng.tensor_tensor(passed_e, slot_f.rearrange("p (s o) -> p s o", o=1).to_broadcast([P, SLOTS, NE]),
                                   ends.rearrange("p (o e) -> p o e", o=1).to_broadcast([P, SLOTS, NE]), ALU.is_ge))
            link(eng.tensor_reduce(expert_f, passed_e, AX, ALU.add))
            link(eng.tensor_scalar(expert_f, expert_f, float(NE - 1), None, ALU.min))
            eng.tensor_copy(expert_i.bitcast(I32), expert_f).then_inc(routed, 1)
            eng.wait_ge(routed, 1)

            def stage_rows(i, b, u):
                if seen(i, 4):
                    eng.wait_ge(sent[b], 32 * u)
                eng.tensor_copy(send[b], xs[:, bass.ds(i, 1), :].rearrange("p o c -> p (o c)"))
                eng.tensor_copy(send_at[b].bitcast(I32), to_i[:, bass.ds(i, 1), :].rearrange("p o n -> p (o n)")
                                .bitcast(I32)).then_inc(staged, 1)

            drive_slots(eng, stage_rows, NT)
            eng.wait_ge(loaded, LOADS)

            def take_weights(s, b):
                e = expert_of(eng, s)
                if seen(s, 2):
                    eng.wait_ge(h_ps, s - 1)
                eng.tensor_copy(w1s[b % 2], w1[:, bass.ds(e * KD, KD), :]).then_inc(w1_ready, 1)

            def weigh(s, b, u):
                e = expert_of(eng, s)
                eng.wait_ge(y_ps, s + 1)
                if seen(s, 4):
                    eng.wait_ge(y_out[b], 16 * u)
                eng.tensor_copy(y_at[b].bitcast(I32), slot[b][:, bass.ds(e + (D + NE), 1)]).then_inc(y_at_ready, 1)
                eng.tensor_tensor(ys[b], YP[b % 2][:, 0:D], b2r[:, bass.ds(e, 1), :].rearrange("p o n -> p (o n)"),
                                  ALU.add).then_inc(y_sum, 1)
                eng.wait_ge(y_sum, s + 1)
                eng.tensor_scalar(ys[b], ys[b], slot[b][:, bass.ds(e + D, 1)], None, ALU.mult).then_inc(y_ready, 1)

            take_weights(0, 0)

            def turn(s, b, u):
                if is_slot(s + 1):
                    take_weights(s + 1, (b + 1) % 4)
                if seen(s) and is_slot(s - 1):
                    weigh(s - 1, (b + 3) % 4, u - (b == 0))

            drive_slots(eng, turn, peeled=2)

            for m in range(MACROS):
                eng.wait_ge(yy_in[m % 2], 16 * (m // 2 + 1))
                rows = acc[:, m * MACRO:(m + 1) * MACRO, :]
                eng.tensor_tensor(rows, rows, yy[m % 2][:, :, 0:D], ALU.add).then_inc(first_added, 1)
                eng.wait_ge(first_added, m + 1)
                eng.tensor_tensor(rows, rows, yy[m % 2][:, :, D:], ALU.add).then_inc(added, 1)


_INS = ["x", "src", "dst", "edge_attr_256", "L0_gnn_Wq", "L0_gnn_bq", "L0_gnn_Wk", "L0_gnn_bk", "L0_gnn_Wv",
        "L0_gnn_bv", "L0_gnn_We", "L0_gnn_Ws", "L0_gnn_bs", "L0_mix_Wq", "L0_mix_bq", "L0_mix_Wk", "L0_mix_bk",
        "L0_mix_Wv", "L0_mix_bv", "L0_mix_Wo", "L0_mix_bo", "L0_mix_W1", "L0_mix_b1", "L0_mix_W2", "L0_mix_b2",
        "L0_mix_ln1_g", "L0_mix_ln1_b", "L0_mix_ln2_g", "L0_mix_ln2_b", "L0_ffn_gate_w", "L0_ffn_gate_b",
        "L0_ffn_W1", "L0_ffn_b1", "L0_ffn_W2", "L0_ffn_b2"]


def kernel(**inputs):
    import numpy as np
    import concourse.bacc as bacc
    from concourse.bass_utils import run_bass_kernel_spmd

    nc = bacc.Bacc("TRN2", target_bir_lowering=False, num_devices=1)
    arrays, args = {}, {}
    for name in _INS:
        a = np.ascontiguousarray(inputs[name])
        if name == "x":
            a = np.concatenate([a, np.zeros((NP - N, D), a.dtype)])
        elif name == "edge_attr_256":
            a = np.concatenate([a, np.zeros((EP - E, D), a.dtype)])
        elif name == "src":
            a = np.concatenate([a, np.zeros(EP - E, a.dtype)])
        elif name == "dst":
            a = np.concatenate([a, np.full(EP - E, N, a.dtype), np.full(P, N + 1, a.dtype)])
        arrays[f"in_{name}"] = a
        args[name] = nc.dram_tensor(f"in_{name}", a.shape, mybir.dt.from_np(a.dtype), kind="ExternalInput").ap()
    out = nc.dram_tensor("out", [N, D], F32, kind="ExternalOutput").ap()
    build(nc, **args, out=out)
    return run_bass_kernel_spmd(nc, [arrays], core_ids=[0]).results[0]["out"]
```
